# Optimizing a Trainium2 kernel written in Bass

```python
import numpy as np
import jax
import jax.numpy as jnp

def _softmax(x, axis=-1):
    return jax.nn.softmax(x, axis=axis)

def _gelu(x):
    return jax.nn.gelu(x, approximate=True)

def _silu(x):
    return jax.nn.silu(x)

def _sigmoid(x):
    return jax.nn.sigmoid(x)

def _layernorm(x, axis=-1, eps=1e-05):
    m = jnp.mean(x, axis=axis, keepdims=True)
    v = jnp.var(x, axis=axis, keepdims=True)
    return (x - m) / jnp.sqrt(v + eps)

def _scatter_add(tgt, idx, src, axis=0):
    return tgt.at[idx].add(src)

def _segment_sum(src, seg, n):
    return jax.ops.segment_sum(src, seg, n)
kernel_name = 'mk_xattn_ffn_d2_seqx_r2_418c9f'

def setup_inputs(seed: int=0):
    np.random.seed(seed)
    _w = jnp.asarray

    def _rec_inputs():
        import jax
        import jax.numpy as jnp
        _rk = jax.random.key(seed)
        x = -0.0002928 + 1 * jax.random.normal(jax.random.fold_in(_rk, 1), (8, 100, 512), jnp.float32)
        _lenS = 100 - jax.random.randint(jax.random.fold_in(_rk, 7), (8,), 0, max(1, 100 // 4) + 1, jnp.int32)
        _lenS2 = 722 - jax.random.randint(jax.random.fold_in(_rk, 8), (8,), 0, max(1, 722 // 4) + 1, jnp.int32)
        _ctx_1024P = jax.random.normal(jax.random.fold_in(_rk, 11), (8, 16, 512), jnp.float32)
        _ctx_1024c = jax.random.dirichlet(jax.random.fold_in(_rk, 511), 0.3 * jnp.ones((16,), jnp.float32), (8, 722))
        _ctx_1024t = jnp.einsum('bsk,bkd->bsd', _ctx_1024c, _ctx_1024P)
        _ctx_1024t = _ctx_1024t * jax.lax.rsqrt(jnp.mean(jnp.square(_ctx_1024t)) + 1e-12) * 0.953939
        ctx_1024 = -1.39393e-06 + 0.999914 * (_ctx_1024t + 0.3 * jax.random.normal(jax.random.fold_in(_rk, 611), (8, 722, 512), jnp.float32))
        return (x, ctx_1024)
    x, ctx_1024 = _rec_inputs()

    def _L0_xattn_setup():
        import jax, jax.numpy as jnp
        import numpy as np
        N_EMBD = 512
        N_HEADS = 16
        HEAD_DIM = N_EMBD // N_HEADS
        key = jax.random.key(seed)
        ks = jax.random.split(key, 12)
        B, T, S, C = (2, 1024, 1024, N_EMBD)
        std = 1.0 / np.sqrt(C)
        inp = {'x': jax.random.normal(ks[0], (B, T, C), dtype=jnp.float32), 'context': jax.random.normal(ks[1], (B, S, C), dtype=jnp.float32), 'q_w': jax.random.uniform(ks[2], (C, C), minval=-std, maxval=std, dtype=jnp.float32), 'q_b': jax.random.uniform(ks[3], (C,), minval=-std, maxval=std, dtype=jnp.float32), 'k_w': jax.random.uniform(ks[4], (C, C), minval=-std, maxval=std, dtype=jnp.float32), 'k_b': jax.random.uniform(ks[5], (C,), minval=-std, maxval=std, dtype=jnp.float32), 'v_w': jax.random.uniform(ks[6], (C, C), minval=-std, maxval=std, dtype=jnp.float32), 'v_b': jax.random.uniform(ks[7], (C,), minval=-std, maxval=std, dtype=jnp.float32), 'o_w': jax.random.uniform(ks[8], (C, C), minval=-std, maxval=std, dtype=jnp.float32), 'o_b': jax.random.uniform(ks[9], (C,), minval=-std, maxval=std, dtype=jnp.float32)}
        return inp
    _L0_xattn_all = _L0_xattn_setup()
    _L0_xattn_in = {k: v for k, v in _L0_xattn_all.items() if k in ('q_w', 'q_b', 'k_w', 'k_b', 'v_w', 'v_b', 'o_w', 'o_b')}
    del _L0_xattn_all

    def _L0_ffn_setup():
        import jax, jax.numpy as jnp
        import numpy as np
        D = 512
        E = 8
        K = 2
        DF = 2048
        B, S = (2, 1024)
        EPS_LN = 1e-05
        EPS_TOPK = 1e-08

        def _xavier(key, shape, fan_in, fan_out, dtype=jnp.float32):
            bound = float(np.sqrt(6.0 / (fan_in + fan_out)))
            return jax.random.uniform(key, shape, dtype, -bound, bound)
        key = jax.random.key(seed)
        kx, kg, k1, k2 = jax.random.split(key, 4)
        return {'x': jax.random.normal(kx, (B, S, D), jnp.float32), 'gamma': jnp.ones((D,), jnp.float32), 'beta': jnp.zeros((D,), jnp.float32), 'Wg': _xavier(kg, (E, D), D, E), 'bg': jnp.zeros((E,), jnp.float32), 'W1': _xavier(k1, (E, DF, D), D, DF), 'b1': jnp.zeros((E, DF), jnp.float32), 'W2': _xavier(k2, (E, D, DF), DF, D), 'b2': jnp.zeros((E, D), jnp.float32)}
    _L0_ffn_all = _L0_ffn_setup()
    _L0_ffn_in = {k: v for k, v in _L0_ffn_all.items() if k in ('gamma', 'beta', 'Wg', 'bg', 'W1', 'b1', 'W2', 'b2')}
    del _L0_ffn_all

    def _L1_xattn_setup():
        import jax, jax.numpy as jnp
        import numpy as np
        DIM = 512
        HEADS = 16
        DIM_HEAD = 64
        INNER = HEADS * DIM_HEAD
        EPS = 1e-05

        def _split_heads(t):
            b, n, _ = t.shape
            return t.reshape(b, n, HEADS, DIM_HEAD).transpose(0, 2, 1, 3)
        key = jax.random.key(seed)
        ks = jax.random.split(key, 9)
        b, n, m = (2, 1024, 128)
        s = DIM ** (-0.5)
        return {'x': jax.random.normal(ks[0], (b, n, DIM), jnp.float32), 'memories': jax.random.normal(ks[1], (b, m, DIM), jnp.float32), 'ln_g': jnp.ones((DIM,), jnp.float32), 'ln_b': jnp.zeros((DIM,), jnp.float32), 'Wq': jax.random.normal(ks[2], (DIM, INNER), jnp.float32) * s, 'Wkv': jax.random.normal(ks[3], (DIM, 2 * INNER), jnp.float32) * s, 'Wm': jax.random.normal(ks[4], (DIM, INNER), jnp.float32) * s, 'Wo': jax.random.normal(ks[5], (INNER, DIM), jnp.float32) * s, 'bo': jnp.zeros((DIM,), jnp.float32)}
    _L1_xattn_all = _L1_xattn_setup()
    _L1_xattn_in = {k: v for k, v in _L1_xattn_all.items() if k in ('ln_g', 'ln_b', 'Wq', 'Wkv', 'Wm', 'Wo', 'bo')}
    del _L1_xattn_all

    def _L1_ffn_setup():
        import jax, jax.numpy as jnp
        import numpy as np
        D_MODEL = 512
        D_FFN = 1024
        N_EXPERTS = 8
        TOP_K = 2
        B, S = (2, 1024)
        LN_EPS = 1e-05
        key = jax.random.key(seed)
        ks = jax.random.split(key, 6)
        scale = 0.02
        x = jax.random.normal(ks[0], (B, S, D_MODEL), dtype=jnp.float32)
        w_router = jax.random.normal(ks[1], (N_EXPERTS, D_MODEL), dtype=jnp.float32) * scale
        w_gate = jax.random.normal(ks[2], (N_EXPERTS, D_FFN, D_MODEL), dtype=jnp.float32) * scale
        w_up = jax.random.normal(ks[3], (N_EXPERTS, D_FFN, D_MODEL), dtype=jnp.float32) * scale
        w_down = jax.random.normal(ks[4], (N_EXPERTS, D_MODEL, D_FFN), dtype=jnp.float32) * scale
        ln_gamma = jnp.ones((D_MODEL,), dtype=jnp.float32)
        ln_beta = jnp.zeros((D_MODEL,), dtype=jnp.float32)
        return {'x': x, 'w_router': w_router, 'w_gate': w_gate, 'w_up': w_up, 'w_down': w_down, 'ln_gamma': ln_gamma, 'ln_beta': ln_beta}
    _L1_ffn_all = _L1_ffn_setup()
    _L1_ffn_in = {k: v for k, v in _L1_ffn_all.items() if k in ('w_router', 'w_gate', 'w_up', 'w_down', 'ln_gamma', 'ln_beta')}
    del _L1_ffn_all
    return {'x': x, 'ctx_1024': ctx_1024, 'L0_xattn_q_w': _L0_xattn_in['q_w'], 'L0_xattn_q_b': _L0_xattn_in['q_b'], 'L0_xattn_k_w': _L0_xattn_in['k_w'], 'L0_xattn_k_b': _L0_xattn_in['k_b'], 'L0_xattn_v_w': _L0_xattn_in['v_w'], 'L0_xattn_v_b': _L0_xattn_in['v_b'], 'L0_xattn_o_w': _L0_xattn_in['o_w'], 'L0_xattn_o_b': _L0_xattn_in['o_b'], 'L0_ffn_gamma': _L0_ffn_in['gamma'], 'L0_ffn_beta': _L0_ffn_in['beta'], 'L0_ffn_Wg': _L0_ffn_in['Wg'], 'L0_ffn_bg': _L0_ffn_in['bg'], 'L0_ffn_W1': _L0_ffn_in['W1'], 'L0_ffn_b1': _L0_ffn_in['b1'], 'L0_ffn_W2': _L0_ffn_in['W2'], 'L0_ffn_b2': _L0_ffn_in['b2'], 'L1_xattn_ln_g': _L1_xattn_in['ln_g'], 'L1_xattn_ln_b': _L1_xattn_in['ln_b'], 'L1_xattn_Wq': _L1_xattn_in['Wq'], 'L1_xattn_Wkv': _L1_xattn_in['Wkv'], 'L1_xattn_Wm': _L1_xattn_in['Wm'], 'L1_xattn_Wo': _L1_xattn_in['Wo'], 'L1_xattn_bo': _L1_xattn_in['bo'], 'L1_ffn_w_router': _L1_ffn_in['w_router'], 'L1_ffn_w_gate': _L1_ffn_in['w_gate'], 'L1_ffn_w_up': _L1_ffn_in['w_up'], 'L1_ffn_w_down': _L1_ffn_in['w_down'], 'L1_ffn_ln_gamma': _L1_ffn_in['ln_gamma'], 'L1_ffn_ln_beta': _L1_ffn_in['ln_beta']}

def reference(x, ctx_1024, L0_xattn_q_w, L0_xattn_q_b, L0_xattn_k_w, L0_xattn_k_b, L0_xattn_v_w, L0_xattn_v_b, L0_xattn_o_w, L0_xattn_o_b, L0_ffn_gamma, L0_ffn_beta, L0_ffn_Wg, L0_ffn_bg, L0_ffn_W1, L0_ffn_b1, L0_ffn_W2, L0_ffn_b2, L1_xattn_ln_g, L1_xattn_ln_b, L1_xattn_Wq, L1_xattn_Wkv, L1_xattn_Wm, L1_xattn_Wo, L1_xattn_bo, L1_ffn_w_router, L1_ffn_w_gate, L1_ffn_w_up, L1_ffn_w_down, L1_ffn_ln_gamma, L1_ffn_ln_beta):
    import jax
    import jax.numpy as jnp

    def _L0_xattn_ref(x, context, q_w, q_b, k_w, k_b, v_w, v_b, o_w, o_b):
        import jax, jax.numpy as jnp
        import numpy as np
        N_EMBD = 512
        N_HEADS = 16
        HEAD_DIM = N_EMBD // N_HEADS
        B, T, C = x.shape
        S = context.shape[1]
        H, D = (N_HEADS, HEAD_DIM)
        q = (x @ q_w + q_b).reshape(B, T, H, D).transpose(0, 2, 1, 3)
        k = (context @ k_w + k_b).reshape(B, S, H, D).transpose(0, 2, 1, 3)
        v = (context @ v_w + v_b).reshape(B, S, H, D).transpose(0, 2, 1, 3)
        att = jnp.einsum('bhtd,bhsd->bhts', q, k) / jnp.sqrt(jnp.float32(D))
        causal = jnp.tril(jnp.ones((T, S), dtype=bool))
        att = jnp.where(causal[None, None, :, :], att, -jnp.inf)
        att = jax.nn.softmax(att, axis=-1)
        y = jnp.einsum('bhts,bhsd->bhtd', att, v)
        y = y.transpose(0, 2, 1, 3).reshape(B, T, C)
        return y @ o_w + o_b

    def _L0_ffn_ref(x, gamma, beta, Wg, bg, W1, b1, W2, b2):
        import jax, jax.numpy as jnp
        import numpy as np
        D = 512
        E = 8
        K = 2
        DF = 2048
        B, S = (2, 1024)
        EPS_LN = 1e-05
        EPS_TOPK = 1e-08

        def _xavier(key, shape, fan_in, fan_out, dtype=jnp.float32):
            bound = float(np.sqrt(6.0 / (fan_in + fan_out)))
            return jax.random.uniform(key, shape, dtype, -bound, bound)
        b, s, d = x.shape
        mu = jnp.mean(x, axis=-1, keepdims=True)
        var = jnp.mean((x - mu) ** 2, axis=-1, keepdims=True)
        xn = (x - mu) / jnp.sqrt(var + EPS_LN) * gamma + beta
        xf = xn.reshape(-1, d)
        logits = xf @ Wg.T + bg
        probs = jax.nn.softmax(logits, axis=-1)
        tp, ti = jax.lax.top_k(probs, K)
        tp = tp / (jnp.sum(tp, axis=-1, keepdims=True) + EPS_TOPK)
        w = jnp.sum(jax.nn.one_hot(ti, E, dtype=xf.dtype) * tp[..., None], axis=1)
        h = jax.nn.gelu(jnp.einsum('td,efd->tef', xf, W1) + b1, approximate=False)
        y = jnp.einsum('tef,edf->ted', h, W2) + b2
        out = jnp.einsum('ted,te->td', y, w)
        return x + out.reshape(b, s, d)

    def _L1_xattn_ref(x, memories, ln_g, ln_b, Wq, Wkv, Wm, Wo, bo):
        import jax, jax.numpy as jnp
        import numpy as np
        DIM = 512
        HEADS = 16
        DIM_HEAD = 64
        INNER = HEADS * DIM_HEAD
        EPS = 1e-05

        def _split_heads(t):
            b, n, _ = t.shape
            return t.reshape(b, n, HEADS, DIM_HEAD).transpose(0, 2, 1, 3)
        mu = jnp.mean(x, axis=-1, keepdims=True)
        var = jnp.mean(jnp.square(x - mu), axis=-1, keepdims=True)
        xn = (x - mu) * jax.lax.rsqrt(var + EPS) * ln_g + ln_b
        q = _split_heads(xn @ Wq)
        kv = xn @ Wkv
        k = _split_heads(kv[..., :INNER])
        v = _split_heads(kv[..., INNER:])
        mem = _split_heads(memories @ Wm)
        k = jnp.concatenate([k, mem], axis=2)
        v = jnp.concatenate([v, mem], axis=2)
        scale = DIM_HEAD ** (-0.5)
        dots = jnp.einsum('bhid,bhjd->bhij', q, k) * scale
        attn = jax.nn.softmax(dots, axis=-1)
        out = jnp.einsum('bhij,bhjd->bhid', attn, v)
        b, h, n, d = out.shape
        out = out.transpose(0, 2, 1, 3).reshape(b, n, h * d)
        return out @ Wo + bo

    def _L1_ffn_ref(x, w_router, w_gate, w_up, w_down, ln_gamma, ln_beta):
        import jax, jax.numpy as jnp
        import numpy as np
        D_MODEL = 512
        D_FFN = 1024
        N_EXPERTS = 8
        TOP_K = 2
        B, S = (2, 1024)
        LN_EPS = 1e-05
        logits = jnp.einsum('bsd,ed->bse', x, w_router)
        top_vals, top_idx = jax.lax.top_k(logits, TOP_K)
        rw = jax.nn.softmax(top_vals, axis=-1)
        gate = jnp.einsum('bsd,efd->ebsf', x, w_gate)
        up = jnp.einsum('bsd,efd->ebsf', x, w_up)
        h = jax.nn.silu(gate) * up
        y = jnp.einsum('ebsf,edf->bsed', h, w_down)
        sel = jnp.take_along_axis(y, top_idx[..., None], axis=2)
        out = jnp.sum(rw[..., None] * sel, axis=2)
        mu = jnp.mean(out, axis=-1, keepdims=True)
        var = jnp.mean(jnp.square(out - mu), axis=-1, keepdims=True)
        out = (out - mu) * jax.lax.rsqrt(var + LN_EPS)
        return out * ln_gamma + ln_beta
    x = x + _L0_xattn_ref(_layernorm(x, axis=-1), ctx_1024, L0_xattn_q_w, L0_xattn_q_b, L0_xattn_k_w, L0_xattn_k_b, L0_xattn_v_w, L0_xattn_v_b, L0_xattn_o_w, L0_xattn_o_b)
    x = x + _L0_ffn_ref(_layernorm(x, axis=-1), L0_ffn_gamma, L0_ffn_beta, L0_ffn_Wg, L0_ffn_bg, L0_ffn_W1, L0_ffn_b1, L0_ffn_W2, L0_ffn_b2)
    x = x + _L1_xattn_ref(_layernorm(x, axis=-1), ctx_1024, L1_xattn_ln_g, L1_xattn_ln_b, L1_xattn_Wq, L1_xattn_Wkv, L1_xattn_Wm, L1_xattn_Wo, L1_xattn_bo)
    x = x + _L1_ffn_ref(_layernorm(x, axis=-1), L1_ffn_w_router, L1_ffn_w_gate, L1_ffn_w_up, L1_ffn_w_down, L1_ffn_ln_gamma, L1_ffn_ln_beta)
    return x

_drawn_inputs = setup_inputs


def setup_inputs(seed=0):
    import zlib

    import numpy as np

    out = dict(_drawn_inputs(seed))
    spreads = {'L0_ffn_gamma': (1.0, 0.2),
     'L0_ffn_beta': (0.0, 0.1),
     'L0_ffn_bg': (0.0, 0.1),
     'L0_ffn_b1': (0.0, 0.1),
     'L0_ffn_b2': (0.0, 0.1),
     'L1_xattn_ln_g': (1.0, 0.2),
     'L1_xattn_ln_b': (0.0, 0.1),
     'L1_xattn_bo': (0.0, 0.1),
     'L1_ffn_ln_gamma': (1.0, 0.2),
     'L1_ffn_ln_beta': (0.0, 0.1)}
    factors = {'L0_xattn_q_b': 5.116, 'L0_xattn_k_b': 8.0}
    for name, (base, spread) in spreads.items():
        noise = np.random.default_rng([zlib.crc32(name.encode()), seed]).standard_normal(out[name].shape)
        drawn = base * np.exp(spread * noise) if base else spread * noise
        out[name] = jnp.asarray(drawn.astype(out[name].dtype))
    for name, factor in factors.items():
        out[name] = (out[name] * factor).astype(out[name].dtype)
    return out
```

```python
from contextlib import ExitStack

import numpy as np
import concourse.bass as bass
from concourse import mybir

F32 = mybir.dt.float32
I32 = mybir.dt.int32
U32 = mybir.dt.uint32
ALU = mybir.AluOpType
ACT = mybir.ActivationFunctionType
AX = mybir.AxisListType.X

B, T, D, S = 8, 100, 512, 722
DC = D // 128
E = 8
CAP = 256
PASSES = (2 * B * T + E * (CAP - 1)) // CAP
LEAST = -(-2 * B * T // CAP)
H0, HD0 = 16, 32
H1, HD1 = 16, 64
INNER = H1 * HD1
IC = INNER // 128
KEYS = T + S
HALF = KEYS // 2
SHALF = S // 2
MB = [(T + 128 * i, min(128, KEYS - T - 128 * i)) for i in range(-(-S // 128))]
KB1 = [(0, T)] + MB
EPS = 1e-5
NEG = -1.0e30


class Steps:

    def __init__(self, eng, sem, first=0):
        self.eng, self.sem, self.first, self.n = eng, sem, first, 0

    def note(self, ins):
        self.n += 1
        return ins.then_inc(self.sem, 1)

    def settle(self):
        self.eng.wait_ge(self.sem, self.first + self.n)

    def link(self, ins):
        self.note(ins)
        self.settle()


class Core:

    def __init__(self, nc, ctx, a):
        self.nc, self.ctx, self.a = nc, ctx, a
        self.ps = ctx.enter_context(nc.psum_tensor("banks", [128, 8, 512], F32))
        self.x = self.sb(ctx, "x_res", [T, B, D])
        self.z = self.sb(ctx, "z", [T, B, D])
        self.ident = self.sb(ctx, "ident", [128, 128])
        self.nhalf = self.sb(ctx, "nhalf", [T, B])
        self.oh = [self.sb(ctx, f"onehot{k}", [T, B, E]) for k in range(2)]
        self.wt = self.sb(ctx, "wt", [T, 2, B])
        self.slot = self.sb(ctx, "slot", [T, 2, B], U32)
        self.table = self.sb(ctx, "table", [1, 16], I32)
        self.rows = nc.dram_tensor("slot_rows", (PASSES * CAP, D), F32, kind="Internal").ap()
        self.outs = nc.dram_tensor("slot_outs", (PASSES * CAP, D), F32, kind="Internal").ap()

    def sb(self, ctx, name, shape, dt=F32):
        return ctx.enter_context(self.nc.sbuf_tensor(name, shape, dt))

    def sem(self, name):
        return self.ctx.enter_context(self.nc.semaphore(name))


def bc(ap, n):
    return ap.unsqueeze(len(ap.shape)).broadcast_to(list(ap.shape) + [n])


def row_stats(k, dve, own, src, st, mv, rs, var_ready, rstd_ready, turn):
    nc = k.nc
    for b in range(B):
        own.note(nc.vector.bn_stats(st[:, b, :], src[:, b, :]))
    own.settle()
    for b in range(B):
        own.note(nc.vector.bn_aggr(mv[:, b, :], st[:, b, :]))
    own.settle()
    nc.vector.tensor_scalar(rs[:], mv[:, :, 1], EPS, None, ALU.add).then_inc(var_ready, 1)
    dve.wait_ge(rstd_ready, turn)


def root(k, pool, rs, var_ready, rstd_ready, turn):
    pool.wait_ge(var_ready, turn)
    pool.tensor_tensor(rs[:], rs[:], k.nhalf[:], ALU.pow).then_inc(rstd_ready, 1)


def at(tile, b):
    return tile[:, bass.ds(b, 1), :].rearrange("p b d -> p (b d)")


def attention_0(k):
    nc, a, ps = k.nc, k.a, k.ps
    with ExitStack() as c:
        w = {n: k.sb(c, f"a0_{n}", [128, DC, D]) for n in "qkvo"}
        qb = k.sb(c, "a0_qb", [128, DC])
        kb = k.sb(c, "a0_kb", [128, DC])
        vb = k.sb(c, "a0_vb", [T, D])
        ob = k.sb(c, "a0_ob", [T, D])
        mask = k.sb(c, "a0_mask", [T, T])
        ctxT = [k.sb(c, f"a0_ctx{u}", [128, DC, T]) for u in range(2)]
        xn = [k.sb(c, f"a0_xn{u}", [T, D]) for u in range(2)]
        xT = [k.sb(c, f"a0_xT{u}", [128, DC, T]) for u in range(2)]
        qT = [k.sb(c, f"a0_qT{u}", [128, DC, T]) for u in range(2)]
        kD = [k.sb(c, f"a0_kD{u}", [128, DC, 4, T]) for u in range(2)]
        v = [k.sb(c, f"a0_v{u}", [T, D]) for u in range(2)]
        P = [k.sb(c, f"a0_P{u}", [T, H0, T]) for u in range(2)]
        PT = [k.sb(c, f"a0_PT{u}", [T, H0, T]) for u in range(2)]
        yT = [k.sb(c, f"a0_yT{u}", [128, DC, T]) for u in range(2)]
        st = k.sb(c, "a0_st", [T, B, 6])
        mv = k.sb(c, "a0_mv", [T, B, 2])
        rs = k.sb(c, "a0_rs", [T, B])
        own_s, va, ri = k.sem("a0_stats_own"), k.sem("a0_variance"), k.sem("a0_rstd")
        nmax = [k.sb(c, f"a0_nm{u}", [T, H0]) for u in range(2)]
        sums = [k.sb(c, f"a0_sum{u}", [T, H0]) for u in range(2)]
        rinv = k.sb(c, "a0_rinv", [T, H0])
        zero = k.sb(c, "a0_zero", [128, 2048])

        x_in = k.sem("a0_x_in")
        w_in = k.sem("a0_w_in")
        ctx_in = [k.sem(f"a0_ctx_in{u}") for u in range(2)]
        made = k.sem("a0_const")
        zmade = k.sem("a0_zero_made")
        zeroed = k.sem("a0_rows_zeroed")
        names = "xn t xT q qs kk ks v vs s nm e p y ys o os".split()
        m = {n: k.sem(f"a0_{n}_done") for n in names}
        pt, pts = k.sem("a0_pt_done"), k.sem("a0_pts_done")
        own_v, own_a = k.sem("a0_dve_own"), k.sem("a0_act_own")
        AHEAD = 2

        def done(b):
            return b + (1 + AHEAD)

        def done_before(b):
            return b + 1

        def schedule(front, back, loop):
            front(0, 0)
            with loop(0, B // 2 - 1) as i:
                front(i, 1)
                back(i, 0, False)
                front(i + 1, 0)
                back(i, 1, False)
            front(B // 2 - 1, 1)
            back(B // 2 - 1, 0, False)
            back(B // 2 - 1, 1, True)

        with nc.Block() as block:
            @block.sync
            def _(sp):
                for b in range(B):
                    sp.dma_start(k.x[:, b, :], a["x"][b]).then_inc(x_in, 16)
                sp.dma_start(w["q"][:], a["q_w"].rearrange("(c p) n -> p c n", p=128)).then_inc(w_in, 16)
                sp.dma_start(w["k"][:], a["k_w"].rearrange("(c p) n -> p c n", p=128)).then_inc(w_in, 16)
                sp.dma_start(w["v"][:], a["v_w"].rearrange("(c p) n -> p c n", p=128)).then_inc(w_in, 16)
                sp.dma_start(qb[:], a["q_b"]).then_inc(w_in, 16)
                sp.dma_start(kb[:], a["k_b"]).then_inc(w_in, 16)
                sp.dma_start(vb[:], a["v_b"].partition_broadcast(T)).then_inc(w_in, 16)
                sp.dma_start(ob[:], a["o_b"].partition_broadcast(T)).then_inc(w_in, 16)
                sp.dma_start(w["o"][:], a["o_w"].rearrange("(c p) n -> p c n", p=128)).then_inc(w_in, 16)

                def load(i, u):
                    b = 2 * i + u
                    sp.wait_ge(m["v"], done_before(b))
                    src = a["ctxT"][bass.ds(b, 1)].rearrange("b (c p) s -> p (b c) s", p=128)
                    sp.dma_start(ctxT[u][:], src[:, :, 0:T]).then_inc(ctx_in[u], 16)

                load(0, 0)
                load(0, 1)
                with sp.Fori(1, B // 2) as i:
                    load(i, 0)
                    load(i, 1)

            @block.gpsimd
            def _(pool):
                pool.memset(k.ident[:], 0.0).then_inc(made, 1)
                pool.memset(mask[:], 0.0).then_inc(made, 1)
                pool.wait_ge(made, 2)
                pool.affine_select(out=k.ident[:], in_=k.ident[:], compare_op=ALU.not_equal, fill=1.0,
                                   base=0, pattern=[[-1, 128]], channel_multiplier=1).then_inc(made, 1)
                pool.affine_select(out=mask[:], in_=mask[:], compare_op=ALU.is_ge, fill=NEG,
                                   base=0, pattern=[[-1, T]], channel_multiplier=1).then_inc(made, 1)
                for u in range(2):
                    pool.memset(kD[u][:], 0.0).then_inc(made, 1)
                pool.memset(k.nhalf[:], -0.5).then_inc(made, 1)
                pool.wait_ge(made, 7)
                root(k, pool, rs, va, ri, 1)
                pool.memset(zero[:], 0.0).then_inc(zmade, 1)
                pool.wait_ge(zmade, 1)
                for r in range(PASSES * CAP // 512):
                    for t in (k.rows, k.outs):
                        pool.dma_start(t[512 * r:512 * (r + 1)].rearrange("(p s) d -> p (s d)", p=128),
                                       zero[:]).then_inc(zeroed, 16)
                pool.wait_ge(zeroed, 2 * 16 * (PASSES * CAP // 512))

            @block.tensor
            def _(pe):
                for n in "t q kk v s y o".split():
                    pe.sem_inc(m[n], AHEAD)
                pe.wait_ge(made, 7)
                pe.wait_ge(w_in, 16 * 8)

                def front(i, u):
                    b = 2 * i + u
                    pe.wait_ge(m["xn"], done(b))
                    pe.wait_ge(m["ys"], done_before(b))
                    for cc in range(DC):
                        mm = nc.tensor.transpose(ps[:, 4, T * cc:T * cc + T],
                                                 xn[u][:, 128 * cc:128 * cc + 128], k.ident[0:T, 0:T])
                    mm.then_inc(m["t"], 1)
                    pe.wait_ge(m["xT"], done(b))
                    pe.wait_ge(m["os"], done_before(b))
                    for mo in range(DC):
                        for cc in range(DC):
                            mm = nc.tensor.matmul(ps[:, 5, T * mo:T * mo + T],
                                                  w["q"][:, cc, 128 * mo:128 * mo + 128], xT[u][:, cc, :],
                                                  start=cc == 0, stop=cc == DC - 1)
                    mm.then_inc(m["q"], 1)
                    pe.wait_ge(ctx_in[u], 16 * i + 16)
                    for mo in range(DC):
                        for cc in range(DC):
                            mm = nc.tensor.matmul(ps[:, 4, T * mo:T * mo + T],
                                                  w["k"][:, cc, 128 * mo:128 * mo + 128], ctxT[u][:, cc, :],
                                                  start=cc == 0, stop=cc == DC - 1)
                    mm.then_inc(m["kk"], 1)
                    pe.wait_ge(m["qs"], done(b))
                    for cc in range(DC):
                        mm = nc.tensor.matmul(ps[0:T, 5, :], ctxT[u][:, cc, :], w["v"][:, cc, :],
                                              start=cc == 0, stop=cc == DC - 1)
                    mm.then_inc(m["v"], 1)
                    pe.wait_ge(m["ks"], done(b))
                    pe.wait_ge(m["nm"], b + AHEAD)
                    for g in range(4):
                        mm = nc.tensor.matmul(ps[0:T, g, 0:4 * T], qT[u][:, g, :],
                                              kD[u][:, g, :, :].rearrange("p h t -> p (h t)"),
                                              start=True, stop=True)
                    mm.then_inc(m["s"], 1)

                def back(i, u, last):
                    b = 2 * i + u
                    pe.wait_ge(m["p"], done(b))
                    for g in range(4):
                        pe.wait_ge(pts, 4 * b + g + 1)
                        for h in range(4 * g, 4 * g + 4):
                            mm = nc.tensor.transpose(ps[0:T, 6 + g % 2, T * (h % 4):T * (h % 4) + T],
                                                     P[u][:, h, :], k.ident[0:T, 0:T])
                        mm.then_inc(pt, 1)
                    if last:
                        pe.wait_ge(m["ks"], done(b))
                    else:
                        pe.wait_ge(m["ks"], done(b + 1))
                    for g in range(4):
                        pe.wait_ge(pts, 4 * b + g + 3)
                        for h in range(4 * g, 4 * g + 4):
                            mm = nc.tensor.matmul(ps[HD0 * (h % 4):HD0 * (h % 4) + HD0, 4, T * g:T * g + T],
                                                  v[u][:, HD0 * h:HD0 * h + HD0], PT[u][:, h, :],
                                                  start=True, stop=True)
                    mm.then_inc(m["y"], 1)
                    pe.wait_ge(m["ys"], done(b))
                    if last:
                        pe.wait_ge(m["vs"], done(b))
                    else:
                        pe.wait_ge(m["vs"], done(b + 1))
                    for cc in range(DC):
                        mm = nc.tensor.matmul(ps[0:T, 5, :], yT[u][:, cc, :], w["o"][:, cc, :],
                                              start=cc == 0, stop=cc == DC - 1)
                    mm.then_inc(m["o"], 1)

                schedule(front, back, pe.Fori)

            @block.vector
            def _(dve):
                for n in "xn xT qs ks vs nm p os".split():
                    dve.sem_inc(m[n], AHEAD)
                dve.wait_ge(x_in, 16 * B)
                dve.wait_ge(w_in, 16 * 8)
                dve.wait_ge(made, 7)
                row_stats(k, dve, Steps(dve, own_s), k.x, st, mv, rs, va, ri, 1)
                FRONT, BACK = 2, 2

                def front(i, u):
                    b = 2 * i + u
                    own = Steps(dve, own_v, 0 if type(b) is int and b == 0 else FRONT * b + BACK * (b - 1))
                    xb = at(k.x, b)
                    dve.wait_ge(m["t"], done_before(b))
                    nc.vector.tensor_scalar(xn[u][:], xb, at(mv, b)[:, 0:1], rs[:, bass.ds(b, 1)], ALU.subtract, ALU.mult)\
                        .then_inc(m["xn"], 1)
                    dve.wait_ge(m["t"], done(b))
                    nc.vector.tensor_copy(xT[u][:].rearrange("p c t -> p (c t)"), ps[:, 4, 0:DC * T])\
                        .then_inc(m["xT"], 1)
                    dve.wait_ge(m["q"], done(b))
                    nc.vector.tensor_tensor(qT[u][:], ps[:, 5, 0:DC * T].rearrange("p (c t) -> p c t", c=DC),
                                            bc(qb[:], T), ALU.add).then_inc(m["qs"], 1)
                    dve.wait_ge(m["kk"], done(b))
                    for r in range(4):
                        q = slice(32 * r, 32 * r + 32)
                        ins = nc.vector.tensor_tensor(kD[u][q, :, r, :],
                                                      ps[q, 4, 0:DC * T].rearrange("p (c t) -> p c t", c=DC),
                                                      bc(kb[q, :], T), ALU.add)
                    ins.then_inc(m["ks"], 1)
                    dve.wait_ge(m["v"], done(b))
                    nc.vector.tensor_tensor(v[u][:], ps[0:T, 5, :], vb[:], ALU.add).then_inc(m["vs"], 1)
                    dve.wait_ge(m["s"], done(b))
                    sc = ps[0:T, 0:4, 0:4 * T].rearrange("p g (h t) -> p g h t", h=4)
                    mk = mask[:].unsqueeze(1).unsqueeze(1).broadcast_to([T, 4, 4, T])
                    dve.wait_ge(m["y"], done_before(b))
                    own.link(nc.vector.tensor_tensor(P[u][:].rearrange("p (g h) t -> p g h t", h=4), sc, mk,
                                                     ALU.add))
                    own.link(nc.vector.tensor_reduce(nmax[u][:], P[u][:], AX, ALU.max, negate=True))
                    nc.vector.tensor_scalar(nmax[u][:], nmax[u][:], HD0 ** -0.5, None, ALU.mult)\
                        .then_inc(m["nm"], 1)
                    assert own.n == FRONT

                def back(i, u, last):
                    b = 2 * i + u
                    own = Steps(dve, own_v, FRONT * (b + 1 if last else b + 2) + BACK * b)
                    dve.wait_ge(m["e"], done(b))
                    own.link(nc.vector.reciprocal(rinv[:], sums[u][:]))
                    nc.vector.tensor_tensor(P[u][:], P[u][:], bc(rinv[:], T), ALU.mult).then_inc(m["p"], 1)
                    dve.wait_ge(m["o"], done(b))
                    xb = at(k.x, b)
                    own.link(nc.vector.tensor_tensor(xb, xb, ps[0:T, 5, :], ALU.add))
                    nc.vector.tensor_tensor(xb, xb, ob[:], ALU.add).then_inc(m["os"], 1)
                    assert own.n == BACK

                schedule(front, back, dve.Fori)

            @block.scalar
            def _(act):
                act.sem_inc(m["e"], AHEAD)
                act.sem_inc(m["ys"], AHEAD)
                act.sem_inc(pts, 2)

                def front(i, u):
                    b = 2 * i + u
                    act.wait_ge(m["nm"], done(b))
                    act.wait_ge(m["p"], done_before(b))
                    for h in range(H0):
                        ins = nc.scalar.activation(P[u][:, h, :], P[u][:, h, :], ACT.Exp, bias=nmax[u][:, h:h + 1],
                                                   scale=HD0 ** -0.5, accum_out=sums[u][:, h:h + 1])
                    ins.then_inc(m["e"], 1)

                def back(i, u, last):
                    b = 2 * i + u
                    act.wait_ge(m["y"], done_before(b))
                    for g in range(4):
                        act.wait_ge(pt, 4 * b + g + 1)
                        nc.scalar.copy(PT[u][:, 4 * g:4 * g + 4, :].rearrange("p h t -> p (h t)"),
                                       ps[0:T, 6 + g % 2, 0:4 * T]).then_inc(pts, 1)
                    act.wait_ge(m["y"], done(b))
                    act.wait_ge(m["o"], done_before(b))
                    nc.scalar.copy(yT[u][:].rearrange("p c t -> p (c t)"), ps[:, 4, 0:DC * T])\
                        .then_inc(m["ys"], 1)

                schedule(front, back, act.Fori)


def route(k, layer):
    nc, a, ps = k.nc, k.a, k.ps
    L = f"r{layer}_"
    with ExitStack() as c:
        rows = k.sb(c, L + "rows", [T, B, D]) if layer == 0 else k.z
        wg = k.sb(c, L + "wg", [128, DC, E])
        gam = k.sb(c, L + "gam", [128, DC])
        bet = k.sb(c, L + "bet", [128, DC])
        bg = k.sb(c, L + "bg", [T, E])
        xT = k.sb(c, L + "xT", [128, B, DC, T])
        st = k.sb(c, L + "st", [T, B, 6])
        mv = k.sb(c, L + "mv", [T, B, 2])
        rs = k.sb(c, L + "rs", [T, B])
        pr = k.sb(c, L + "pr", [T, B, E])
        t1 = k.sb(c, L + "t1", [T, B, E])
        m1 = k.sb(c, L + "m1", [T, 2, B])
        sm = k.sb(c, L + "sm", [T, B])
        rev = k.sb(c, L + "rev", [T, E])
        upper = k.sb(c, L + "upper", [T, T])
        ones = k.sb(c, L + "ones", [T, T])
        sel = k.sb(c, L + "sel", [T, B, E])
        before = k.sb(c, L + "before", [T, B + 1, E])
        npass = k.sb(c, L + "npass", [T, E])
        start = k.sb(c, L + "start", [T, E + 1])
        slotf = k.sb(c, L + "slotf", [T, 2, B])
        passno = k.sb(c, L + "passno", [1, PASSES, E])
        tf = k.sb(c, L + "tf", [1, 16])

        w_in = k.sem(L + "w_in")
        made = k.sem(L + "const")
        norm = k.sem(L + "rows_ready")
        t_done, x_done = k.sem(L + "transposed"), k.sem(L + "xT_ready")
        lg = k.sem(L + "logits")
        ex, exd = k.sem(L + "exp_asked"), k.sem(L + "exp_done")
        sel_r, cnt = k.sem(L + "chosen"), k.sem(L + "counted")
        slots = k.sem(L + "slots")
        scat = k.sem(L + "scattered")
        own_v = k.sem(L + "dve_own")
        va, ri = k.sem(L + "variance"), k.sem(L + "rstd")
        NORMS = 2 - layer

        with nc.Block() as block:
            @block.sync
            def _(sp):
                sp.dma_start(wg[:], a[f"Wg{layer}"].rearrange("(c p) e -> p c e", p=128)).then_inc(w_in, 16)
                if layer == 0:
                    sp.dma_start(gam[:], a["gam0"]).then_inc(w_in, 16)
                    sp.dma_start(bet[:], a["bet0"]).then_inc(w_in, 16)
                    sp.dma_start(bg[:], a["bg0"].partition_broadcast(T)).then_inc(w_in, 16)

            @block.gpsimd
            def _(pool):
                pool.memset(ones[:], 1.0).then_inc(made, 1)
                pool.iota(rev[:], pattern=[[-1, E]], base=E, channel_multiplier=0,
                          allow_small_or_imprecise_dtypes=True).then_inc(made, 1)
                pool.iota(passno[:], pattern=[[1, PASSES], [0, E]], base=0, channel_multiplier=0,
                          allow_small_or_imprecise_dtypes=True).then_inc(made, 1)
                pool.wait_ge(made, 3)
                pool.affine_select(out=upper[:], in_=ones[:], compare_op=ALU.is_gt, fill=0.0,
                                   base=0, pattern=[[1, T]], channel_multiplier=-1).then_inc(made, 1)
                for n in range(NORMS):
                    root(k, pool, rs, va, ri, n + 1)
                pool.wait_ge(slots, 1)
                for b in range(B):
                    for j in range(2):
                        pool.indirect_dma_start(out=k.rows[:, :],
                                                out_offset=bass.IndirectOffsetOnAxis(ap=k.slot[:, j, b:b + 1], axis=0),
                                                in_=rows[:, b, :], in_offset=None).then_inc(scat, 16)
                pool.wait_ge(scat, 16 * 2 * B)

            @block.tensor
            def _(pe):
                for b in range(B):
                    pe.wait_ge(norm, b + 1)
                    if b >= 4:
                        pe.wait_ge(x_done, b - 3)
                    for cc in range(DC):
                        mm = nc.tensor.transpose(ps[:, b % 4, T * cc:T * cc + T],
                                                 rows[:, b, 128 * cc:128 * cc + 128], k.ident[0:T, 0:T])
                    mm.then_inc(t_done, 1)
                pe.wait_ge(w_in, 64 if layer == 0 else 16)
                for b in range(B):
                    pe.wait_ge(x_done, b + 1)
                    for cc in range(DC):
                        mm = nc.tensor.matmul(ps[0:T, 4, E * b:E * b + E], xT[:, b, cc, :], wg[:, cc, :],
                                              start=cc == 0, stop=cc == DC - 1)
                mm.then_inc(lg, 1)
                pe.wait_ge(sel_r, 1)
                pe.wait_ge(made, 4)
                flat = sel[:].rearrange("p b e -> p (b e)")
                nc.tensor.matmul(ps[0:T, 5, 0:B * E], upper[:], flat, start=True, stop=True)
                nc.tensor.matmul(ps[0:T, 6, 0:B * E], ones[:], flat, start=True, stop=True).then_inc(cnt, 1)

            @block.vector
            def _(dve):
                own = Steps(dve, own_v)

                def layernorm(turn, src, dst, last=None):
                    row_stats(k, dve, own, src, st, mv, rs, va, ri, turn)
                    for b in range(B):
                        ins = nc.vector.tensor_scalar(dst[:, b, :], src[:, b, :], mv[:, b, 0:1], rs[:, b:b + 1],
                                                      ALU.subtract, ALU.mult)
                        if last is None:
                            own.note(ins)
                        else:
                            ins.then_inc(last, 1)
                    if last is None:
                        own.settle()

                if layer == 0:
                    layernorm(1, k.x, k.z)
                    layernorm(2, k.z, rows, norm)
                    for b in range(B):
                        own.note(nc.vector.tensor_tensor(k.x[:, b, :], k.x[:, b, :], k.z[:, b, :], ALU.add))
                    dve.wait_ge(w_in, 64)
                else:
                    layernorm(1, k.x, k.z, norm)
                for b in range(B):
                    dve.wait_ge(t_done, b + 1)
                    if layer == 0:
                        for cc in range(DC):
                            ins = nc.vector.tensor_scalar(xT[:, b, cc, :], ps[:, b % 4, T * cc:T * cc + T],
                                                          gam[:, cc:cc + 1], bet[:, cc:cc + 1], ALU.mult, ALU.add)
                    else:
                        ins = nc.vector.tensor_copy(xT[:, b].rearrange("p c t -> p (c t)"), ps[:, b % 4, 0:DC * T])
                    ins.then_inc(x_done, 1)
                dve.wait_ge(lg, 1)
                dve.wait_ge(made, 4)
                logits = ps[0:T, 4, 0:B * E].rearrange("p (b e) -> p b e", e=E)
                if layer == 0:
                    own.link(nc.vector.tensor_tensor(pr[:], logits, bg[:].unsqueeze(1).broadcast_to([T, B, E]), ALU.add))
                    own.link(nc.vector.tensor_reduce(sm[:], pr[:], AX, ALU.max))
                    nc.vector.tensor_tensor(pr[:], pr[:], bc(sm[:], E), ALU.subtract).then_inc(ex, 1)
                    dve.wait_ge(exd, 1)
                    own.link(nc.vector.tensor_reduce(sm[:], pr[:], AX, ALU.add))
                    own.link(nc.vector.reciprocal(sm[:], sm[:]))
                    own.link(nc.vector.tensor_tensor(pr[:], pr[:], bc(sm[:], E), ALU.mult))
                else:
                    own.link(nc.vector.tensor_copy(pr[:], logits))
                for j in range(2):
                    own.link(nc.vector.tensor_reduce(m1[:, j, :], pr[:], AX, ALU.max))
                    own.link(nc.vector.tensor_tensor(t1[:], pr[:], bc(m1[:, j, :], E), ALU.is_equal))
                    own.link(nc.vector.tensor_tensor(t1[:], t1[:], rev[:].unsqueeze(1).broadcast_to([T, B, E]), ALU.mult))
                    own.link(nc.vector.tensor_reduce(sm[:], t1[:], AX, ALU.max))
                    own.link(nc.vector.tensor_tensor(k.oh[j][:], bc(sm[:], E),
                                                     rev[:].unsqueeze(1).broadcast_to([T, B, E]), ALU.is_equal))
                    if j == 0:
                        own.link(nc.vector.scalar_tensor_tensor(out=pr[:], in0=k.oh[0][:], scalar=-3.0e38, in1=pr[:],
                                                                op0=ALU.mult, op1=ALU.add))
                nc.vector.tensor_tensor(sel[:], k.oh[0][:], k.oh[1][:], ALU.add).then_inc(sel_r, 1)
                if layer == 0:
                    own.link(nc.vector.tensor_tensor(sm[:], m1[:, 0, :], m1[:, 1, :], ALU.add))
                    own.link(nc.vector.tensor_scalar(sm[:], sm[:], 1e-8, None, ALU.add))
                    own.link(nc.vector.reciprocal(sm[:], sm[:]))
                    for j in range(2):
                        own.note(nc.vector.tensor_tensor(k.wt[:, j, :], m1[:, j, :], sm[:], ALU.mult))
                else:
                    nc.vector.tensor_tensor(sm[:], m1[:, 1, :], m1[:, 0, :], ALU.subtract).then_inc(ex, 1)
                    dve.wait_ge(exd, 1)
                    own.link(nc.vector.tensor_scalar(rs[:], sm[:], 1.0, None, ALU.add))
                    own.link(nc.vector.reciprocal(k.wt[:, 0, :], rs[:]))
                    own.note(nc.vector.tensor_tensor(k.wt[:, 1, :], k.wt[:, 0, :], sm[:], ALU.mult))
                own.note(nc.vector.memset(before[:, 0, :], 0.0))
                own.note(nc.vector.memset(start[:, 0:1], 0.0))
                own.link(nc.vector.memset(npass[:], 0.0))
                dve.wait_ge(cnt, 1)
                for b in range(B):
                    own.link(nc.vector.tensor_tensor(before[:, b + 1, :], before[:, b, :], ps[0:T, 6, E * b:E * b + E],
                                                     ALU.add))
                for n in range(-(-B * T // CAP)):
                    own.link(nc.vector.scalar_tensor_tensor(out=npass[:], in0=before[:, B, :], scalar=float(n * CAP),
                                                            in1=npass[:], op0=ALU.is_gt, op1=ALU.add))
                for e in range(E):
                    own.link(nc.vector.tensor_tensor(start[:, e + 1:e + 2], start[:, e:e + 1], npass[:, e:e + 1], ALU.add))
                own.link(nc.vector.scalar_tensor_tensor(out=pr[:], in0=start[:, 0:E].unsqueeze(1).broadcast_to([T, B, E]),
                                                        scalar=float(CAP), in1=before[:, 0:B, :],
                                                        op0=ALU.mult, op1=ALU.add))
                own.link(nc.vector.tensor_tensor(pr[:], pr[:], ps[0:T, 5, 0:B * E].rearrange("p (b e) -> p b e", e=E),
                                                 ALU.add))
                for j in range(2):
                    own.link(nc.vector.tensor_tensor(t1[:], pr[:], k.oh[j][:], ALU.mult))
                    own.link(nc.vector.tensor_reduce(slotf[:, j, :], t1[:], AX, ALU.add))
                nc.vector.tensor_copy(k.slot[:], slotf[:]).then_inc(slots, 1)
                own.link(nc.vector.tensor_tensor(passno[:], passno[:],
                                                 start[0:1, 1:E + 1].unsqueeze(1).broadcast_to([1, PASSES, E]), ALU.is_ge))
                own.note(nc.vector.memset(tf[:], 0.0))
                own.settle()
                own.link(nc.vector.tensor_reduce(tf[:, 0:PASSES], passno[:], AX, ALU.add))
                own.link(nc.vector.tensor_copy(tf[:, 15:16], start[0:1, E:E + 1]))
                own.link(nc.vector.tensor_copy(k.table[:], tf[:]))

            @block.scalar
            def _(act):
                act.wait_ge(ex, 1)
                if layer == 0:
                    nc.scalar.activation(pr[:], pr[:], ACT.Exp).then_inc(exd, 1)
                else:
                    nc.scalar.activation(sm[:], sm[:], ACT.Exp).then_inc(exd, 1)


def experts(k, layer):
    nc, a, ps = k.nc, k.a, k.ps
    L = f"e{layer}_"
    gated = layer == 1
    FG = 2 if gated else 4
    NB = 4 * FG
    CH = 3 if gated else 2
    ups = ["wgate", "wup"] if gated else ["w1"]
    with ExitStack() as c:
        ring = [[k.sb(c, f"{L}w{g}_{n}", [128, 4, 512]) for n in range(CH)] for g in range(FG)]
        xs = k.sb(c, L + "xs", [128, 2, D])
        xT = k.sb(c, L + "xT", [128, DC, CAP])
        hT = [k.sb(c, f"{L}hT{n}", [128, CAP]) for n in range(4)]
        gt = [k.sb(c, f"{L}gt{n}", [128, CAP]) for n in range(2)]
        y = k.sb(c, L + "y", [128, 2, D])
        b1 = k.sb(c, L + "b1", [128, E * NB])
        gam = k.sb(c, L + "gam", [128, DC])
        bet = k.sb(c, L + "bet", [128, DC])

        w_in = [[k.sem(f"{L}w_in{g}_{n}") for n in range(CH)] for g in range(FG)]
        c_in, x_in = k.sem(L + "c_in"), k.sem(L + "x_in")
        t_done, xT_v, xT_a = k.sem(L + "transposed"), k.sem(L + "xT_dve"), k.sem(L + "xT_act")
        up_done, out_done = k.sem(L + "up_done"), k.sem(L + "out_done")
        g_done, h_done = k.sem(L + "gate_done"), k.sem(L + "h_done")
        y_v, y_a, y_out, y_free = (k.sem(L + n) for n in ("y_dve", "y_act", "y_out", "y_free"))
        last = k.table[0:1, 15:16]

        with nc.Block() as block:
            @block.sync
            def _(sp):
                if not gated:
                    sp.dma_start(b1[:], a["b1"]).then_inc(c_in, 16)
                    sp.dma_start(gam[:], a["gam0"]).then_inc(c_in, 16)
                    sp.dma_start(bet[:], a["bet0"]).then_inc(c_in, 16)
                n = sp.value_load(last, min_val=LEAST, max_val=PASSES)
                with sp.Fori(0, n) as j:
                    e = sp.value_load(k.table[0:1, bass.ds(j, 1)], min_val=0, max_val=E - 1)
                    sp.wait_ge(t_done, j + 1)
                    sp.dma_start(xs[:], k.rows[bass.ds(j * CAP, CAP), :].rearrange("(s p) d -> p s d", p=128))\
                        .then_inc(x_in, 16)
                    for g in range(FG):
                        sp.wait_ge(up_done, NB * j + 4 * g + 4)
                        for i, name in enumerate(ups):
                            sp.dma_start(ring[g][i][:], a[name][bass.ds(e * FG + g, 1)]
                                         .rearrange("o p c f -> (o p) c f")).then_inc(w_in[g][i], 16)
                        sp.wait_ge(out_done, NB * j + 4 * g + 4)
                        sp.dma_start(ring[g][CH - 1][:], a[f"wout{layer}"][bass.ds(e * FG + g, 1)]
                                     .rearrange("o p c f -> (o p) c f")).then_inc(w_in[g][CH - 1], 16)

            @block.gpsimd
            def _(pool):
                n = pool.value_load(last, min_val=LEAST, max_val=PASSES)
                pool.sem_inc(y_free, 1)
                with pool.Fori(0, n) as j:
                    pool.wait_ge(y_v, j + 2)
                    pool.wait_ge(y_a, j + 2)
                    pool.dma_start(k.outs[bass.ds(j * CAP, CAP), :].rearrange("(s p) d -> p s d", p=128), y[:])\
                        .then_inc(y_out, 16)
                    pool.wait_ge(y_out, j * 16 + 16)
                    pool.sem_inc(y_free, 1)

            @block.tensor
            def _(pe):
                n = pe.value_load(last, min_val=LEAST, max_val=PASSES)
                pe.sem_inc(t_done, 1)
                pe.sem_inc(up_done, NB)
                pe.sem_inc(out_done, NB)
                with pe.Fori(0, n) as j:
                    pe.wait_ge(x_in, j * 16 + 16)
                    pe.wait_ge(xT_v, j + 1)
                    pe.wait_ge(xT_a, j + 1)
                    for s in range(2):
                        for cc in range(DC):
                            mm = nc.tensor.transpose(ps[:, 6 + s, 128 * cc:128 * cc + 128],
                                                     xs[:, s, 128 * cc:128 * cc + 128], k.ident[:])
                    mm.then_inc(t_done, 1)
                    pe.wait_ge(xT_v, j + 2)
                    pe.wait_ge(xT_a, j + 2)
                    for kb in range(NB + 2):
                        if kb < NB:
                            g = kb // 4
                            pe.wait_ge(h_done, NB * j + kb + (3 if gated else 1))
                            for i in range(len(ups)):
                                if kb % 4 == 0:
                                    pe.wait_ge(w_in[g][i], j * 16 + 16)
                                bank = 2 * i + kb % 2 if gated else kb % 4
                                for cc in range(DC):
                                    mm = nc.tensor.matmul(ps[:, bank, 0:CAP],
                                                          ring[g][i][:, cc, 128 * (kb % 4):128 * (kb % 4) + 128],
                                                          xT[:, cc, :], start=cc == 0, stop=cc == DC - 1)
                            mm.then_inc(up_done, 1)
                        if kb >= 2:
                            q = kb - 2
                            if q == 0:
                                pe.wait_ge(y_v, j + 1)
                                pe.wait_ge(y_a, j + 1)
                            if q % 4 == 0:
                                pe.wait_ge(w_in[q // 4][CH - 1], j * 16 + 16)
                            pe.wait_ge(h_done, NB * j + q + 5)
                            for s in range(2):
                                mm = nc.tensor.matmul(ps[:, 4 + s, :], hT[q % 4][:, 128 * s:128 * s + 128],
                                                      ring[q // 4][CH - 1][:, q % 4, :],
                                                      start=q == 0, stop=q == NB - 1)
                            mm.then_inc(out_done, 1)

            @block.vector
            def _(dve):
                n = dve.value_load(last, min_val=LEAST, max_val=PASSES)
                dve.sem_inc(xT_v, 1)
                dve.sem_inc(y_v, 1)
                if gated:
                    dve.sem_inc(h_done, 4)
                else:
                    dve.wait_ge(c_in, 48)
                with dve.Fori(0, n) as j:
                    dve.wait_ge(t_done, j + 2)
                    dve.wait_ge(up_done, j * NB + NB)
                    if gated:
                        ins = nc.vector.tensor_copy(xT[:, :, 0:128], ps[:, 6, :].rearrange("p (c t) -> p c t", c=DC))
                    else:
                        for cc in range(DC):
                            ins = nc.vector.tensor_scalar(xT[:, cc, 0:128], ps[:, 6, 128 * cc:128 * cc + 128],
                                                          gam[:, cc:cc + 1], bet[:, cc:cc + 1], ALU.mult, ALU.add)
                    ins.then_inc(xT_v, 1)
                    if gated:
                        for kb in range(NB):
                            dve.wait_ge(g_done, NB * j + kb + 1 + 2)
                            dve.wait_ge(out_done, NB * j + NB + kb - 3)
                            nc.vector.tensor_tensor(hT[kb % 4][:], gt[kb % 2][:], ps[:, 2 + kb % 2, 0:CAP],
                                                    ALU.mult).then_inc(h_done, 1)
                    dve.wait_ge(out_done, NB * j + 2 * NB)
                    dve.wait_ge(y_free, j + 1)
                    nc.vector.tensor_copy(y[:, 0, :], ps[:, 4, :]).then_inc(y_v, 1)

            @block.scalar
            def _(act):
                n = act.value_load(last, min_val=LEAST, max_val=PASSES)
                act.sem_inc(xT_a, 1)
                act.sem_inc(y_a, 1)
                if gated:
                    act.sem_inc(g_done, 2)
                else:
                    act.sem_inc(h_done, 4)
                    act.wait_ge(c_in, 48)
                with act.Fori(0, n) as j:
                    act.wait_ge(t_done, j + 2)
                    act.wait_ge(up_done, j * NB + NB)
                    if gated:
                        ins = nc.scalar.copy(xT[:, :, 128:256], ps[:, 7, :].rearrange("p (c t) -> p c t", c=DC))
                    else:
                        e = act.value_load(k.table[0:1, bass.ds(j, 1)], min_val=0, max_val=E - 1)
                        for cc in range(DC):
                            ins = nc.scalar.activation(xT[:, cc, 128:256], ps[:, 7, 128 * cc:128 * cc + 128],
                                                       ACT.Identity, bias=bet[:, cc:cc + 1], scale=gam[:, cc:cc + 1])
                    ins.then_inc(xT_a, 1)
                    for kb in range(NB):
                        act.wait_ge(up_done, NB * j + NB + kb + 1)
                        if gated:
                            act.wait_ge(h_done, NB * j + kb + 3)
                            nc.scalar.activation(gt[kb % 2][:], ps[:, kb % 2, 0:CAP], ACT.Silu).then_inc(g_done, 1)
                        else:
                            act.wait_ge(out_done, NB * j + NB + kb - 3)
                            nc.scalar.activation(hT[kb % 4][:], ps[:, kb % 4, 0:CAP], ACT.Gelu,
                                                 bias=b1[:, bass.ds(e * NB + kb, 1)]).then_inc(h_done, 1)
                    act.wait_ge(out_done, NB * j + 2 * NB)
                    act.wait_ge(y_free, j + 1)
                    nc.scalar.copy(y[:, 1, :], ps[:, 5, :]).then_inc(y_a, 1)


def combine(k, layer):
    nc, a, ps = k.nc, k.a, k.ps
    L = f"c{layer}_"
    with ExitStack() as c:
        y = k.sb(c, L + "y", [T, 2, B, D])
        w8 = k.sb(c, L + "w8", [T, B, E])
        w8b = k.sb(c, L + "w8b", [T, B, E])
        w8T = k.sb(c, L + "w8T", [E, B, T])
        b2 = k.sb(c, L + "b2", [E, D])
        lg = k.sb(c, L + "lg", [T, D])
        lb = k.sb(c, L + "lb", [T, D])
        st = k.sb(c, L + "st", [T, B, 6])
        mv = k.sb(c, L + "mv", [T, B, 2])
        rs = k.sb(c, L + "rs", [T, B])
        y_in = [k.sem(f"{L}y_in{b}") for b in range(B // 2)]
        c_in = k.sem(L + "c_in")
        wr, wt, wc = k.sem(L + "w8_ready"), k.sem(L + "w8_turned"), k.sem(L + "w8T_ready")
        bias, added = k.sem(L + "bias"), k.sem(L + "added")
        own_v, own_p = k.sem(L + "dve_own"), k.sem(L + "pool_own")
        fin, stored = k.sem(L + "out_ready"), k.sem(L + "stored")
        va, ri = k.sem(L + "variance"), k.sem(L + "rstd")
        with nc.Block() as block:
            @block.sync
            def _(sp):
                if layer == 0:
                    sp.dma_start(b2[:], a["b2"]).then_inc(c_in, 16)
                else:
                    sp.dma_start(lg[:], a["gam1"].partition_broadcast(T)).then_inc(c_in, 16)
                    sp.dma_start(lb[:], a["bet1"].partition_broadcast(T)).then_inc(c_in, 16)
                    for b in range(B):
                        sp.wait_ge(fin, b + 1)
                        sp.dma_start(a["out"][b], k.x[:, b, :]).then_inc(stored, 16)
                    sp.wait_ge(stored, 16 * B)

            @block.gpsimd
            def _(pool):
                for b in range(B):
                    for j in range(2):
                        pool.indirect_dma_start(out=y[:, j, b, :], out_offset=None, in_=k.outs[:, :],
                                                in_offset=bass.IndirectOffsetOnAxis(ap=k.slot[:, j, b:b + 1], axis=0))\
                            .then_inc(y_in[b // 2], 16)
                if layer == 1:
                    pool.wait_ge(va, B)
                    pool.tensor_tensor(rs[:], rs[:], k.nhalf[:], ALU.pow).then_inc(ri, 1)

            if layer == 0:
                @block.tensor
                def _(pe):
                    pe.wait_ge(wr, 1)
                    for b in range(B):
                        mm = nc.tensor.transpose(ps[0:E, b // 4, T * (b % 4):T * (b % 4) + T], w8[:, b, :],
                                                 k.ident[0:T, 0:T])
                    mm.then_inc(wt, 1)
                    pe.wait_ge(wc, 1)
                    pe.wait_ge(c_in, 16)
                    for b in range(B):
                        if b >= 4:
                            pe.wait_ge(added, b - 3)
                        nc.tensor.matmul(ps[0:T, 2 + b % 4, :], w8T[:, b, :], b2[:], start=True, stop=True)\
                            .then_inc(bias, 1)

            @block.vector
            def _(dve):
                own = Steps(dve, own_v)
                if layer == 0:
                    own.note(nc.vector.tensor_tensor(w8[:], k.oh[0][:], bc(k.wt[:, 0, :], E), ALU.mult))
                    own.link(nc.vector.tensor_tensor(w8b[:], k.oh[1][:], bc(k.wt[:, 1, :], E), ALU.mult))
                    nc.vector.tensor_tensor(w8[:], w8[:], w8b[:], ALU.add).then_inc(wr, 1)
                    dve.wait_ge(wt, 1)
                    for g in range(2):
                        ins = nc.vector.tensor_copy(w8T[:, 4 * g:4 * g + 4, :].rearrange("p b t -> p (b t)"),
                                                    ps[0:E, g, 0:4 * T])
                    ins.then_inc(wc, 1)
                    for b in range(B):
                        dve.wait_ge(y_in[b // 2], 64)
                        own.link(nc.vector.scalar_tensor_tensor(out=k.x[:, b, :], in0=y[:, 0, b, :],
                                                                scalar=k.wt[:, 0, b:b + 1], in1=k.x[:, b, :],
                                                                op0=ALU.mult, op1=ALU.add))
                        own.link(nc.vector.scalar_tensor_tensor(out=k.x[:, b, :], in0=y[:, 1, b, :],
                                                                scalar=k.wt[:, 1, b:b + 1], in1=k.x[:, b, :],
                                                                op0=ALU.mult, op1=ALU.add))
                        dve.wait_ge(bias, b + 1)
                        nc.vector.tensor_tensor(k.x[:, b, :], k.x[:, b, :], ps[0:T, 2 + b % 4, :], ALU.add)\
                            .then_inc(added, 1)
                else:
                    dve.wait_ge(c_in, 32)
                    for b in range(B):
                        dve.wait_ge(y_in[b // 2], 64)
                        z, y0, y1, xb = k.z[:, b, :], y[:, 0, b, :], y[:, 1, b, :], k.x[:, b, :]
                        own.link(nc.vector.tensor_scalar(y0, y0, k.wt[:, 0, b:b + 1], None, ALU.mult))
                        own.link(nc.vector.scalar_tensor_tensor(out=z, in0=y1, scalar=k.wt[:, 1, b:b + 1], in1=y0,
                                                                op0=ALU.mult, op1=ALU.add))
                        own.link(nc.vector.bn_stats(st[:, b, :], z))
                        own.link(nc.vector.bn_aggr(mv[:, b, :], st[:, b, :]))
                        nc.vector.tensor_scalar(rs[:, b:b + 1], mv[:, b, 1:2], EPS, None, ALU.add).then_inc(va, 1)
                    dve.wait_ge(ri, 1)
                    for b in range(B):
                        z, xb = k.z[:, b, :], k.x[:, b, :]
                        own.link(nc.vector.tensor_scalar(z, z, mv[:, b, 0:1], rs[:, b:b + 1], ALU.subtract, ALU.mult))
                        own.link(nc.vector.tensor_tensor(z, z, lg[:], ALU.mult))
                        own.link(nc.vector.tensor_tensor(xb, xb, lb[:], ALU.add))
                        nc.vector.tensor_tensor(xb, xb, z, ALU.add).then_inc(fin, 1)


def attention_1(k):
    nc, a, ps = k.nc, k.a, k.ps
    with ExitStack() as c:
        wq = k.sb(c, "a1_wq", [128, DC, INNER])
        wkv = k.sb(c, "a1_wkv", [128, DC, 2 * INNER])
        wm = k.sb(c, "a1_wm", [128, DC, INNER])
        wo = k.sb(c, "a1_wo", [128, IC, D])
        bo = k.sb(c, "a1_bo", [T, D])
        gam = k.sb(c, "a1_gam", [128, DC])
        bet = k.sb(c, "a1_bet", [128, DC])
        ctxT = k.sb(c, "a1_ctxT", [128, DC, S])
        xn = k.sb(c, "a1_xn", [T, D])
        xT = k.sb(c, "a1_xT", [128, DC, T])
        qD = k.sb(c, "a1_qD", [128, H1, T])
        kT = k.sb(c, "a1_kT", [128, IC, KEYS])
        v = k.sb(c, "a1_v", [128, len(KB1), INNER])
        P = [k.sb(c, f"a1_P{u}", [T, KEYS]) for u in range(2)]
        PT = [k.sb(c, f"a1_PT{u}", [128, len(KB1), T]) for u in range(2)]
        yT = k.sb(c, "a1_yT", [128, IC, T])
        st = k.sb(c, "a1_st", [T, B, 6])
        mv = k.sb(c, "a1_mv", [T, B, 2])
        rs = k.sb(c, "a1_rs", [T, B])
        own_s = k.sem("a1_stats_own")
        nmax = k.sb(c, "a1_nmax", [T, H1])
        sums = k.sb(c, "a1_sums", [T, H1])
        rinv = k.sb(c, "a1_rinv", [T, H1])

        w_in, ctx_in = k.sem("a1_w_in"), k.sem("a1_ctx_in")
        made = k.sem("a1_const")
        xn_r, t_done, xT_r = k.sem("a1_xn_ready"), k.sem("a1_transposed"), k.sem("a1_xT_ready")
        pj, pj_v, pj_a = k.sem("a1_projected"), k.sem("a1_copied_dve"), k.sem("a1_copied_act")
        sc, nm, ex = k.sem("a1_scores"), k.sem("a1_max"), k.sem("a1_exp")
        pn, pt, pts = k.sem("a1_prob"), k.sem("a1_prob_turned"), k.sem("a1_probT_ready")
        yd, ys = k.sem("a1_y"), k.sem("a1_yT_ready")
        od, os_ = k.sem("a1_o"), k.sem("a1_added")
        own_v = k.sem("a1_dve_own")
        va, ri = k.sem("a1_variance"), k.sem("a1_rstd")

        jobs = [("q", m) for m in range(IC // 4)] + [("k", m) for m in range(IC // 4)] \
            + [("v", m) for m in range(INNER // 512)] + [("m", m) for m in range(2 * IC)] \
            + [("t", (n, g)) for n in range(len(MB)) for g in range(2)]
        NJ = len(jobs)
        MEM_LAST = max(i for i, (kind, _) in enumerate(jobs) if kind == "m")
        assert NJ % 2 == 0
        HJ = NJ // 2

        def copied(eng, b, n):
            if n < 0:
                return
            eng.wait_ge(pj_v if n % 2 == 0 else pj_a, HJ * b + n // 2 + 1 + 2)

        def copy_out(eng, cp, add_bias, n):
            kind, i = jobs[n]
            bank = ps[:, n % 4, :]
            if kind == "q":
                src = bank[:, 0:4 * T].rearrange("p (m t) -> p m t", t=T)
                dst = qD[:].rearrange("p (m two) t -> p m two t", two=2)
                cp(dst[0:64, 4 * i:4 * i + 4, 0, :], src[0:64])
                return cp(dst[64:128, 4 * i:4 * i + 4, 1, :], src[64:128])
            if kind == "k":
                return cp(kT[:, 4 * i:4 * i + 4, 0:T], bank[:, 0:4 * T].rearrange("p (m t) -> p m t", t=T))
            if kind == "v":
                return cp(v[0:T, 0, 512 * i:512 * i + 512], bank[0:T, :])
            if kind == "m":
                m, hf = i // 2, i % 2
                return cp(kT[:, m, T + SHALF * hf:T + SHALF * (hf + 1)], bank[:, 0:SHALF])
            n_, g = i
            size = MB[n_][1]
            return cp(v[0:size, 1 + n_, 512 * g:512 * g + 512], bank[0:size, :])

        with nc.Block() as block:
            @block.sync
            def _(sp):
                sp.dma_start(gam[:], a["ln_g"]).then_inc(w_in, 16)
                sp.dma_start(bet[:], a["ln_b"]).then_inc(w_in, 16)
                sp.dma_start(bo[:], a["bo"].partition_broadcast(T)).then_inc(w_in, 16)
                sp.dma_start(wq[:], a["Wq"].rearrange("(c p) n -> p c n", p=128)).then_inc(w_in, 16)
                sp.dma_start(wkv[:], a["Wkv"].rearrange("(c p) n -> p c n", p=128)).then_inc(w_in, 16)
                sp.dma_start(ctxT[:], a["ctxT"][0].rearrange("(c p) s -> p c s", p=128)).then_inc(ctx_in, 16)
                sp.dma_start(wm[:], a["Wm"].rearrange("(c p) n -> p c n", p=128)).then_inc(w_in, 16)
                sp.dma_start(wo[:], a["Wo"].rearrange("(c p) n -> p c n", p=128)).then_inc(w_in, 16)
                with sp.Fori(1, B) as b:
                    sp.wait_ge(pj, NJ * (b - 1) + MEM_LAST + 1)
                    sp.dma_start(ctxT[:], a["ctxT"][bass.ds(b, 1)].rearrange("b (c p) s -> p (b c) s", p=128))\
                        .then_inc(ctx_in, 16)

            @block.gpsimd
            def _(pool):
                pool.memset(qD[:], 0.0).then_inc(made, 1)
                root(k, pool, rs, va, ri, 1)
                root(k, pool, rs, va, ri, 2)

            @block.tensor
            def _(pe):
                pe.sem_inc(t_done, 1)
                pe.sem_inc(od, 1)
                pe.sem_inc(yd, 2)
                pe.wait_ge(w_in, 16 * 7)
                with pe.Fori(0, B) as b:
                    pe.wait_ge(xn_r, b + 1)
                    pe.wait_ge(os_, b + 1)
                    for cc in range(DC):
                        mm = nc.tensor.transpose(ps[:, 7, T * cc:T * cc + T], xn[:, 128 * cc:128 * cc + 128],
                                                 k.ident[0:T, 0:T])
                    mm.then_inc(t_done, 1)
                    pe.wait_ge(xT_r, b + 1)
                    pe.wait_ge(ex, H1 * b + 2)
                    for n, (kind, i) in enumerate(jobs):
                        bank = ps[:, n % 4, :]
                        if n >= 4:
                            copied(pe, b, n - 4)
                        if kind in "qk":
                            for m in range(4):
                                for cc in range(DC):
                                    wt = wq if kind == "q" else wkv
                                    mm = nc.tensor.matmul(bank[:, T * m:T * m + T],
                                                          wt[:, cc, 128 * (4 * i + m):128 * (4 * i + m) + 128],
                                                          xT[:, cc, :], start=cc == 0, stop=cc == DC - 1)
                        elif kind == "v":
                            for cc in range(DC):
                                mm = nc.tensor.matmul(bank[0:T, :], xT[:, cc, :],
                                                      wkv[:, cc, INNER + 512 * i:INNER + 512 * i + 512],
                                                      start=cc == 0, stop=cc == DC - 1)
                        elif kind == "m":
                            if i == 0:
                                pe.wait_ge(ctx_in, b * 16 + 16)
                            m, hf = i // 2, i % 2
                            for cc in range(DC):
                                mm = nc.tensor.matmul(bank[:, 0:SHALF], wm[:, cc, 128 * m:128 * m + 128],
                                                      ctxT[:, cc, SHALF * hf:SHALF * hf + SHALF],
                                                      start=cc == 0, stop=cc == DC - 1)
                        else:
                            nb, g = i
                            first, size = MB[nb]
                            if g == 0 and nb == 0:
                                copied(pe, b, MEM_LAST)
                                copied(pe, b, MEM_LAST - 1)
                            for m in range(4):
                                mm = nc.tensor.transpose(bank[0:size, 128 * m:128 * m + 128],
                                                         kT[:, 4 * g + m, first:first + size], k.ident[:])
                        mm.then_inc(pj, 1)
                    copied(pe, b, NJ - 1)
                    copied(pe, b, NJ - 2)

                    def scores(h):
                        s = 2 * (h % 2)
                        if h >= 2:
                            pe.wait_ge(ex, H1 * b + h + 1)
                        for f in range(2):
                            mm = nc.tensor.matmul(ps[0:T, s + f, 0:HALF], qD[:, h, :],
                                                  kT[:, h // 2, HALF * f:HALF * f + HALF], start=True, stop=True)
                        mm.then_inc(sc, 1)

                    def turn(h):
                        pe.wait_ge(pn, H1 * b + h + 1 + 2)
                        pe.wait_ge(pts, H1 * b + h + 1)
                        for n, (first, size) in enumerate(KB1):
                            mm = nc.tensor.transpose(ps[0:size, 4 + n // 4, T * (n % 4):T * (n % 4) + T],
                                                     P[h % 2][:, first:first + size], k.ident[0:T, 0:T])
                        mm.then_inc(pt, 1)

                    def values(m):
                        pe.wait_ge(pts, H1 * b + 2 * m + 2 + 1)
                        pe.wait_ge(ys, IC * b + m + 1)
                        for n, (first, size) in enumerate(KB1):
                            for u in range(2):
                                h = 2 * m + u
                                mm = nc.tensor.matmul(ps[64 * u:64 * u + 64, 6, 0:T],
                                                      v[0:size, n, HD1 * h:HD1 * h + HD1], PT[u][0:size, n, :],
                                                      start=n == 0, stop=n == len(KB1) - 1)
                        mm.then_inc(yd, 1)

                    for m in range(IC + 1):
                        if m < IC:
                            scores(2 * m)
                        if m >= 1:
                            turn(2 * m - 2)
                        if m < IC:
                            scores(2 * m + 1)
                        if m >= 1:
                            turn(2 * m - 1)
                            values(m - 1)
                    pe.wait_ge(ys, IC * b + IC + 1)
                    for m in range(IC):
                        mm = nc.tensor.matmul(ps[0:T, 7, :], yT[:, m, :], wo[:, m, :], start=m == 0, stop=m == IC - 1)
                    mm.then_inc(od, 1)

            @block.vector
            def _(dve):
                dve.sem_inc(pj_v, 2)
                dve.sem_inc(pn, 2)
                dve.sem_inc(os_, 1)
                dve.wait_ge(w_in, 16 * 7)
                dve.wait_ge(made, 1)
                stats = Steps(dve, own_s)
                row_stats(k, dve, stats, k.x, st, mv, rs, va, ri, 1)
                for b in range(B):
                    stats.note(nc.vector.tensor_scalar(k.z[:, b, :], k.x[:, b, :], mv[:, b, 0:1], rs[:, b:b + 1],
                                                       ALU.subtract, ALU.mult))
                stats.settle()
                row_stats(k, dve, stats, k.z, st, mv, rs, va, ri, 2)
                OWN = 1 + H1
                with dve.Fori(0, B) as b:
                    own = Steps(dve, own_v, OWN * b)
                    xb = at(k.x, b)

                    dve.wait_ge(t_done, b + 1)
                    nc.vector.tensor_scalar(xn[:], at(k.z, b), at(mv, b)[:, 0:1], rs[:, bass.ds(b, 1)],
                                            ALU.subtract, ALU.mult).then_inc(xn_r, 1)
                    dve.wait_ge(t_done, b + 2)
                    for cc in range(DC):
                        ins = nc.vector.tensor_scalar(xT[:, cc, :], ps[:, 7, T * cc:T * cc + T],
                                                      gam[:, cc:cc + 1], bet[:, cc:cc + 1], ALU.mult, ALU.add)
                    ins.then_inc(xT_r, 1)
                    dve.wait_ge(yd, IC * b + 2)
                    for n in range(0, NJ, 2):
                        dve.wait_ge(pj, NJ * b + n + 1)
                        copy_out(dve, nc.vector.tensor_copy, None, n).then_inc(pj_v, 1)
                    def normalise(h):
                        dve.wait_ge(ex, H1 * b + h + 1 + 2)
                        own.link(nc.vector.reciprocal(rinv[:, h:h + 1], sums[:, h:h + 1]))
                        nc.vector.tensor_scalar(P[h % 2][:], P[h % 2][:], rinv[:, h:h + 1], None, ALU.mult)\
                            .then_inc(pn, 1)

                    for h in range(H1):
                        s = 2 * (h % 2)
                        dve.wait_ge(sc, H1 * b + h + 1)
                        nc.vector.tensor_reduce(nmax[:, h:h + 1], ps[0:T, s:s + 2, 0:HALF], mybir.AxisListType.XY,
                                                ALU.max, negate=True).then_inc(nm, 1)
                        if h >= 1:
                            normalise(h - 1)
                    normalise(H1 - 1)
                    dve.wait_ge(od, b + 2)
                    own.link(nc.vector.tensor_tensor(xb, xb, ps[0:T, 7, :], ALU.add))
                    nc.vector.tensor_tensor(xb, xb, bo[:], ALU.add).then_inc(os_, 1)
                    assert own.n == OWN, own.n

            @block.scalar
            def _(act):
                act.sem_inc(pj_a, 2)
                act.sem_inc(ex, 2)
                act.sem_inc(pts, 1)
                act.sem_inc(ys, 1)
                act.wait_ge(made, 1)
                own_a = k.sem("a1_act_own")
                with act.Fori(0, B) as b:
                    own = Steps(act, own_a, H1 * b)
                    act.wait_ge(yd, IC * b + 2)
                    for n in range(1, NJ, 2):
                        act.wait_ge(pj, NJ * b + n + 1)
                        copy_out(act, nc.scalar.copy, None, n).then_inc(pj_a, 1)

                    def copy_turned(h):
                        act.wait_ge(pt, H1 * b + h + 1)
                        act.wait_ge(yd, IC * b + h // 2 + 2 - 0)
                        nc.scalar.copy(PT[h % 2][:, 0:4, :].rearrange("p n t -> p (n t)"), ps[:, 4, 0:4 * T])
                        nc.scalar.copy(PT[h % 2][:, 4:7, :].rearrange("p n t -> p (n t)"), ps[:, 5, 0:3 * T])\
                            .then_inc(pts, 1)

                    def copy_y(m):
                        act.wait_ge(yd, IC * b + m + 1 + 2)
                        if m == 0:
                            act.wait_ge(od, b + 1)
                        nc.scalar.copy(yT[:, m, :], ps[:, 6, 0:T]).then_inc(ys, 1)

                    for h in range(H1):
                        if h >= 2:
                            copy_turned(h - 2)
                        if h >= 4 and h % 2 == 0:
                            copy_y(h // 2 - 2)
                        s = 2 * (h % 2)
                        act.wait_ge(nm, H1 * b + h + 1)
                        own.link(nc.scalar.mul(nmax[:, h:h + 1], nmax[:, h:h + 1], HD1 ** -0.5))
                        act.wait_ge(pt, H1 * b + h - 1) if h >= 2 else None
                        nc.scalar.activation(P[h % 2][:].rearrange("p (f t) -> p f t", f=2), ps[0:T, s:s + 2, 0:HALF],
                                             ACT.Exp, bias=nmax[:, h:h + 1], scale=HD1 ** -0.5,
                                             accum_out=sums[:, h:h + 1]).then_inc(ex, 1)
                    copy_turned(H1 - 2)
                    copy_y(IC - 2)
                    copy_turned(H1 - 1)
                    copy_y(IC - 1)


def build(nc, a):
    with ExitStack() as ctx:
        k = Core(nc, ctx, a)
        attention_0(k)
        route(k, 0)
        experts(k, 0)
        combine(k, 0)
        attention_1(k)
        route(k, 1)
        experts(k, 1)
        combine(k, 1)


def lay_out(i):
    g = {n: np.asarray(v) for n, v in i.items()}

    def chunks_in(w, fg):
        return w.reshape(E, fg, 512, DC, 128).transpose(0, 1, 4, 3, 2).reshape(E * fg, 128, DC, 512)

    def chunks_out(w, fg):
        return w.reshape(E, D, fg, 4, 128).transpose(0, 2, 4, 3, 1).reshape(E * fg, 128, 4, D)

    def column(b):
        return b.reshape(-1, 128).T

    p0, p1, q0, q1 = "L0_xattn_", "L1_xattn_", "L0_ffn_", "L1_ffn_"
    return {k_: np.ascontiguousarray(v) for k_, v in {
        "x": g["x"], "ctxT": g["ctx_1024"].transpose(0, 2, 1),
        "q_w": g[p0 + "q_w"], "k_w": g[p0 + "k_w"], "v_w": g[p0 + "v_w"], "o_w": g[p0 + "o_w"],
        "q_b": column(g[p0 + "q_b"]), "k_b": column(g[p0 + "k_b"]), "v_b": g[p0 + "v_b"], "o_b": g[p0 + "o_b"],
        "gam0": column(g[q0 + "gamma"]), "bet0": column(g[q0 + "beta"]),
        "Wg0": g[q0 + "Wg"].T, "bg0": g[q0 + "bg"],
        "w1": chunks_in(g[q0 + "W1"], 4), "b1": g[q0 + "b1"].reshape(E * 16, 128).T,
        "wout0": chunks_out(g[q0 + "W2"], 4), "b2": g[q0 + "b2"],
        "ln_g": column(g[p1 + "ln_g"]), "ln_b": column(g[p1 + "ln_b"]),
        "Wq": g[p1 + "Wq"], "Wkv": g[p1 + "Wkv"], "Wm": g[p1 + "Wm"], "Wo": g[p1 + "Wo"], "bo": g[p1 + "bo"],
        "Wg1": g[q1 + "w_router"].T, "wgate": chunks_in(g[q1 + "w_gate"], 2), "wup": chunks_in(g[q1 + "w_up"], 2),
        "wout1": chunks_out(g[q1 + "w_down"], 2), "gam1": g[q1 + "ln_gamma"], "bet1": g[q1 + "ln_beta"],
    }.items()}


def kernel(**inputs):
    import concourse.bacc as bacc
    from concourse.bass_utils import run_bass_kernel_spmd

    nc = bacc.Bacc("TRN2", target_bir_lowering=False, num_devices=1)
    arrays = lay_out(inputs)
    a = {n: nc.dram_tensor(n, v.shape, F32, kind="ExternalInput").ap() for n, v in arrays.items()}
    a["out"] = nc.dram_tensor("out", (B, T, D), F32, kind="ExternalOutput").ap()
    build(nc, a)
    r = run_bass_kernel_spmd(nc, [arrays], core_ids=[0])
    return r.results[0]["out"]
```

```python
from contextlib import ExitStack

import numpy as np
import concourse.bass as bass
from concourse import mybir

F32 = mybir.dt.float32
F32R = mybir.dt.float32r
I32 = mybir.dt.int32
U32 = mybir.dt.uint32
ALU = mybir.AluOpType
ACT = mybir.ActivationFunctionType
AX = mybir.AxisListType.X

B, T, D, S = 8, 100, 512, 722
DC = D // 128
E = 8
CAP = 256
PASSES = (2 * B * T + E * (CAP - 1)) // CAP
LEAST = -(-2 * B * T // CAP)
H0, HD0 = 16, 32
H1, HD1 = 16, 64
INNER = H1 * HD1
IC = INNER // 128
KEYS = T + S
HALF = KEYS // 2
SHALF = S // 2
MB = [(T + 128 * i, min(128, KEYS - T - 128 * i)) for i in range(-(-S // 128))]
KB1 = [(0, T)] + MB
EPS = 1e-5
NEG = -1.0e30


class Steps:

    def __init__(self, eng, sem, first=0):
        self.eng, self.sem, self.first, self.n = eng, sem, first, 0

    def note(self, ins):
        self.n += 1
        return ins.then_inc(self.sem, 1)

    def settle(self):
        self.eng.wait_ge(self.sem, self.first + self.n)

    def link(self, ins):
        self.note(ins)
        self.settle()


class Core:

    def __init__(self, nc, ctx, a):
        self.nc, self.ctx, self.a, self.sems = nc, ctx, a, []
        self.ps = ctx.enter_context(nc.psum_tensor("banks", [128, 8, 512], F32))
        self.x = self.sb(ctx, "x_res", [T, B, D])
        self.ident = self.sb(ctx, "ident", [128, 128])
        self.nhalf = self.sb(ctx, "nhalf", [T, B])
        self.oh = [self.sb(ctx, f"onehot{k}", [T, B, E]) for k in range(2)]
        self.wt = self.sb(ctx, "wt", [T, 2, B])
        self.slot = self.sb(ctx, "slot", [T, 2, B], U32)
        self.table = self.sb(ctx, "table", [1, 16], I32)
        self.rows = nc.dram_tensor("slot_rows", ((PASSES + 1) * CAP, D), F32, kind="Internal").ap()
        self.outs = nc.dram_tensor("slot_outs", (PASSES * CAP, D), F32, kind="Internal").ap()

    def sb(self, ctx, name, shape, dt=F32):
        return ctx.enter_context(self.nc.sbuf_tensor(name, shape, dt))

    def sem(self, name):
        self.sems.append(self.nc.alloc_semaphore(name=name))
        return self.sems[-1]

    def end_stage(self):
        self.nc.clear_and_free_semaphores(self.sems)
        self.nc.all_engine_barrier()
        self.sems = []


def bc(ap, n):
    return ap.unsqueeze(len(ap.shape)).broadcast_to(list(ap.shape) + [n])


def row_stats(k, dve, own, src, st, mv, rs, var_ready, rstd_ready, turn):
    nc = k.nc
    for b in range(B):
        own.note(nc.vector.bn_stats(st[:, b, :], src[:, b, :]))
    own.settle()
    for b in range(B):
        own.note(nc.vector.bn_aggr(mv[:, b, :], st[:, b, :]))
    own.settle()
    nc.vector.tensor_scalar(rs[:], mv[:, :, 1], EPS, None, ALU.add).then_inc(var_ready, 1)
    dve.wait_ge(rstd_ready, turn)


def root(k, pool, rs, var_ready, rstd_ready, turn):
    pool.wait_ge(var_ready, turn)
    pool.tensor_tensor(rs[:], rs[:], k.nhalf[:], ALU.pow).then_inc(rstd_ready, 1)


def at(tile, b):
    return tile[:, bass.ds(b, 1), :].rearrange("p b d -> p (b d)")


def attention_0(k):
    nc, a, ps = k.nc, k.a, k.ps
    with ExitStack() as c:
        w = {n: k.sb(c, f"a0_{n}", [128, DC, D]) for n in "qkvo"}
        qb = k.sb(c, "a0_qb", [128, DC])
        kb = k.sb(c, "a0_kb", [128, DC])
        vb = k.sb(c, "a0_vb", [T, D])
        ob = k.sb(c, "a0_ob", [T, D])
        mask = k.sb(c, "a0_mask", [T, T])
        ctxT = [k.sb(c, f"a0_ctx{u}", [128, DC, T]) for u in range(2)]
        xn = [k.sb(c, f"a0_xn{u}", [T, D]) for u in range(2)]
        xT = [k.sb(c, f"a0_xT{u}", [128, DC, T]) for u in range(2)]
        qT = [k.sb(c, f"a0_qT{u}", [128, DC, T]) for u in range(2)]
        kD = [k.sb(c, f"a0_kD{u}", [128, DC, 4, T]) for u in range(2)]
        v = [k.sb(c, f"a0_v{u}", [T, D]) for u in range(2)]
        P = [k.sb(c, f"a0_P{u}", [T, H0, T]) for u in range(2)]
        PT = [k.sb(c, f"a0_PT{u}", [T, H0, T]) for u in range(2)]
        yT = [k.sb(c, f"a0_yT{u}", [128, DC, T]) for u in range(2)]
        st = k.sb(c, "a0_st", [T, B, 6])
        mv = k.sb(c, "a0_mv", [T, B, 2])
        rs = k.sb(c, "a0_rs", [T, B])
        own_s, va, ri = k.sem("a0_stats_own"), k.sem("a0_variance"), k.sem("a0_rstd")
        nmax = [k.sb(c, f"a0_nm{u}", [T, H0]) for u in range(2)]
        sums = [k.sb(c, f"a0_sum{u}", [T, H0]) for u in range(2)]
        rinv = k.sb(c, "a0_rinv", [T, H0])
        zero = k.sb(c, "a0_zero", [128, CAP * D // 128])

        x_in = k.sem("a0_x_in")
        w_in = {n: k.sem(f"a0_w_in_{n}") for n in "qkvo"}
        b_in = k.sem("a0_b_in")
        kd_zero = k.sem("a0_kD_zero")
        ctx_in = [k.sem(f"a0_ctx_in{u}") for u in range(2)]
        made = k.sem("a0_const")
        zmade = k.sem("a0_zero_made")
        zeroed = k.sem("a0_rows_zeroed")
        names = "xn t xT q qs kk ks v vs s nm e p y ys o os".split()
        m = {n: k.sem(f"a0_{n}_done") for n in names}
        pt, pts = k.sem("a0_pt_done"), k.sem("a0_pts_done")
        own_v, own_a = k.sem("a0_dve_own"), k.sem("a0_act_own")
        AHEAD = 2

        def done(b):
            return b + (1 + AHEAD)

        def done_before(b):
            return b + 1

        def over_batches(loop, head, step, tail):
            head()
            with loop(0, B // 2 - 1) as i:
                step(2 * i + 1, 1, False)
                step(2 * i + 2, 0, False)
            step(B - 1, 1, True)
            tail(B - 1, 1)

        with nc.Block() as block:
            @block.sync
            def _(sp):
                for b in range(B):
                    sp.dma_start(k.x[:, b, :], a["x"][b]).then_inc(x_in, 16)
                sp.dma_start(qb[:], a["q_b"]).then_inc(b_in, 16)
                sp.dma_start(kb[:], a["k_b"]).then_inc(b_in, 16)
                sp.dma_start(vb[:], a["v_b"].partition_broadcast(T)).then_inc(b_in, 16)
                sp.dma_start(ob[:], a["o_b"].partition_broadcast(T)).then_inc(b_in, 16)

                def load(b, u):
                    sp.wait_ge(m["v"], done_before(b))
                    src = a["ctxT"][bass.ds(b, 1)].rearrange("b (c p) s -> p (b c) s", p=128)
                    sp.dma_start(ctxT[u][:], src[:, :, 0:T]).then_inc(ctx_in[u], 16)

                load(0, 0)
                load(1, 1)
                with sp.Fori(1, B // 2) as i:
                    load(2 * i, 0)
                    load(2 * i + 1, 1)

            @block.gpsimd
            def _(pool):
                pool.memset(k.ident[:], 0.0).then_inc(made, 1)
                pool.memset(mask[:], 0.0).then_inc(made, 1)
                pool.memset(k.nhalf[:], -0.5).then_inc(made, 1)
                pool.wait_ge(made, 3)
                pool.affine_select(out=k.ident[:], in_=k.ident[:], compare_op=ALU.not_equal, fill=1.0,
                                   base=0, pattern=[[-1, 128]], channel_multiplier=1).then_inc(made, 1)
                pool.affine_select(out=mask[:], in_=mask[:], compare_op=ALU.is_ge, fill=NEG,
                                   base=0, pattern=[[-1, T]], channel_multiplier=1).then_inc(made, 1)
                for u in range(2):
                    pool.memset(kD[u][:], 0.0).then_inc(kd_zero, 1)
                root(k, pool, rs, va, ri, 1)
                pool.memset(zero[:], 0.0).then_inc(zmade, 1)
                pool.wait_ge(zmade, 1)
                for t, n in ((k.rows, PASSES + 1), (k.outs, PASSES)):
                    for r in range(n):
                        pool.dma_start(t[CAP * r:CAP * (r + 1)].rearrange("(p s) d -> p (s d)", p=128),
                                       zero[:]).then_inc(zeroed, 16)
                pool.wait_ge(zeroed, 16 * (2 * PASSES + 1))

            @block.tensor
            def _(pe):
                for n in "t q kk v s y o".split():
                    pe.sem_inc(m[n], AHEAD)
                pe.wait_ge(made, 5)

                def turn(b, u, first=False):
                    pe.wait_ge(m["xn"], done(b))
                    if not first:
                        pe.wait_ge(pts, 4 * b - 3)
                    for cc in range(DC):
                        mm = nc.tensor.transpose(ps[:, 6, T * cc:T * cc + T],
                                                 xn[u][:, 128 * cc:128 * cc + 128], k.ident[0:T, 0:T])
                    mm.then_inc(m["t"], 1)

                def projections(b, u, first=False):
                    pe.wait_ge(m["xT"], done(b))
                    if first:
                        pe.wait_ge(w_in["q"], 16)
                    else:
                        pe.wait_ge(pts, 4 * b - 2)
                    for mo in range(DC):
                        for cc in range(DC):
                            mm = nc.tensor.matmul(ps[:, 7, T * mo:T * mo + T],
                                                  w["q"][:, cc, 128 * mo:128 * mo + 128], xT[u][:, cc, :],
                                                  start=cc == 0, stop=cc == DC - 1)
                    mm.then_inc(m["q"], 1)
                    pe.wait_ge(ctx_in[u], 8 * (b - u) + 16)
                    if first:
                        pe.wait_ge(w_in["k"], 16)
                    pe.wait_ge(m["ys"], done_before(b))
                    for mo in range(DC):
                        for cc in range(DC):
                            mm = nc.tensor.matmul(ps[:, 4, T * mo:T * mo + T],
                                                  w["k"][:, cc, 128 * mo:128 * mo + 128], ctxT[u][:, cc, :],
                                                  start=cc == 0, stop=cc == DC - 1)
                    mm.then_inc(m["kk"], 1)
                    if first:
                        pe.wait_ge(w_in["v"], 16)
                    pe.wait_ge(m["os"], done_before(b))
                    for cc in range(DC):
                        mm = nc.tensor.matmul(ps[0:T, 5, :], ctxT[u][:, cc, :], w["v"][:, cc, :],
                                              start=cc == 0, stop=cc == DC - 1)
                    mm.then_inc(m["v"], 1)

                def scores(b, u):
                    pe.wait_ge(m["ks"], done(b))
                    pe.wait_ge(m["nm"], b + AHEAD)
                    for g in range(4):
                        mm = nc.tensor.matmul(ps[0:T, g, 0:4 * T], qT[u][:, g, :],
                                              kD[u][:, g, :, :].rearrange("p h t -> p (h t)"),
                                              start=True, stop=True)
                    mm.then_inc(m["s"], 1)

                def turn_probabilities(b, u, last):
                    pe.wait_ge(m["p"], done(b))
                    for g in range(4):
                        if g == 0 and not last:
                            pe.wait_ge(m["xT"], done(b + 1))
                        if g == 1 and not last:
                            pe.wait_ge(m["qs"], done(b + 1))
                        if g >= 2:
                            pe.wait_ge(pts, 4 * b + g + 1)
                        for h in range(4 * g, 4 * g + 4):
                            mm = nc.tensor.transpose(ps[0:T, 6 + g % 2, T * (h % 4):T * (h % 4) + T],
                                                     P[u][:, h, :], k.ident[0:T, 0:T])
                        mm.then_inc(pt, 1)

                def attended(b, u, last):
                    pe.wait_ge(m["vs"], done(b))
                    if not last:
                        pe.wait_ge(m["ks"], done(b + 1))
                    for g in range(4):
                        pe.wait_ge(pts, 4 * b + g + 3)
                        for h in range(4 * g, 4 * g + 4):
                            mm = nc.tensor.matmul(ps[HD0 * (h % 4):HD0 * (h % 4) + HD0, 4, T * g:T * g + T],
                                                  v[u][:, HD0 * h:HD0 * h + HD0], PT[u][:, h, :],
                                                  start=True, stop=True)
                    mm.then_inc(m["y"], 1)

                def output(b, u, last):
                    pe.wait_ge(m["ys"], done(b))
                    if not last:
                        pe.wait_ge(m["vs"], done(b + 1))
                    for cc in range(DC):
                        mm = nc.tensor.matmul(ps[0:T, 5, :], yT[u][:, cc, :], w["o"][:, cc, :],
                                              start=cc == 0, stop=cc == DC - 1)
                    mm.then_inc(m["o"], 1)

                def head():
                    turn(0, 0, True)
                    projections(0, 0, True)
                    scores(0, 0)
                    turn(1, 1)
                    pe.wait_ge(w_in["o"], 16)

                def step(n, u, last):
                    projections(n, u)
                    turn_probabilities(n - 1, 1 - u, False)
                    scores(n, u)
                    attended(n - 1, 1 - u, False)
                    if not last:
                        turn(n + 1, 1 - u)
                    output(n - 1, 1 - u, False)

                def tail(b, u):
                    turn_probabilities(b, u, True)
                    attended(b, u, True)
                    output(b, u, True)

                over_batches(pe.Fori, head, step, tail)

            @block.vector
            def _(dve):
                for n in "xn xT qs ks vs nm p os".split():
                    dve.sem_inc(m[n], AHEAD)
                dve.wait_ge(x_in, 16 * B)
                row_stats(k, dve, Steps(dve, own_s), k.x, st, mv, rs, va, ri, 1)
                HEAD, STEP = 2, 4

                def normalise_rows(b, u):
                    dve.wait_ge(m["t"], done_before(b))
                    nc.vector.tensor_scalar(xn[u][:], at(k.x, b), at(mv, b)[:, 0:1], rs[:, bass.ds(b, 1)],
                                            ALU.subtract, ALU.mult).then_inc(m["xn"], 1)

                def rows_turned(b, u):
                    dve.wait_ge(m["t"], done(b))
                    nc.vector.tensor_copy(xT[u][:].rearrange("p c t -> p (c t)"), ps[:, 6, 0:DC * T])\
                        .then_inc(m["xT"], 1)

                def queries(b, u):
                    dve.wait_ge(m["q"], done(b))
                    nc.vector.tensor_tensor(qT[u][:], ps[:, 7, 0:DC * T].rearrange("p (c t) -> p c t", c=DC),
                                            bc(qb[:], T), ALU.add).then_inc(m["qs"], 1)

                def keys(b, u):
                    dve.wait_ge(m["kk"], done(b))
                    for r in range(4):
                        q = slice(32 * r, 32 * r + 32)
                        ins = nc.vector.tensor_tensor(kD[u][q, :, r, :],
                                                      ps[q, 4, 0:DC * T].rearrange("p (c t) -> p c t", c=DC),
                                                      bc(kb[q, :], T), ALU.add)
                    ins.then_inc(m["ks"], 1)

                def values(b, u):
                    dve.wait_ge(m["v"], done(b))
                    nc.vector.tensor_tensor(v[u][:], ps[0:T, 5, :], vb[:], ALU.add).then_inc(m["vs"], 1)

                def highest(b, u, own):
                    dve.wait_ge(m["s"], done(b))
                    sc = ps[0:T, 0:4, 0:4 * T].rearrange("p g (h t) -> p g h t", h=4)
                    mk = mask[:].unsqueeze(1).unsqueeze(1).broadcast_to([T, 4, 4, T])
                    dve.wait_ge(m["y"], done_before(b))
                    own.link(nc.vector.tensor_tensor(P[u][:].rearrange("p (g h) t -> p g h t", h=4), sc, mk,
                                                     ALU.add))
                    own.link(nc.vector.tensor_reduce(nmax[u][:], P[u][:], AX, ALU.max, negate=True))
                    nc.vector.tensor_scalar(nmax[u][:], nmax[u][:], HD0 ** -0.5, None, ALU.mult)\
                        .then_inc(m["nm"], 1)

                def normalise(b, u, own):
                    dve.wait_ge(m["e"], done(b))
                    own.link(nc.vector.reciprocal(rinv[:], sums[u][:]))
                    nc.vector.tensor_tensor(P[u][:], P[u][:], bc(rinv[:], T), ALU.mult).then_inc(m["p"], 1)

                def add_output(b, own):
                    dve.wait_ge(m["o"], done(b))
                    xb = at(k.x, b)
                    own.link(nc.vector.tensor_tensor(xb, xb, ps[0:T, 5, :], ALU.add))
                    nc.vector.tensor_tensor(xb, xb, ob[:], ALU.add).then_inc(m["os"], 1)

                def head():
                    own = Steps(dve, own_v)
                    normalise_rows(0, 0)
                    rows_turned(0, 0)
                    dve.wait_ge(b_in, 64)
                    queries(0, 0)
                    dve.wait_ge(kd_zero, 2)
                    keys(0, 0)
                    values(0, 0)
                    normalise_rows(1, 1)
                    highest(0, 0, own)
                    rows_turned(1, 1)
                    assert own.n == HEAD

                def step(n, u, last):
                    own = Steps(dve, own_v, HEAD + STEP * (n - 1))
                    queries(n, u)
                    normalise(n - 1, 1 - u, own)
                    keys(n, u)
                    values(n, u)
                    if not last:
                        normalise_rows(n + 1, 1 - u)
                    highest(n, u, own)
                    if not last:
                        rows_turned(n + 1, 1 - u)
                    add_output(n - 1, own)
                    assert own.n == STEP

                def tail(b, u):
                    own = Steps(dve, own_v, HEAD + STEP * b)
                    normalise(b, u, own)
                    add_output(b, own)

                over_batches(dve.Fori, head, step, tail)

            @block.scalar
            def _(act):
                for n in "qkvo":
                    act.dma_start(w[n][:], a[n + "_w"].rearrange("(c p) n -> p c n", p=128)).then_inc(w_in[n], 16)
                act.sem_inc(m["e"], AHEAD)
                act.sem_inc(m["ys"], AHEAD)
                act.sem_inc(pts, 2)

                def exponents(b, u):
                    act.wait_ge(m["nm"], done(b))
                    act.wait_ge(m["p"], done_before(b))
                    for h in range(H0):
                        ins = nc.scalar.activation(P[u][:, h, :], P[u][:, h, :], ACT.Exp, bias=nmax[u][:, h:h + 1],
                                                   scale=HD0 ** -0.5, accum_out=sums[u][:, h:h + 1])
                    ins.then_inc(m["e"], 1)

                def copy_turned(b, u):
                    act.wait_ge(m["y"], done_before(b))
                    for g in range(4):
                        act.wait_ge(pt, 4 * b + g + 1)
                        nc.scalar.copy(PT[u][:, 4 * g:4 * g + 4, :].rearrange("p h t -> p (h t)"),
                                       ps[0:T, 6 + g % 2, 0:4 * T]).then_inc(pts, 1)
                    act.wait_ge(m["y"], done(b))
                    act.wait_ge(m["o"], done_before(b))
                    nc.scalar.copy(yT[u][:].rearrange("p c t -> p (c t)"), ps[:, 4, 0:DC * T])\
                        .then_inc(m["ys"], 1)

                def step(n, u, last):
                    copy_turned(n - 1, 1 - u)
                    exponents(n, u)

                over_batches(act.Fori, lambda: exponents(0, 0), step, copy_turned)


def route(k, layer):
    nc, a, ps = k.nc, k.a, k.ps
    L = f"r{layer}_"
    with ExitStack() as c:
        z = k.sb(c, L + "z", [T, B, D])
        rows = k.sb(c, L + "rows", [T, B, D]) if layer == 0 else z
        wg = k.sb(c, L + "wg", [128, DC, E])
        gam = k.sb(c, L + "gam", [128, DC])
        bet = k.sb(c, L + "bet", [128, DC])
        bg = k.sb(c, L + "bg", [T, E])
        xT = k.sb(c, L + "xT", [128, B, DC, T])
        st = k.sb(c, L + "st", [T, B, 6])
        mv = k.sb(c, L + "mv", [T, B, 2])
        rs = k.sb(c, L + "rs", [T, B])
        pr = k.sb(c, L + "pr", [T, B, E])
        t1 = k.sb(c, L + "t1", [T, B, E])
        m1 = k.sb(c, L + "m1", [T, 2, B])
        sm = k.sb(c, L + "sm", [T, B])
        rev = k.sb(c, L + "rev", [T, E])
        upper = k.sb(c, L + "upper", [T, T])
        ones = k.sb(c, L + "ones", [T, T])
        sel = k.sb(c, L + "sel", [T, B, E])
        before = k.sb(c, L + "before", [T, B + 1, E])
        npass = k.sb(c, L + "npass", [T, E])
        start = k.sb(c, L + "start", [T, E + 1])
        slotf = k.sb(c, L + "slotf", [T, 2, B])
        passno = k.sb(c, L + "passno", [1, PASSES + 1, E])
        tf = k.sb(c, L + "tf", [1, 16])

        w_in = k.sem(L + "w_in")
        made = k.sem(L + "const")
        norm = k.sem(L + "rows_ready")
        t_done, x_done = k.sem(L + "transposed"), k.sem(L + "xT_ready")
        lg = k.sem(L + "logits")
        ex, exd = k.sem(L + "exp_asked"), k.sem(L + "exp_done")
        sel_r, cnt = k.sem(L + "chosen"), k.sem(L + "counted")
        slots = k.sem(L + "slots")
        scat = k.sem(L + "scattered")
        own_v = k.sem(L + "dve_own")
        va, ri = k.sem(L + "variance"), k.sem(L + "rstd")
        NORMS = 2 - layer

        with nc.Block() as block:
            @block.sync
            def _(sp):
                sp.dma_start(wg[:], a[f"Wg{layer}"].rearrange("(c p) e -> p c e", p=128)).then_inc(w_in, 16)
                if layer == 0:
                    sp.dma_start(gam[:], a["gam0"]).then_inc(w_in, 16)
                    sp.dma_start(bet[:], a["bet0"]).then_inc(w_in, 16)
                    sp.dma_start(bg[:], a["bg0"].partition_broadcast(T)).then_inc(w_in, 16)

            @block.gpsimd
            def _(pool):
                pool.memset(ones[:], 1.0).then_inc(made, 1)
                pool.iota(rev[:], pattern=[[-1, E]], base=E, channel_multiplier=0,
                          allow_small_or_imprecise_dtypes=True).then_inc(made, 1)
                pool.iota(passno[:], pattern=[[1, PASSES + 1], [0, E]], base=0, channel_multiplier=0,
                          allow_small_or_imprecise_dtypes=True).then_inc(made, 1)
                pool.wait_ge(made, 3)
                pool.affine_select(out=upper[:], in_=ones[:], compare_op=ALU.is_gt, fill=0.0,
                                   base=0, pattern=[[1, T]], channel_multiplier=-1).then_inc(made, 1)
                for n in range(NORMS):
                    root(k, pool, rs, va, ri, n + 1)
                pool.wait_ge(slots, 1)
                for b in range(B):
                    for j in range(2):
                        pool.indirect_dma_start(out=k.rows[:, :],
                                                out_offset=bass.IndirectOffsetOnAxis(ap=k.slot[:, j, b:b + 1], axis=0),
                                                in_=rows[:, b, :], in_offset=None).then_inc(scat, 16)
                pool.wait_ge(scat, 16 * 2 * B)

            @block.tensor
            def _(pe):
                for b in range(B):
                    pe.wait_ge(norm, b + 1)
                    if b >= 4:
                        pe.wait_ge(x_done, b - 3)
                    for cc in range(DC):
                        mm = nc.tensor.transpose(ps[:, b % 4, T * cc:T * cc + T],
                                                 rows[:, b, 128 * cc:128 * cc + 128], k.ident[0:T, 0:T])
                    mm.then_inc(t_done, 1)
                pe.wait_ge(w_in, 64 if layer == 0 else 16)
                for b in range(B):
                    pe.wait_ge(x_done, b + 1)
                    for cc in range(DC):
                        mm = nc.tensor.matmul(ps[0:T, 4, E * b:E * b + E], xT[:, b, cc, :], wg[:, cc, :],
                                              start=cc == 0, stop=cc == DC - 1)
                mm.then_inc(lg, 1)
                pe.wait_ge(sel_r, 1)
                pe.wait_ge(made, 4)
                flat = sel[:].rearrange("p b e -> p (b e)")
                nc.tensor.matmul(ps[0:T, 5, 0:B * E], upper[:], flat, start=True, stop=True)
                nc.tensor.matmul(ps[0:T, 6, 0:B * E], ones[:], flat, start=True, stop=True).then_inc(cnt, 1)

            @block.vector
            def _(dve):
                own = Steps(dve, own_v)

                def layernorm(turn, src, dst, last=None):
                    row_stats(k, dve, own, src, st, mv, rs, va, ri, turn)
                    for b in range(B):
                        ins = nc.vector.tensor_scalar(dst[:, b, :], src[:, b, :], mv[:, b, 0:1], rs[:, b:b + 1],
                                                      ALU.subtract, ALU.mult)
                        if last is None:
                            own.note(ins)
                        else:
                            ins.then_inc(last, 1)
                    if last is None:
                        own.settle()

                if layer == 0:
                    layernorm(1, k.x, z)
                    layernorm(2, z, rows, norm)
                    for b in range(B):
                        own.note(nc.vector.tensor_tensor(k.x[:, b, :], k.x[:, b, :], z[:, b, :], ALU.add))
                    dve.wait_ge(w_in, 64)
                else:
                    layernorm(1, k.x, z, norm)
                for b in range(B):
                    dve.wait_ge(t_done, b + 1)
                    if layer == 0:
                        for cc in range(DC):
                            ins = nc.vector.tensor_scalar(xT[:, b, cc, :], ps[:, b % 4, T * cc:T * cc + T],
                                                          gam[:, cc:cc + 1], bet[:, cc:cc + 1], ALU.mult, ALU.add)
                    else:
                        ins = nc.vector.tensor_copy(xT[:, b].rearrange("p c t -> p (c t)"), ps[:, b % 4, 0:DC * T])
                    ins.then_inc(x_done, 1)
                dve.wait_ge(lg, 1)
                dve.wait_ge(made, 4)
                logits = ps[0:T, 4, 0:B * E].rearrange("p (b e) -> p b e", e=E)
                if layer == 0:
                    own.link(nc.vector.tensor_tensor(pr[:], logits, bg[:].unsqueeze(1).broadcast_to([T, B, E]), ALU.add))
                    own.link(nc.vector.tensor_reduce(sm[:], pr[:], AX, ALU.max))
                    nc.vector.tensor_tensor(pr[:], pr[:], bc(sm[:], E), ALU.subtract).then_inc(ex, 1)
                    dve.wait_ge(exd, 1)
                    own.link(nc.vector.tensor_reduce(sm[:], pr[:], AX, ALU.add))
                    own.link(nc.vector.reciprocal(sm[:], sm[:]))
                    own.link(nc.vector.tensor_tensor(pr[:], pr[:], bc(sm[:], E), ALU.mult))
                else:
                    own.link(nc.vector.tensor_copy(pr[:], logits))
                for j in range(2):
                    own.link(nc.vector.tensor_reduce(m1[:, j, :], pr[:], AX, ALU.max))
                    own.link(nc.vector.tensor_tensor(t1[:], pr[:], bc(m1[:, j, :], E), ALU.is_equal))
                    own.link(nc.vector.tensor_tensor(t1[:], t1[:], rev[:].unsqueeze(1).broadcast_to([T, B, E]), ALU.mult))
                    own.link(nc.vector.tensor_reduce(sm[:], t1[:], AX, ALU.max))
                    own.link(nc.vector.tensor_tensor(k.oh[j][:], bc(sm[:], E),
                                                     rev[:].unsqueeze(1).broadcast_to([T, B, E]), ALU.is_equal))
                    if j == 0:
                        own.link(nc.vector.scalar_tensor_tensor(out=pr[:], in0=k.oh[0][:], scalar=-3.0e38, in1=pr[:],
                                                                op0=ALU.mult, op1=ALU.add))
                nc.vector.tensor_tensor(sel[:], k.oh[0][:], k.oh[1][:], ALU.add).then_inc(sel_r, 1)
                if layer == 0:
                    own.link(nc.vector.tensor_tensor(sm[:], m1[:, 0, :], m1[:, 1, :], ALU.add))
                    own.link(nc.vector.tensor_scalar(sm[:], sm[:], 1e-8, None, ALU.add))
                    own.link(nc.vector.reciprocal(sm[:], sm[:]))
                    for j in range(2):
                        own.note(nc.vector.tensor_tensor(k.wt[:, j, :], m1[:, j, :], sm[:], ALU.mult))
                else:
                    nc.vector.tensor_tensor(sm[:], m1[:, 1, :], m1[:, 0, :], ALU.subtract).then_inc(ex, 1)
                    dve.wait_ge(exd, 1)
                    own.link(nc.vector.tensor_scalar(rs[:], sm[:], 1.0, None, ALU.add))
                    own.link(nc.vector.reciprocal(k.wt[:, 0, :], rs[:]))
                    own.note(nc.vector.tensor_tensor(k.wt[:, 1, :], k.wt[:, 0, :], sm[:], ALU.mult))
                own.note(nc.vector.memset(before[:, 0, :], 0.0))
                own.note(nc.vector.memset(start[:, 0:1], 0.0))
                own.link(nc.vector.memset(npass[:], 0.0))
                dve.wait_ge(cnt, 1)
                for b in range(B):
                    own.link(nc.vector.tensor_tensor(before[:, b + 1, :], before[:, b, :], ps[0:T, 6, E * b:E * b + E],
                                                     ALU.add))
                for n in range(-(-B * T // CAP)):
                    own.link(nc.vector.scalar_tensor_tensor(out=npass[:], in0=before[:, B, :], scalar=float(n * CAP),
                                                            in1=npass[:], op0=ALU.is_gt, op1=ALU.add))
                for e in range(E):
                    own.link(nc.vector.tensor_tensor(start[:, e + 1:e + 2], start[:, e:e + 1], npass[:, e:e + 1], ALU.add))
                own.link(nc.vector.scalar_tensor_tensor(out=pr[:], in0=start[:, 0:E].unsqueeze(1).broadcast_to([T, B, E]),
                                                        scalar=float(CAP), in1=before[:, 0:B, :],
                                                        op0=ALU.mult, op1=ALU.add))
                own.link(nc.vector.tensor_tensor(pr[:], pr[:], ps[0:T, 5, 0:B * E].rearrange("p (b e) -> p b e", e=E),
                                                 ALU.add))
                for j in range(2):
                    own.link(nc.vector.tensor_tensor(t1[:], pr[:], k.oh[j][:], ALU.mult))
                    own.link(nc.vector.tensor_reduce(slotf[:, j, :], t1[:], AX, ALU.add))
                nc.vector.tensor_copy(k.slot[:], slotf[:]).then_inc(slots, 1)
                own.link(nc.vector.tensor_tensor(passno[:], passno[:],
                                                 start[0:1, 1:E + 1].unsqueeze(1).broadcast_to([1, PASSES + 1, E]), ALU.is_ge))
                own.note(nc.vector.memset(tf[:], 0.0))
                own.settle()
                own.link(nc.vector.tensor_reduce(tf[:, 0:PASSES + 1], passno[:], AX, ALU.add))
                own.link(nc.vector.tensor_scalar(tf[:], tf[:], float(E - 1), None, ALU.min))
                own.link(nc.vector.tensor_copy(tf[:, 15:16], start[0:1, E:E + 1]))
                own.link(nc.vector.tensor_copy(k.table[:], tf[:]))

            @block.scalar
            def _(act):
                act.wait_ge(ex, 1)
                if layer == 0:
                    nc.scalar.activation(pr[:], pr[:], ACT.Exp).then_inc(exd, 1)
                else:
                    nc.scalar.activation(sm[:], sm[:], ACT.Exp).then_inc(exd, 1)


def experts(k, layer):
    nc, a, ps = k.nc, k.a, k.ps
    L = f"e{layer}_"
    gated = layer == 1
    FG = 2 if gated else 4
    NB = 4 * FG
    ups = ["wgate", "wup"] if gated else ["w1"]
    CH = len(ups) + 1
    OUT = CH - 1
    Q = FG * CH
    RAW = Q // 2
    USED = 8
    with ExitStack() as c:
        raw = [k.sb(c, f"{L}raw{q}", [128, 4, 512]) for q in range(RAW)]
        hi = [[k.sb(c, f"{L}hi{u}_{n}", [128, 4, 512], F32R) for n in range(CH)] for u in range(2)]
        lo = [[k.sb(c, f"{L}lo{u}_{n}", [128, 4, 512], F32R) for n in range(CH)] for u in range(2)]
        xs = k.sb(c, L + "xs", [128, 2, D])
        xf = k.sb(c, L + "xf", [128, DC, CAP])
        xh = k.sb(c, L + "xh", [128, DC, CAP], F32R)
        xl = k.sb(c, L + "xl", [128, DC, CAP], F32R)
        hf = [k.sb(c, f"{L}hf{n}", [128, CAP]) for n in range(4)]
        hh = [k.sb(c, f"{L}hh{n}", [128, CAP], F32R) for n in range(4)]
        hl = [k.sb(c, f"{L}hl{n}", [128, CAP], F32R) for n in range(4)]
        gt = [k.sb(c, f"{L}gt{n}", [128, CAP]) for n in range(2)]
        y = k.sb(c, L + "y", [128, 2, D])
        b1 = k.sb(c, L + "b1", [128, E * NB])
        gam = k.sb(c, L + "gam", [128, DC])
        bet = k.sb(c, L + "bet", [128, DC])

        w_in = [k.sem(f"{L}w_in{q}") for q in range(Q)]
        c_in, x_in = k.sem(L + "c_in"), k.sem(L + "x_in")
        t_done, xf_v, xf_a = k.sem(L + "transposed"), k.sem(L + "xf_dve"), k.sem(L + "xf_act")
        xh_done, xl_done = k.sem(L + "xh_done"), k.sem(L + "xl_done")
        hi_done, lo_done = k.sem(L + "hi_done"), k.sem(L + "lo_done")
        up_done, out_done = k.sem(L + "up_done"), k.sem(L + "out_done")
        a_done, f_done = k.sem(L + "act_done"), k.sem(L + "hf_done")
        hh_done, h_done = k.sem(L + "hh_done"), k.sem(L + "hl_done")
        y_v, y_a, y_out, y_free = (k.sem(L + n) for n in ("y_dve", "y_act", "y_out", "y_free"))
        last = k.table[0:1, 15:16]

        def next_chunks(kb):
            g, r = kb // 4, kb % 4
            at_block = {0: [0], 1: [1], 2: [2]} if gated else {0: [0], 2: [1]}
            return [((g + 1) // FG, (g + 1) % FG, i) for i in at_block.get(r, [])]

        with nc.Block() as block:
            @block.sync
            def _(sp):
                if not gated:
                    sp.dma_start(b1[:], a["b1"]).then_inc(c_in, 16)
                    sp.dma_start(gam[:], a["gam0"]).then_inc(c_in, 16)
                    sp.dma_start(bet[:], a["bet0"]).then_inc(c_in, 16)
                n = sp.value_load(last, min_val=LEAST, max_val=PASSES)

                def rows(j):
                    sp.wait_ge(t_done, j + 1)
                    sp.dma_start(xs[:], k.rows[bass.ds(j * CAP, CAP), :].rearrange("(s p) d -> p s d", p=128))\
                        .then_inc(x_in, 16)

                def group(j, e, g):
                    for i in range(CH):
                        q = g * CH + i
                        src = a[ups[i] if i < OUT else f"wout{layer}"][bass.ds(e * FG + g, 1)]
                        sp.wait_ge(lo_done, Q * j + q + 1 + Q - RAW)
                        sp.dma_start(raw[q % RAW][:], src.rearrange("o p c f -> (o p) c f")).then_inc(w_in[q], 16)

                def expert(j):
                    return sp.value_load(k.table[0:1, bass.ds(j, 1)], min_val=0, max_val=E - 1)

                rows(0)
                group(0, expert(0), 0)
                with sp.Fori(0, n) as j:
                    e = expert(j)
                    for g in range(1, FG):
                        group(j, e, g)
                    rows(j + 1)
                    group(j + 1, expert(j + 1), 0)

            @block.gpsimd
            def _(pool):
                n = pool.value_load(last, min_val=LEAST, max_val=PASSES)
                pool.sem_inc(y_free, 1)
                with pool.Fori(0, n) as j:
                    pool.wait_ge(y_v, j + 2)
                    pool.wait_ge(y_a, j + 2)
                    pool.dma_start(k.outs[bass.ds(j * CAP, CAP), :].rearrange("(s p) d -> p s d", p=128), y[:])\
                        .then_inc(y_out, 16)
                    pool.wait_ge(y_out, j * 16 + 16)
                    pool.sem_inc(y_free, 1)

            @block.tensor
            def _(pe):
                n = pe.value_load(last, min_val=LEAST, max_val=PASSES)
                pe.sem_inc(t_done, 1)
                pe.sem_inc(up_done, USED)
                pe.sem_inc(out_done, USED)

                def turn(j):
                    pe.wait_ge(x_in, j * 16 + 16)
                    pe.wait_ge(xf_v, j + 1)
                    pe.wait_ge(xf_a, j + 1)
                    for s in range(2):
                        for cc in range(DC):
                            mm = nc.tensor.transpose(ps[:, 6 + s, 128 * cc:128 * cc + 128],
                                                     xs[:, s, 128 * cc:128 * cc + 128], k.ident[:])
                    mm.then_inc(t_done, 1)

                turn(0)
                with pe.Fori(0, n) as j:
                    for kb in range(NB + 2):
                        if kb < NB:
                            g = kb // 4
                            if kb == 0:
                                pe.wait_ge(xl_done, j + 1 + 1)
                            pe.wait_ge(f_done, NB * j + kb + (3 if gated else 1))
                            cut = slice(128 * (kb % 4), 128 * (kb % 4) + 128)
                            for i in range(len(ups)):
                                if kb % 4 == 0:
                                    pe.wait_ge(lo_done, Q * j + Q + g * CH + i + 1)
                                bank = 2 * i + kb % 2 if gated else kb % 4
                                wh, wl = hi[g % 2][i], lo[g % 2][i]
                                terms = [(w, x, cc) for cc in range(DC) for w, x in ((wh, xh), (wh, xl), (wl, xh))]
                                for t, (w, x, cc) in enumerate(terms):
                                    mm = nc.tensor.matmul(ps[:, bank, 0:CAP], w[:, cc, cut], x[:, cc, :],
                                                          start=t == 0, stop=t == len(terms) - 1)
                            mm.then_inc(up_done, 1)
                        if kb == NB - 3:
                            turn(j + 1)
                        if kb >= 2:
                            q = kb - 2
                            if q == 0:
                                pe.wait_ge(y_v, j + 1)
                                pe.wait_ge(y_a, j + 1)
                            if q % 4 == 0:
                                pe.wait_ge(lo_done, Q * j + Q + (q // 4) * CH + OUT + 1)
                            pe.wait_ge(h_done, NB * j + q + 4 + 1)
                            wh, wl = hi[q // 4 % 2][OUT], lo[q // 4 % 2][OUT]
                            for s in range(2):
                                cut = slice(128 * s, 128 * s + 128)
                                for t, (h, w) in enumerate(((hh, wh), (hh, wl), (hl, wh))):
                                    mm = nc.tensor.matmul(ps[:, 4 + s, :], h[q % 4][:, cut], w[:, q % 4, :],
                                                          start=q == 0 and t == 0, stop=q == NB - 1 and t == 2)
                            mm.then_inc(out_done, 1)

            @block.vector
            def _(dve):
                n = dve.value_load(last, min_val=LEAST, max_val=PASSES)
                dve.sem_inc(xf_v, 1)
                dve.sem_inc(xl_done, 1)
                dve.sem_inc(lo_done, Q)
                dve.sem_inc(h_done, 4)
                dve.sem_inc(y_v, 1)
                if gated:
                    dve.sem_inc(f_done, 4)
                else:
                    dve.wait_ge(c_in, 48)

                def low(j, g, i):
                    q = g * CH + i
                    dve.wait_ge(hi_done, Q * j + q + 1)
                    nc.vector.tensor_tensor(lo[g % 2][i][:], raw[q % RAW][:], hi[g % 2][i][:].bitcast(F32), ALU.subtract)\
                        .then_inc(lo_done, 1)

                def rows(j):
                    dve.wait_ge(t_done, j + 2)
                    dve.wait_ge(xl_done, j + 1)
                    if gated:
                        ins = nc.vector.tensor_copy(xf[:, :, 0:128], ps[:, 6, :].rearrange("p (c t) -> p c t", c=DC))
                    else:
                        for cc in range(DC):
                            ins = nc.vector.tensor_scalar(xf[:, cc, 0:128], ps[:, 6, 128 * cc:128 * cc + 128],
                                                          gam[:, cc:cc + 1], bet[:, cc:cc + 1], ALU.mult, ALU.add)
                    ins.then_inc(xf_v, 1)

                def rows_low(j):
                    dve.wait_ge(xh_done, j + 1)
                    nc.vector.tensor_tensor(xl[:], xf[:], xh[:].bitcast(F32), ALU.subtract).then_inc(xl_done, 1)

                rows(0)
                for i in range(CH):
                    low(0, 0, i)
                rows_low(0)
                with dve.Fori(0, n) as j:
                    for kb in range(NB):
                        dve.wait_ge(out_done, NB * j + USED + kb - 3)
                        if gated:
                            dve.wait_ge(a_done, NB * j + kb + 1 + 2)
                            nc.vector.tensor_tensor(hf[kb % 4][:], gt[kb % 2][:], ps[:, 2 + kb % 2, 0:CAP],
                                                    ALU.mult).then_inc(f_done, 1)
                        dve.wait_ge(f_done, NB * j + kb + 4 + 1)
                        nc.vector.tensor_copy(hh[kb % 4][:], hf[kb % 4][:]).then_inc(hh_done, 1)
                        dve.wait_ge(hh_done, NB * j + kb + 1)
                        nc.vector.tensor_tensor(hl[kb % 4][:], hf[kb % 4][:], hh[kb % 4][:].bitcast(F32),
                                                ALU.subtract).then_inc(h_done, 1)
                        for dj, g, i in next_chunks(kb):
                            low(j + dj, g, i)
                        if kb == NB - 2:
                            rows(j + 1)
                    rows_low(j + 1)
                    dve.wait_ge(out_done, NB * j + USED + NB)
                    dve.wait_ge(y_free, j + 1)
                    nc.vector.tensor_copy(y[:, 0, :], ps[:, 4, :]).then_inc(y_v, 1)

            @block.scalar
            def _(act):
                n = act.value_load(last, min_val=LEAST, max_val=PASSES)
                act.sem_inc(xf_a, 1)
                act.sem_inc(y_a, 1)
                if gated:
                    act.sem_inc(a_done, 2)
                else:
                    act.sem_inc(f_done, 4)
                    act.wait_ge(c_in, 48)

                def high(j, g, i):
                    q = g * CH + i
                    act.wait_ge(w_in[q], j * 16 + 16)
                    act.wait_ge(out_done if i == OUT else up_done, NB * j + 4 * g + 4)
                    nc.scalar.copy(hi[g % 2][i][:], raw[q % RAW][:]).then_inc(hi_done, 1)

                def rows(j):
                    act.wait_ge(t_done, j + 2)
                    act.wait_ge(xl_done, j + 1)
                    if gated:
                        ins = nc.scalar.copy(xf[:, :, 128:256], ps[:, 7, :].rearrange("p (c t) -> p c t", c=DC))
                    else:
                        for cc in range(DC):
                            ins = nc.scalar.activation(xf[:, cc, 128:256], ps[:, 7, 128 * cc:128 * cc + 128],
                                                       ACT.Identity, bias=bet[:, cc:cc + 1], scale=gam[:, cc:cc + 1])
                    ins.then_inc(xf_a, 1)

                def rows_high(j):
                    act.wait_ge(xf_v, j + 2)
                    act.wait_ge(xf_a, j + 2)
                    act.wait_ge(up_done, NB * j + USED)
                    nc.scalar.copy(xh[:], xf[:]).then_inc(xh_done, 1)

                rows(0)
                for i in range(CH):
                    high(0, 0, i)
                rows_high(0)
                with act.Fori(0, n) as j:
                    e = 0 if gated else act.value_load(k.table[0:1, bass.ds(j, 1)], min_val=0, max_val=E - 1)
                    for kb in range(NB):
                        act.wait_ge(up_done, NB * j + USED + kb + 1)
                        act.wait_ge(h_done, NB * j + kb + 1)
                        if gated:
                            act.wait_ge(f_done, NB * j + kb + 3)
                            nc.scalar.activation(gt[kb % 2][:], ps[:, kb % 2, 0:CAP], ACT.Silu).then_inc(a_done, 1)
                        else:
                            nc.scalar.activation(hf[kb % 4][:], ps[:, kb % 4, 0:CAP], ACT.Gelu,
                                                 bias=b1[:, bass.ds(e * NB + kb, 1)]).then_inc(f_done, 1)
                        for dj, g, i in next_chunks(kb):
                            high(j + dj, g, i)
                        if kb == NB - 2:
                            rows(j + 1)
                    rows_high(j + 1)
                    act.wait_ge(out_done, NB * j + USED + NB)
                    act.wait_ge(y_free, j + 1)
                    nc.scalar.copy(y[:, 1, :], ps[:, 5, :]).then_inc(y_a, 1)


def combine(k, layer, pr=None):
    nc, a, ps = k.nc, k.a, k.ps
    L = f"c{layer}_"
    with ExitStack() as c:
        y = k.sb(c, L + "y", [T, 2, B, D])
        zz = k.sb(c, L + "z", [T, B, D])
        w8 = k.sb(c, L + "w8", [T, B, E])
        w8b = k.sb(c, L + "w8b", [T, B, E])
        w8T = k.sb(c, L + "w8T", [E, B, T])
        b2 = k.sb(c, L + "b2", [E, D])
        lg = k.sb(c, L + "lg", [T, D])
        lb = k.sb(c, L + "lb", [T, D])
        st = k.sb(c, L + "st", [T, B, 6])
        mv = k.sb(c, L + "mv", [T, B, 2])
        rs = k.sb(c, L + "rs", [T, B])
        y_in = [k.sem(f"{L}y_in{b}") for b in range(B // 2)]
        c_in, ahead = k.sem(L + "c_in"), k.sem(L + "ahead")
        wr, wt, wc = k.sem(L + "w8_ready"), k.sem(L + "w8_turned"), k.sem(L + "w8T_ready")
        bias, added = k.sem(L + "bias"), k.sem(L + "added")
        own_v, own_p = k.sem(L + "dve_own"), k.sem(L + "pool_own")
        fin, stored = k.sem(L + "out_ready"), k.sem(L + "stored")
        va, ri = k.sem(L + "variance"), k.sem(L + "rstd")
        with nc.Block() as block:
            @block.sync
            def _(sp):
                if layer == 0:
                    sp.dma_start(b2[:], a["b2"]).then_inc(c_in, 16)
                    for n in range(4):
                        sp.dma_start(pr.raw[:, n], pr.chunk(a, n)).then_inc(ahead, 16)
                    sp.dma_start(pr.gam[:], a["ln_g"]).then_inc(ahead, 16)
                    sp.dma_start(pr.bet[:], a["ln_b"]).then_inc(ahead, 16)
                    sp.wait_ge(ahead, 96)
                else:
                    sp.dma_start(lg[:], a["gam1"].partition_broadcast(T)).then_inc(c_in, 16)
                    sp.dma_start(lb[:], a["bet1"].partition_broadcast(T)).then_inc(c_in, 16)
                    for b in range(B):
                        sp.wait_ge(fin, b + 1)
                        sp.dma_start(a["out"][b], k.x[:, b, :]).then_inc(stored, 16)
                    sp.wait_ge(stored, 16 * B)

            @block.gpsimd
            def _(pool):
                for b in range(B):
                    for j in range(2):
                        pool.indirect_dma_start(out=y[:, j, b, :], out_offset=None, in_=k.outs[:, :],
                                                in_offset=bass.IndirectOffsetOnAxis(ap=k.slot[:, j, b:b + 1], axis=0))\
                            .then_inc(y_in[b // 2], 16)
                if layer == 1:
                    pool.wait_ge(va, B)
                    pool.tensor_tensor(rs[:], rs[:], k.nhalf[:], ALU.pow).then_inc(ri, 1)

            if layer == 0:
                @block.tensor
                def _(pe):
                    pe.wait_ge(wr, 1)
                    for b in range(B):
                        mm = nc.tensor.transpose(ps[0:E, b // 4, T * (b % 4):T * (b % 4) + T], w8[:, b, :],
                                                 k.ident[0:T, 0:T])
                    mm.then_inc(wt, 1)
                    pe.wait_ge(wc, 1)
                    pe.wait_ge(c_in, 16)
                    for b in range(B):
                        if b >= 4:
                            pe.wait_ge(added, b - 3)
                        nc.tensor.matmul(ps[0:T, 2 + b % 4, :], w8T[:, b, :], b2[:], start=True, stop=True)\
                            .then_inc(bias, 1)

            @block.vector
            def _(dve):
                own = Steps(dve, own_v)
                if layer == 0:
                    own.note(nc.vector.tensor_tensor(w8[:], k.oh[0][:], bc(k.wt[:, 0, :], E), ALU.mult))
                    own.link(nc.vector.tensor_tensor(w8b[:], k.oh[1][:], bc(k.wt[:, 1, :], E), ALU.mult))
                    nc.vector.tensor_tensor(w8[:], w8[:], w8b[:], ALU.add).then_inc(wr, 1)
                    dve.wait_ge(wt, 1)
                    for g in range(2):
                        ins = nc.vector.tensor_copy(w8T[:, 4 * g:4 * g + 4, :].rearrange("p b t -> p (b t)"),
                                                    ps[0:E, g, 0:4 * T])
                    ins.then_inc(wc, 1)
                    for b in range(B):
                        dve.wait_ge(y_in[b // 2], 64)
                        own.link(nc.vector.scalar_tensor_tensor(out=k.x[:, b, :], in0=y[:, 0, b, :],
                                                                scalar=k.wt[:, 0, b:b + 1], in1=k.x[:, b, :],
                                                                op0=ALU.mult, op1=ALU.add))
                        own.link(nc.vector.scalar_tensor_tensor(out=k.x[:, b, :], in0=y[:, 1, b, :],
                                                                scalar=k.wt[:, 1, b:b + 1], in1=k.x[:, b, :],
                                                                op0=ALU.mult, op1=ALU.add))
                        dve.wait_ge(bias, b + 1)
                        nc.vector.tensor_tensor(k.x[:, b, :], k.x[:, b, :], ps[0:T, 2 + b % 4, :], ALU.add)\
                            .then_inc(added, 1)
                else:
                    dve.wait_ge(c_in, 32)
                    for b in range(B):
                        dve.wait_ge(y_in[b // 2], 64)
                        z, y0, y1, xb = zz[:, b, :], y[:, 0, b, :], y[:, 1, b, :], k.x[:, b, :]
                        own.link(nc.vector.tensor_scalar(y0, y0, k.wt[:, 0, b:b + 1], None, ALU.mult))
                        own.link(nc.vector.scalar_tensor_tensor(out=z, in0=y1, scalar=k.wt[:, 1, b:b + 1], in1=y0,
                                                                op0=ALU.mult, op1=ALU.add))
                        own.link(nc.vector.bn_stats(st[:, b, :], z))
                        own.link(nc.vector.bn_aggr(mv[:, b, :], st[:, b, :]))
                        nc.vector.tensor_scalar(rs[:, b:b + 1], mv[:, b, 1:2], EPS, None, ALU.add).then_inc(va, 1)
                    dve.wait_ge(ri, 1)
                    for b in range(B):
                        z, xb = zz[:, b, :], k.x[:, b, :]
                        own.link(nc.vector.tensor_scalar(z, z, mv[:, b, 0:1], rs[:, b:b + 1], ALU.subtract, ALU.mult))
                        own.link(nc.vector.tensor_tensor(z, z, lg[:], ALU.mult))
                        own.link(nc.vector.tensor_tensor(xb, xb, lb[:], ALU.add))
                        nc.vector.tensor_tensor(xb, xb, z, ALU.add).then_inc(fin, 1)


class Attention1:

    def __init__(self, k, ctx):
        nc = k.nc
        self.q = nc.dram_tensor("own_q", (2, B, 128, IC, T), F32, kind="Internal").ap()
        self.kk = nc.dram_tensor("own_k", (2, B, 128, IC, T), F32, kind="Internal").ap()
        self.v = nc.dram_tensor("own_v", (B, T, INNER), F32, kind="Internal").ap()
        self.wm = [k.sb(ctx, f"a1_wm{n}", [128, DC, INNER], F32R) for n in range(2)]
        self.wo = k.sb(ctx, "a1_wo", [128, IC, D])
        self.bo = k.sb(ctx, "a1_bo", [T, D])


class Projection:

    def __init__(self, k, ctx):
        self.raw = k.sb(ctx, "p_raw", [128, 4, DC, 512])
        self.gam = k.sb(ctx, "p_gam", [128, DC])
        self.bet = k.sb(ctx, "p_bet", [128, DC])

    @staticmethod
    def chunk(a, n):
        w, first = [(a["Wq"], 0), (a["Wkv"], 0), (a["Wkv"], INNER), (a["Wm"], 0)][n // 2]
        first += 512 * (n % 2)
        return w[:, first:first + 512].rearrange("(c p) n -> p c n", p=128)


def project(k, s1, pr):
    nc, a, ps = k.nc, k.a, k.ps
    N = 4 * T
    with ExitStack() as c:
        hi = [k.sb(c, f"p_hi{u}", [128, DC, 512], F32R) for u in range(2)]
        lo = [k.sb(c, f"p_lo{u}", [128, DC, 512], F32R) for u in range(2)]
        xn = [k.sb(c, f"p_xn{u}", [T, D]) for u in range(2)]
        xf = k.sb(c, "p_xf", [128, DC, B * T])
        xh = k.sb(c, "p_xh", [128, DC, B * T], F32R)
        xl = k.sb(c, "p_xl", [128, DC, B * T], F32R)
        sth = [k.sb(c, f"p_sth{u}", [128, 4, 4, T], F32R) for u in range(2)]
        stl = [k.sb(c, f"p_stl{u}", [128, 4, 4, T], F32R) for u in range(2)]
        vst = [k.sb(c, f"p_vst{u}", [T, 512]) for u in range(2)]
        scale = (HD1 ** -0.5, 1.0)
        st = k.sb(c, "p_st", [T, B, 6])
        mv = k.sb(c, "p_mv", [T, B, 2])
        rs = k.sb(c, "p_rs", [T, 2, B])

        va, ri, own_v = k.sem("p_variance"), k.sem("p_rstd"), k.sem("p_dve_own")
        raw_r = k.sem("p_raw_ready")
        xn_r, t_done = k.sem("p_xn_ready"), k.sem("p_transposed")
        xf_r, xh_r, xl_r = k.sem("p_xf"), k.sem("p_xh"), k.sem("p_xl")
        w_in, o_in = [k.sem(f"p_w_in{n}") for n in range(4)], k.sem("p_o_in")
        hi_done, lo_done = k.sem("p_hi_done"), k.sem("p_lo_done")
        pj, st_hi, st_lo = k.sem("p_projected"), k.sem("p_staged_hi"), k.sem("p_staged_lo")
        st_out, st_free = k.sem("p_stored"), k.sem("p_stage_free")
        v_st, v_out = [k.sem(f"p_v_staged{u}") for u in range(2)], [k.sem(f"p_v_stored{u}") for u in range(2)]

        def out_of(t, pair, g, i, half):
            return t[pair, 4 * half:4 * half + 4, :, 4 * i:4 * i + 4, :].rearrange("b p m t -> p b (m t)")

        with nc.Block() as block:
            @block.sync
            def _(sp):
                sp.sem_inc(st_free, 2)
                sp.sem_inc(raw_r, 1)
                for n in range(4, 8):
                    sp.wait_ge(lo_done, n - 3)
                    sp.dma_start(pr.raw[:, n - 4], pr.chunk(a, n)).then_inc(w_in[n - 4], 16)
                    if n == 4:
                        sp.wait_ge(w_in[0], 16)
                        sp.sem_inc(raw_r, 1)
                sp.dma_start(s1.wo[:], a["Wo"].rearrange("(c p) n -> p c n", p=128)).then_inc(o_in, 16)
                sp.dma_start(s1.bo[:], a["bo"].partition_broadcast(T)).then_inc(o_in, 16)
                sp.wait_ge(o_in, 32)

            @block.gpsimd
            def _(pool):
                root(k, pool, rs[:, 0, :], va, ri, 1)
                root(k, pool, rs[:, 1, :], va, ri, 2)
                for t, n in ((s1.q, 0), (s1.kk, 1)):
                    for i in range(2):
                        for half in range(2):
                            g = 4 * n + 2 * i + half
                            pool.wait_ge(st_lo, 4 * g + 4 + 4)
                            for pair, tile in ((0, sth), (1, stl)):
                                pool.dma_start(out_of(t, pair, g, i, half),
                                               tile[half][:].bitcast(F32).rearrange("p b m t -> p b (m t)"))\
                                    .then_inc(st_out, 16)
                            pool.wait_ge(st_out, 32 * (g + 1))
                            pool.sem_inc(st_free, 1)
                for n in range(2):
                    for b in range(B):
                        u = b % 2
                        pool.wait_ge(v_st[u], 4 * n + b // 2 + 1)
                        pool.dma_start(s1.v[b][:, 512 * n:512 * n + 512], vst[u][:]).then_inc(v_out[u], 16)
                for u in range(2):
                    pool.wait_ge(v_out[u], 16 * B)

            @block.tensor
            def _(pe):
                pe.sem_inc(pj, 8)
                for b in range(B):
                    pe.wait_ge(xn_r, b + 1)
                    if b >= 4:
                        pe.wait_ge(xf_r, b - 3)
                    for cc in range(DC):
                        mm = nc.tensor.transpose(ps[:, 4 + b % 4, T * cc:T * cc + T],
                                                 xn[b % 2][:, 128 * cc:128 * cc + 128], k.ident[0:T, 0:T])
                    mm.then_inc(t_done, 1)
                pe.wait_ge(xl_r, B)
                for t in range(2):
                    for i in range(2):
                        pe.wait_ge(lo_done, 2 * t + i + 1)
                        for half in range(2):
                            for m in range(4):
                                job = 8 * i + 4 * half + m
                                pe.wait_ge(st_lo, 16 * t + job + 1)
                                terms = [(w, x, cc) for cc in range(DC)
                                         for w, x in ((hi[i], xh), (hi[i], xl), (lo[i], xh))]
                                for n, (w, x, cc) in enumerate(terms):
                                    mm = nc.tensor.matmul(ps[:, m, 0:N], w[:, cc, 128 * m:128 * m + 128],
                                                          x[:, cc, N * half:N * half + N],
                                                          start=n == 0, stop=n == len(terms) - 1)
                                mm.then_inc(pj, 1)
                for n in range(2):
                    pe.wait_ge(lo_done, 4 + n + 1)
                    for b in range(B):
                        if n == 0 and b < 4:
                            pe.wait_ge(st_lo, 4 + 32 - 3 + b)
                        else:
                            pe.wait_ge(v_st[b % 2], 4 * n + b // 2 - 1)
                        terms = [(x, w, cc) for cc in range(DC)
                                 for x, w in ((xh, hi[n]), (xh, lo[n]), (xl, hi[n]))]
                        for q, (x, w, cc) in enumerate(terms):
                            mm = nc.tensor.matmul(ps[0:T, b % 4, :], x[:, cc, T * b:T * b + T], w[:, cc, :],
                                                  start=q == 0, stop=q == len(terms) - 1)
                        mm.then_inc(pj, 1)

            def staged_v(eng, copy, u):
                def run(n):
                    for b in range(u, B, 2):
                        eng.wait_ge(pj, 8 + 32 + 8 * n + b + 1)
                        if 4 * n + b // 2 >= 1:
                            eng.wait_ge(v_out[u], 16 * (4 * n + b // 2))
                        copy(vst[u][:], ps[0:T, b % 4, :]).then_inc(v_st[u], 1)
                return run

            @block.vector
            def _(dve):
                own = Steps(dve, own_v)
                dve.sem_inc(st_lo, 4)
                for b in range(B):
                    own.note(nc.vector.bn_stats(st[:, b, :], k.x[:, b, :]))
                own.settle()
                for b in range(B):
                    own.note(nc.vector.bn_aggr(mv[:, b, :], st[:, b, :]))
                own.settle()
                nc.vector.tensor_scalar(rs[:, 0, :], mv[:, :, 1], EPS, None, ALU.add).then_inc(va, 1)
                dve.wait_ge(ri, 1)
                own.link(nc.vector.tensor_tensor(rs[:, 1, :], rs[:, 0, :], rs[:, 0, :], ALU.mult))
                own.link(nc.vector.tensor_tensor(rs[:, 1, :], rs[:, 1, :], mv[:, :, 1], ALU.mult))
                nc.vector.tensor_scalar(rs[:, 1, :], rs[:, 1, :], EPS, None, ALU.add).then_inc(va, 1)
                dve.wait_ge(ri, 2)
                own.link(nc.vector.tensor_tensor(rs[:, 0, :], rs[:, 0, :], rs[:, 1, :], ALU.mult))

                def low(n):
                    dst = lo[n % 2][:] if n < 6 else s1.wm[1][:, :, 512 * (n - 6):512 * (n - 5)]
                    top = hi[n % 2][:] if n < 6 else s1.wm[0][:, :, 512 * (n - 6):512 * (n - 5)]
                    return dst, top

                def low_of(slot, n, dst, top):
                    dve.wait_ge(hi_done, n + 1)
                    nc.vector.tensor_tensor(dst, pr.raw[:, slot],
                                            top.bitcast(F32), ALU.subtract).then_inc(lo_done, 1)

                for b in range(B):
                    if b >= 2:
                        dve.wait_ge(t_done, b - 1)
                    nc.vector.tensor_scalar(xn[b % 2][:], k.x[:, b, :], mv[:, b, 0:1], rs[:, 0, b:b + 1],
                                            ALU.subtract, ALU.mult).then_inc(xn_r, 1)
                    if b >= 1:
                        q = b - 1
                        dve.wait_ge(xh_r, q + 1)
                        nc.vector.tensor_tensor(xl[:, :, T * q:T * b], xf[:, :, T * q:T * b],
                                                xh[:, :, T * q:T * b].bitcast(F32), ALU.subtract).then_inc(xl_r, 1)
                low_of(0, 0, lo[0][:], hi[0][:])
                dve.wait_ge(xh_r, B)
                nc.vector.tensor_tensor(xl[:, :, T * (B - 1):], xf[:, :, T * (B - 1):],
                                        xh[:, :, T * (B - 1):].bitcast(F32), ALU.subtract).then_inc(xl_r, 1)
                for t in range(2):
                    for i in range(2):
                        for half in range(2):
                            for m in range(4):
                                job = 8 * i + 4 * half + m
                                dve.wait_ge(st_hi, 16 * t + job + 1)
                                nc.vector.scalar_tensor_tensor(
                                    out=stl[half][:, :, m, :], in0=ps[:, m, 0:N].rearrange("p (b t) -> p b t", t=T),
                                    scalar=scale[t], in1=sth[half][:, :, m, :].bitcast(F32),
                                    op0=ALU.mult, op1=ALU.subtract).then_inc(st_lo, 1)
                            if half == 0:
                                if i == 0:
                                    low_of(2 * t + 1, 2 * t + 1, lo[1][:], hi[1][:])
                                else:
                                    low_of(2 - 2 * t, 2 * t + 2, lo[0][:], hi[0][:])
                run = staged_v(dve, nc.vector.tensor_copy, 1)
                low_of(1, 5, lo[1][:], hi[1][:])
                run(0)
                low_of(2, 6, *low(6))
                run(1)
                low_of(3, 7, *low(7))

            @block.scalar
            def _(act):
                for b in range(B):
                    act.wait_ge(t_done, b + 1)
                    for cc in range(DC):
                        ins = nc.scalar.activation(xf[:, cc, T * b:T * b + T], ps[:, 4 + b % 4, T * cc:T * cc + T],
                                                   ACT.Identity, bias=pr.bet[:, cc:cc + 1], scale=pr.gam[:, cc:cc + 1])
                    ins.then_inc(xf_r, 1)
                    act.wait_ge(xf_r, b + 1)
                    nc.scalar.copy(xh[:, :, T * b:T * b + T], xf[:, :, T * b:T * b + T]).then_inc(xh_r, 1)
                    if b == 0:
                        nc.scalar.copy(hi[0][:], pr.raw[:, 0]).then_inc(hi_done, 1)

                def high(slot, n, dst):
                    nc.scalar.copy(dst, pr.raw[:, slot])\
                        .then_inc(hi_done, 1)

                for t in range(2):
                    for i in range(2):
                        for half in range(2):
                            act.wait_ge(st_free, 4 * t + 2 * i + half + 1)
                            for m in range(4):
                                job = 8 * i + 4 * half + m
                                act.wait_ge(pj, 16 * t + job + 8 + 1)
                                nc.scalar.activation(sth[half][:, :, m, :], ps[:, m, 0:N].rearrange("p (b t) -> p b t", t=T),
                                                     ACT.Identity, scale=scale[t]).then_inc(st_hi, 1)
                            if half == 0:
                                if i == 0:
                                    act.wait_ge(pj, 16 * t + 8)
                                    high(2 * t + 1, 2 * t + 1, hi[1][:])
                                else:
                                    act.wait_ge(pj, 16 * t + 16)
                                    act.wait_ge(raw_r, t + 1)
                                    high(2 - 2 * t, 2 * t + 2, hi[0][:])
                run = staged_v(act, nc.scalar.copy, 0)
                act.wait_ge(w_in[1], 16)
                act.wait_ge(pj, 8 + 32)
                high(1, 5, hi[1][:])
                run(0)
                act.wait_ge(w_in[2], 16)
                high(2, 6, s1.wm[0][:, :, 0:512])
                run(1)
                act.wait_ge(w_in[3], 16)
                high(3, 7, s1.wm[0][:, :, 512:1024])


def attend(k, s1):
    nc, a, ps = k.nc, k.a, k.ps
    NB = len(MB)
    WIDE = [(0, 512), (512, KEYS - 512)]
    with ExitStack() as c:
        craw = [k.sb(c, f"a1_craw{u}", [128, S]) for u in range(2)]
        ch = k.sb(c, "a1_ch", [128, DC, S], F32R)
        cl = k.sb(c, "a1_cl", [128, DC, S], F32R)
        qD = [k.sb(c, f"a1_qD{n}", [128, H1, T], F32R) for n in range(2)]
        kT = [k.sb(c, f"a1_kT{n}", [128, IC, KEYS], F32R) for n in range(2)]
        v = k.sb(c, "a1_v", [128, len(KB1), INNER])
        P = [k.sb(c, f"a1_P{u}", [T, KEYS]) for u in range(2)]
        PT = [k.sb(c, f"a1_PT{u}", [128, len(KB1), T]) for u in range(2)]
        yT = k.sb(c, "a1_yT", [128, IC, T])
        nmax = k.sb(c, "a1_nmax", [T, H1])
        sums = k.sb(c, "a1_sums", [T, H1])
        rinv = k.sb(c, "a1_rinv", [T, H1])

        made = k.sem("a1_const")
        craw_in = [k.sem(f"a1_craw_in{u}") for u in range(2)]
        ch_done, cl_done = k.sem("a1_ch_done"), k.sem("a1_cl_done")
        q_in, k_in, v_in = k.sem("a1_q_in"), k.sem("a1_k_in"), k.sem("a1_v_in")
        val, val_v, val_a = k.sem("a1_values"), k.sem("a1_values_dve"), k.sem("a1_values_act")
        tk, th, tl = k.sem("a1_keys_turned"), k.sem("a1_keys_hi"), k.sem("a1_keys_lo")
        sc, nm, ex = k.sem("a1_scores"), k.sem("a1_max"), k.sem("a1_exp")
        pn, pt = k.sem("a1_prob"), k.sem("a1_prob_turned")
        pt_v, pt_a = k.sem("a1_probT_dve"), k.sem("a1_probT_act")
        yd, ys = k.sem("a1_y"), k.sem("a1_yT_ready")
        od, os_ = k.sem("a1_o"), k.sem("a1_added")
        own_v = k.sem("a1_dve_own")
        NV = 2 * NB

        later = {0: [NB, NB + 1], 1: [NB + 2, NB + 3], 2: [NB + 4, NB + 5]}

        def two_banks(n):
            return ps[:, n:n + 2, :].rearrange("p a n -> p (a n)")

        def over_batches(eng, batch):
            with eng.Fori(0, B - 1) as b:
                batch(b, False)
            batch(B - 1, True)

        def value_bank(n):
            return n % 4 if n < NB else 6

        with nc.Block() as block:
            @block.sync
            def _(sp):
                sp.wait_ge(made, 2)
                def context(b):
                    for cc in range(DC):
                        sp.wait_ge(cl_done, DC * b + cc + 1)
                        src = a["ctxT"][bass.ds(b, 1)].rearrange("b (c p) s -> p (b c) s", p=128)
                        sp.dma_start(craw[cc % 2][:], src[:, cc, :]).then_inc(craw_in[cc % 2], 16)

                def batch(b, last):
                    sp.wait_ge(sc, H1 * (b + 1))
                    for n in range(2):
                        for two in range(2):
                            r = slice(64 * two, 64 * two + 64)
                            sp.dma_start(qD[n][r].bitcast(F32).rearrange("p (m two) t -> p m two t", two=2)[:, :, two, :],
                                         s1.q[n][bass.ds(b, 1), r].rearrange("b p m t -> p (b m) t")).then_inc(q_in, 16)
                        sp.dma_start(kT[n][:, :, 0:T].bitcast(F32),
                                     s1.kk[n][bass.ds(b, 1)].rearrange("b p m t -> p (b m) t")).then_inc(k_in, 16)
                    sp.wait_ge(yd, IC * (b + 1))
                    sp.dma_start(v[0:T, 0, :], s1.v[bass.ds(b, 1)].rearrange("b t n -> t (b n)")).then_inc(v_in, 16)
                    if not last:
                        context(b + 1)

                context(0)
                over_batches(sp, batch)

            @block.gpsimd
            def _(pool):
                for n in range(2):
                    pool.memset(qD[n][:].bitcast(U32), 0).then_inc(made, 1)

            @block.tensor
            def _(pe):
                pe.sem_inc(val, NV)
                pe.sem_inc(sc, H1)
                pe.sem_inc(yd, IC)
                pe.sem_inc(od, 1)
                pe.sem_inc(pt, 2)
                pe.sem_inc(tk, IC)
                def batch(b, last):
                    def values(n):
                        nb, g = n % NB, n // NB
                        first, size = MB[nb][0] - T, MB[nb][1]
                        if n == 0:
                            pe.wait_ge(cl_done, DC * b + DC + 2)
                            pe.wait_ge(ex, H1 * b + 2)
                        if n >= NB:
                            pe.wait_ge(val_v if (n - 1) % 2 else val_a, NB * b + (n - 1) // 2 + 1)
                        elif n >= 4:
                            pe.wait_ge(val_v if n % 2 else val_a, NB * b + (n - 4) // 2 + 1)
                        if n == NB:
                            pe.wait_ge(os_, b + 1)
                        terms = [(x, w, cc) for cc in range(DC)
                                 for x, w in ((ch, s1.wm[0]), (ch, s1.wm[1]), (cl, s1.wm[0]))]
                        for t, (x, w, cc) in enumerate(terms):
                            mm = nc.tensor.matmul(ps[0:size, value_bank(n), :], x[:, cc, first:first + size],
                                                  w[:, cc, 512 * g:512 * g + 512],
                                                  start=t == 0, stop=t == len(terms) - 1)
                        mm.then_inc(val, 1)

                    def keys(m):
                        pe.wait_ge(pt_v, H1 * b + max(2 * m - 4, 0) + 1)
                        pe.wait_ge(pt_a, H1 * b + max(2 * m - 4, 0) + 1)
                        pe.wait_ge(tl, IC * b + m + 1)
                        if m % 4 == 0:
                            last = NB * (m // 4 + 1) - 1
                            pe.wait_ge(val_v, NB * b + (last + 1) // 2)
                            pe.wait_ge(val_a, NB * b + (last + 1) // 2)
                        for nb, (first, size) in enumerate(MB):
                            o = 128 * nb
                            mm = nc.tensor.transpose(ps[:, 4 + o // 512, o % 512:o % 512 + size],
                                                     v[0:size, 1 + nb, 128 * m:128 * m + 128], k.ident[0:size, 0:size])
                        mm.then_inc(tk, 1)

                    def scores(h):
                        if h == 0:
                            pe.wait_ge(q_in, b * 64 + 64)
                            pe.wait_ge(k_in, b * 32 + 32)
                            pe.wait_ge(val_v, NB * b + NB // 2)
                            pe.wait_ge(val_a, NB * b + NB // 2)
                        if h % 2 == 0:
                            pe.wait_ge(tl, IC * b + h // 2 + 1 + 1)
                        pe.wait_ge(ex, H1 * b + h + 1)
                        s = 2 * (h % 2)
                        m = h // 2
                        for f, (first, wide) in enumerate(WIDE):
                            for t, (q, kk) in enumerate(((0, 0), (0, 1), (1, 0))):
                                mm = nc.tensor.matmul(ps[0:T, s + f, 0:wide], qD[q][:, h, :],
                                                      kT[kk][:, m, first:first + wide], start=t == 0, stop=t == 2)
                        mm.then_inc(sc, 1)

                    def turn(h):
                        pe.wait_ge(pn, H1 * b + h + 1)
                        pe.wait_ge(pt_v, H1 * b + h + 1)
                        pe.wait_ge(pt_a, H1 * b + h + 1)
                        pe.wait_ge(tl, IC * b + min(h // 2 + 2, IC - 1) + 1 + 1)
                        for n, (first, size) in enumerate(KB1):
                            mm = nc.tensor.transpose(ps[0:size, 4 + n // 5, T * (n % 5):T * (n % 5) + T],
                                                     P[h % 2][:, first:first + size], k.ident[0:T, 0:T])
                        mm.then_inc(pt, 1)

                    def attended(m):
                        if m == 0:
                            pe.wait_ge(v_in, b * 16 + 16)
                        pe.wait_ge(pt_v, H1 * b + 2 * m + 2 + 1)
                        pe.wait_ge(pt_a, H1 * b + 2 * m + 2 + 1)
                        pe.wait_ge(ys, IC * b + m + 1)
                        for n, (first, size) in enumerate(KB1):
                            for u in range(2):
                                h = 2 * m + u
                                mm = nc.tensor.matmul(ps[64 * u:64 * u + 64, 7, 128 * (m % 2):128 * (m % 2) + T],
                                                      v[0:size, n, HD1 * h:HD1 * h + HD1], PT[u][0:size, n, :],
                                                      start=n == 0, stop=n == len(KB1) - 1)
                        mm.then_inc(yd, 1)

                    for n in range(NB):
                        values(n)
                    keys(0)
                    for m in range(IC + 2):
                        if m < IC:
                            scores(2 * m)
                        if m + 1 < IC:
                            keys(m + 1)
                        if m >= 2:
                            attended(m - 2)
                        if 1 <= m <= IC:
                            turn(2 * m - 2)
                        if m < IC:
                            scores(2 * m + 1)
                        if 1 <= m <= IC:
                            turn(2 * m - 1)
                        for n in later.get(m, []):
                            values(n)
                    pe.wait_ge(ys, IC * b + IC + 2)
                    pe.wait_ge(val_v, NB * b + NB)
                    for m in range(IC):
                        mm = nc.tensor.matmul(ps[0:T, 6, :], yT[:, m, :], s1.wo[:, m, :], start=m == 0, stop=m == IC - 1)
                    mm.then_inc(od, 1)

                over_batches(pe, batch)

            def copy_values(eng, copy, done, b, n):
                nb, g = n % NB, n // NB
                size = MB[nb][1]
                eng.wait_ge(val, NV * b + n + 1 + NV)
                copy(v[0:size, 1 + nb, 512 * g:512 * g + 512], ps[0:size, value_bank(n), :]).then_inc(done, 1)

            @block.vector
            def _(dve):
                for s, n in ((os_, 1), (cl_done, 2), (tl, 1), (pt_v, 1)):
                    dve.sem_inc(s, n)
                OWN = 1 + H1

                def context(b, cc):
                    dve.wait_ge(ch_done, DC * b + cc + 1)
                    nc.vector.tensor_tensor(cl[:, cc, :], craw[cc % 2][:], ch[:, cc, :].bitcast(F32), ALU.subtract)\
                        .then_inc(cl_done, 1)

                def batch(b, last):
                    own = Steps(dve, own_v, OWN * b)
                    xb = at(k.x, b)

                    def values(n):
                        if n == 1:
                            dve.wait_ge(yd, IC * b + IC)
                        if n % 2 == 1:
                            copy_values(dve, nc.vector.tensor_copy, val_v, b, n)

                    def keys(m):
                        dve.wait_ge(th, IC * b + m + 1)
                        nc.vector.tensor_tensor(kT[1][:, m, T:KEYS], two_banks(4)[:, 0:S],
                                                kT[0][:, m, T:KEYS].bitcast(F32), ALU.subtract).then_inc(tl, 1)

                    def highest(h):
                        s = 2 * (h % 2)
                        dve.wait_ge(sc, H1 * b + H1 + h + 1)
                        nc.vector.tensor_reduce(nmax[:, h:h + 1], two_banks(s)[0:T, 0:KEYS], AX, ALU.max, negate=True)\
                            .then_inc(nm, 1)

                    def normalise(h):
                        dve.wait_ge(ex, H1 * b + h + 1 + 2)
                        own.link(nc.vector.reciprocal(rinv[:, h:h + 1], sums[:, h:h + 1]))
                        nc.vector.tensor_scalar(P[h % 2][:], P[h % 2][:], rinv[:, h:h + 1], None, ALU.mult)\
                            .then_inc(pn, 1)

                    def turned(h):
                        dve.wait_ge(pt, H1 * b + h + 1 + 2)
                        dve.wait_ge(yd, IC * b + h // 2 + IC)
                        nc.vector.tensor_copy(PT[h % 2][:, 5:7, :].rearrange("p n t -> p (n t)"), ps[:, 5, 0:2 * T])\
                            .then_inc(pt_v, 1)

                    for n in range(NB):
                        values(n)
                    keys(0)
                    for m in range(IC + 2):
                        if m < IC:
                            highest(2 * m)
                        if m + 1 < IC:
                            keys(m + 1)
                        if 1 <= m <= IC:
                            normalise(2 * m - 1)
                            turned(2 * m - 2)
                        if m < IC:
                            highest(2 * m + 1)
                            normalise(2 * m)
                        if 1 <= m <= IC:
                            turned(2 * m - 1)
                        for n in later.get(m, []):
                            values(n)
                        if not last and 0 <= m - 4 < DC:
                            context(b + 1, m - 4)
                    dve.wait_ge(od, b + 2)
                    own.link(nc.vector.tensor_tensor(xb, xb, ps[0:T, 6, :], ALU.add))
                    nc.vector.tensor_tensor(xb, xb, s1.bo[:], ALU.add).then_inc(os_, 1)
                    assert own.n == OWN, own.n

                for cc in range(DC):
                    context(0, cc)
                over_batches(dve, batch)

            @block.scalar
            def _(act):
                for s, n in ((ex, 2), (ys, 2), (pt_a, 1)):
                    act.sem_inc(s, n)

                def context(b, cc):
                    act.wait_ge(craw_in[cc % 2], b * 32 + 16 * (cc // 2) + 16)
                    act.wait_ge(val, NV * b + NV)
                    nc.scalar.copy(ch[:, cc, :], craw[cc % 2][:]).then_inc(ch_done, 1)

                def batch(b, last):
                    def values(n):
                        if n == 0:
                            act.wait_ge(yd, IC * b + IC)
                        if n % 2 == 0:
                            copy_values(act, nc.scalar.copy, val_a, b, n)

                    def keys(m):
                        act.wait_ge(tk, IC * b + IC + m + 1)
                        act.wait_ge(sc, H1 * b + H1)
                        nc.scalar.copy(kT[0][:, m, T:KEYS], two_banks(4)[:, 0:S])\
                            .then_inc(th, 1)

                    def exponent(h):
                        s = 2 * (h % 2)
                        act.wait_ge(nm, H1 * b + h + 1)
                        act.wait_ge(pt, H1 * b + h + 1)
                        nc.scalar.activation(P[h % 2][:], two_banks(s)[0:T, 0:KEYS], ACT.Exp, bias=nmax[:, h:h + 1],
                                             accum_out=sums[:, h:h + 1]).then_inc(ex, 1)

                    def turned(h):
                        act.wait_ge(pt, H1 * b + h + 1 + 2)
                        act.wait_ge(yd, IC * b + h // 2 + IC)
                        nc.scalar.copy(PT[h % 2][:, 0:5, :].rearrange("p n t -> p (n t)"), ps[:, 4, 0:5 * T])\
                            .then_inc(pt_a, 1)

                    def attended(m):
                        act.wait_ge(yd, IC * b + m + 1 + IC)
                        if m == 0:
                            act.wait_ge(od, b + 1)
                        nc.scalar.copy(yT[:, m, :], ps[:, 7, 128 * (m % 2):128 * (m % 2) + T]).then_inc(ys, 1)

                    for n in range(NB):
                        values(n)
                    keys(0)
                    for m in range(IC + 2):
                        if m + 1 < IC:
                            keys(m + 1)
                        if m >= 2:
                            attended(m - 2)
                        if 1 <= m <= IC:
                            turned(2 * m - 2)
                        if m < IC:
                            exponent(2 * m)
                        if 1 <= m <= IC:
                            turned(2 * m - 1)
                        if m < IC:
                            exponent(2 * m + 1)
                        for n in later.get(m, []):
                            values(n)
                        if not last and 0 <= m - 4 < DC:
                            context(b + 1, m - 4)

                for cc in range(DC):
                    context(0, cc)
                over_batches(act, batch)


def build(nc, a):
    with ExitStack() as ctx:
        k = Core(nc, ctx, a)
        for stage, args in ((attention_0, ()), (route, (0,)), (experts, (0,))):
            stage(k, *args)
            k.end_stage()
        with ExitStack() as shared:
            s1 = Attention1(k, shared)
            with ExitStack() as ahead:
                pr = Projection(k, ahead)
                combine(k, 0, pr)
                k.end_stage()
                project(k, s1, pr)
                k.end_stage()
            attend(k, s1)
            k.end_stage()
        for stage, args in ((route, (1,)), (experts, (1,)), (combine, (1,))):
            stage(k, *args)
            k.end_stage()


def lay_out(i):
    g = {n: np.asarray(v) for n, v in i.items()}

    def chunks_in(w, fg):
        return w.reshape(E, fg, 512, DC, 128).transpose(0, 1, 4, 3, 2).reshape(E * fg, 128, DC, 512)

    def chunks_out(w, fg):
        return w.reshape(E, D, fg, 4, 128).transpose(0, 2, 4, 3, 1).reshape(E * fg, 128, 4, D)

    def column(b):
        return b.reshape(-1, 128).T

    p0, p1, q0, q1 = "L0_xattn_", "L1_xattn_", "L0_ffn_", "L1_ffn_"
    return {k_: np.ascontiguousarray(v) for k_, v in {
        "x": g["x"], "ctxT": g["ctx_1024"].transpose(0, 2, 1),
        "q_w": g[p0 + "q_w"], "k_w": g[p0 + "k_w"], "v_w": g[p0 + "v_w"], "o_w": g[p0 + "o_w"],
        "q_b": column(g[p0 + "q_b"]), "k_b": column(g[p0 + "k_b"]), "v_b": g[p0 + "v_b"], "o_b": g[p0 + "o_b"],
        "gam0": column(g[q0 + "gamma"]), "bet0": column(g[q0 + "beta"]),
        "Wg0": g[q0 + "Wg"].T, "bg0": g[q0 + "bg"],
        "w1": chunks_in(g[q0 + "W1"], 4), "b1": g[q0 + "b1"].reshape(E * 16, 128).T,
        "wout0": chunks_out(g[q0 + "W2"], 4), "b2": g[q0 + "b2"],
        "ln_g": column(g[p1 + "ln_g"]), "ln_b": column(g[p1 + "ln_b"]),
        "Wq": g[p1 + "Wq"], "Wkv": g[p1 + "Wkv"], "Wm": g[p1 + "Wm"], "Wo": g[p1 + "Wo"], "bo": g[p1 + "bo"],
        "Wg1": g[q1 + "w_router"].T, "wgate": chunks_in(g[q1 + "w_gate"], 2), "wup": chunks_in(g[q1 + "w_up"], 2),
        "wout1": chunks_out(g[q1 + "w_down"], 2), "gam1": g[q1 + "ln_gamma"], "bet1": g[q1 + "ln_beta"],
    }.items()}


def kernel(**inputs):
    import concourse.bacc as bacc
    from concourse.bass_utils import run_bass_kernel_spmd

    nc = bacc.Bacc("TRN2", target_bir_lowering=False, num_devices=1)
    arrays = lay_out(inputs)
    a = {n: nc.dram_tensor(n, v.shape, F32, kind="ExternalInput").ap() for n, v in arrays.items()}
    a["out"] = nc.dram_tensor("out", (B, T, D), F32, kind="ExternalOutput").ap()
    build(nc, a)
    r = run_bass_kernel_spmd(nc, [arrays], core_ids=[0])
    return r.results[0]["out"]
```

```python
from contextlib import ExitStack

import numpy as np
import concourse.bass as bass
from concourse import mybir

F32 = mybir.dt.float32
F32R = mybir.dt.float32r
I32 = mybir.dt.int32
U32 = mybir.dt.uint32
ALU = mybir.AluOpType
ACT = mybir.ActivationFunctionType
AX = mybir.AxisListType.X

B, T, D, S = 8, 100, 512, 722
DC = D // 128
E = 8
CAP = 256
PASSES = (2 * B * T + E * (CAP - 1)) // CAP
LEAST = -(-2 * B * T // CAP)
H0, HD0 = 16, 32
H1, HD1 = 16, 64
INNER = H1 * HD1
IC = INNER // 128
KEYS = T + S
MB = [(T + 128 * i, min(128, KEYS - T - 128 * i)) for i in range(-(-S // 128))]
KB1 = [(0, T)] + MB
EPS = 1e-5
NEG = -1.0e30


class Steps:

    def __init__(self, eng, sem, first=0):
        self.eng, self.sem, self.first, self.n = eng, sem, first, 0

    def note(self, ins):
        self.n += 1
        return ins.then_inc(self.sem, 1)

    def settle(self):
        self.eng.wait_ge(self.sem, self.first + self.n)

    def link(self, ins):
        self.note(ins)
        self.settle()


class Core:

    def __init__(self, nc, ctx, a):
        self.nc, self.ctx, self.a, self.sems = nc, ctx, a, []
        self.ps = ctx.enter_context(nc.psum_tensor("banks", [128, 8, 512], F32))
        self.x = self.sb(ctx, "x_res", [T, B, D])
        self.ident = self.sb(ctx, "ident", [128, 128])
        self.nhalf = self.sb(ctx, "nhalf", [T, B])
        self.st = self.sb(ctx, "stats", [T, B, 6])
        self.oh = [self.sb(ctx, f"onehot{k}", [T, B, E]) for k in range(2)]
        self.wt = self.sb(ctx, "wt", [T, 2, B])
        self.slot = self.sb(ctx, "slot", [T, 2, B], U32)
        self.table = self.sb(ctx, "table", [1, 16], I32)
        self.rows = nc.dram_tensor("slot_rows", ((PASSES + 1) * CAP, D), F32, kind="Internal").ap()
        self.outs = nc.dram_tensor("slot_outs", (PASSES * CAP, D), F32, kind="Internal").ap()

    def sb(self, ctx, name, shape, dt=F32):
        return ctx.enter_context(self.nc.sbuf_tensor(name, shape, dt))

    def sem(self, name):
        self.sems.append(self.nc.alloc_semaphore(name=name))
        return self.sems[-1]

    def end_stage(self):
        self.nc.clear_and_free_semaphores(self.sems)
        self.nc.all_engine_barrier()
        self.sems = []


def after(eng, sem, n):
    if type(n) is not int or n > 0:
        eng.wait_ge(sem, n)


def bc(ap, n):
    return ap.unsqueeze(len(ap.shape)).broadcast_to(list(ap.shape) + [n])


def aggregate(k, own, st, mv, rs, var_ready, some=range(B)):
    nc = k.nc
    for b in some:
        own.note(nc.vector.bn_aggr(mv[:, b, :], st[:, b, :]))
    own.settle()
    part = slice(some[0], some[-1] + 1)
    nc.vector.tensor_scalar(rs[:, part], mv[:, part, 1], EPS, None, ALU.add).then_inc(var_ready, 1)


def root(k, pool, rs, var_ready, rstd_ready, turn):
    pool.wait_ge(var_ready, turn)
    pool.tensor_tensor(rs, rs, k.nhalf[:, 0:rs.shape[1]], ALU.pow).then_inc(rstd_ready, 1)


def both_norms(k, mv, rs):
    return k.nc.vector.tensor_scalar(rs, mv[:, :, 1], 1.0 + EPS, EPS * EPS, ALU.mult, ALU.add)


def at(tile, b):
    return tile[:, bass.ds(b, 1), :].rearrange("p b d -> p (b d)")


def attention_0(k):
    nc, a, ps = k.nc, k.a, k.ps
    with ExitStack() as c:
        w = {n: k.sb(c, f"a0_{n}", [128, DC, D]) for n in "qkvo"}
        qb = k.sb(c, "a0_qb", [128, DC])
        kb = k.sb(c, "a0_kb", [128, DC])
        vb = k.sb(c, "a0_vb", [T, D])
        ob = k.sb(c, "a0_ob", [T, D])
        mask = k.sb(c, "a0_mask", [T, T])
        wv, wo = ([k.sb(c, f"a0_{n}_{part}", [128, DC, D], F32R) for part in ("hi", "lo")] for n in ("wv", "wo"))
        ctxT = [k.sb(c, f"a0_ctx{u}", [128, DC, T]) for u in range(2)]
        ctxS = [[k.sb(c, f"a0_ctx{part}{u}", [128, DC, T], F32R) for part in ("hi", "lo")] for u in range(2)]
        xn = [k.sb(c, f"a0_xn{u}", [T, D]) for u in range(2)]
        xT = [k.sb(c, f"a0_xT{u}", [128, DC, T]) for u in range(2)]
        qT = [k.sb(c, f"a0_qT{u}", [128, DC, T]) for u in range(2)]
        kD = [k.sb(c, f"a0_kD{u}", [128, DC, 4, T]) for u in range(2)]
        v = [k.sb(c, f"a0_v{u}", [T, D]) for u in range(2)]
        P = [k.sb(c, f"a0_P{u}", [T, H0, T]) for u in range(2)]
        PT = [k.sb(c, f"a0_PT{u}", [T, H0, T]) for u in range(2)]
        yT = [[k.sb(c, f"a0_y{part}{u}", [128, DC, T], F32R) for part in ("hi", "lo")] for u in range(2)]
        st = k.sb(c, "a0_st", [T, B, 6])
        mv = k.sb(c, "a0_mv", [T, B, 2])
        rs = k.sb(c, "a0_rs", [T, B])
        own_s, va, ri = k.sem("a0_stats_own"), k.sem("a0_variance"), k.sem("a0_rstd")
        nmax = [k.sb(c, f"a0_nm{u}", [T, H0]) for u in range(2)]
        sums = [k.sb(c, f"a0_sum{u}", [T, H0]) for u in range(2)]
        rinv = k.sb(c, "a0_rinv", [T, H0])
        zero = k.sb(c, "a0_zero", [128, CAP * D // 128])

        FIRST = 2
        x_in = [k.sem(f"a0_x_in{n}") for n in range(2)]
        w_in = {n: k.sem(f"a0_w_in_{n}") for n in "qkvo"}
        b_in = [k.sem(f"a0_b_in{n}") for n in range(2)]
        kd_zero = k.sem("a0_kD_zero")
        wh_done, wl_done = k.sem("a0_w_hi_done"), k.sem("a0_w_lo_done")
        ctx_in = [k.sem(f"a0_ctx_in{u}") for u in range(2)]
        made = k.sem("a0_const")
        zmade = k.sem("a0_zero_made")
        zeroed = k.sem("a0_rows_zeroed")
        names = "xn t xT q qs kk ks ch cl v vs s nm e p y yh ys o os".split()
        m = {n: k.sem(f"a0_{n}_done") for n in names}
        pt, pts = k.sem("a0_pt_done"), k.sem("a0_pts_done")
        own_v = k.sem("a0_dve_own")
        AHEAD = 2

        def done(b):
            return b + (1 + AHEAD)

        def done_before(b):
            return b + 1

        def over_batches(loop, head, step, tail):
            head()
            with loop(0, B // 2 - 1) as i:
                step(2 * i + 1, 1, False)
                step(2 * i + 2, 0, False)
            step(B - 1, 1, True)
            tail(B - 1, 1)

        with nc.Block() as block:
            @block.sync
            def _(sp):
                for b in range(B):
                    sp.dma_start(k.x[:, b, :], a["x"][b]).then_inc(x_in[b >= FIRST], 16)

                def weights(n):
                    sp.dma_start(w[n][:], a[n + "_w"].rearrange("(c p) n -> p c n", p=128)).then_inc(w_in[n], 16)

                def load(b, u):
                    sp.wait_ge(m["v"], done_before(b))
                    src = a["ctxT"][bass.ds(b, 1)].rearrange("b (c p) s -> p (b c) s", p=128)
                    sp.dma_start(ctxT[u][:], src[:, :, 0:T]).then_inc(ctx_in[u], 16)

                sp.dma_start(qb[:], a["q_b"]).then_inc(b_in[0], 16)
                sp.dma_start(kb[:], a["k_b"]).then_inc(b_in[0], 16)
                weights("q")
                load(0, 0)
                weights("k")
                load(1, 1)
                weights("v")
                sp.dma_start(vb[:], a["v_b"].partition_broadcast(T)).then_inc(b_in[1], 16)
                weights("o")
                sp.dma_start(ob[:], a["o_b"].partition_broadcast(T)).then_inc(b_in[1], 16)
                with sp.Fori(1, B // 2) as i:
                    load(2 * i, 0)
                    load(2 * i + 1, 1)

            @block.gpsimd
            def _(pool):
                pool.memset(k.ident[:], 0.0).then_inc(made, 1)
                pool.memset(mask[:], 0.0).then_inc(made, 1)
                pool.memset(k.nhalf[:], -0.5).then_inc(made, 1)
                pool.wait_ge(made, 3)
                pool.affine_select(out=k.ident[:], in_=k.ident[:], compare_op=ALU.not_equal, fill=1.0,
                                   base=0, pattern=[[-1, 128]], channel_multiplier=1).then_inc(made, 1)
                pool.affine_select(out=mask[:], in_=mask[:], compare_op=ALU.is_ge, fill=NEG,
                                   base=0, pattern=[[-1, T]], channel_multiplier=1).then_inc(made, 1)
                root(k, pool, rs[:, 0:FIRST], va, ri, 1)
                root(k, pool, rs[:, FIRST:B], va, ri, 2)
                for u in range(2):
                    pool.memset(kD[u][:], 0.0).then_inc(kd_zero, 1)
                pool.memset(zero[:], 0.0).then_inc(zmade, 1)
                pool.wait_ge(zmade, 1)
                for t, n in ((k.rows, PASSES + 1), (k.outs, PASSES)):
                    for r in range(n):
                        pool.dma_start(t[CAP * r:CAP * (r + 1)].rearrange("(p s) d -> p (s d)", p=128),
                                       zero[:]).then_inc(zeroed, 16)
                pool.wait_ge(zeroed, 16 * (2 * PASSES + 1))

            @block.tensor
            def _(pe):
                for n in "t q kk v s y o".split():
                    pe.sem_inc(m[n], AHEAD)
                pe.wait_ge(made, 5)

                def split_product(x, w):
                    terms = [(p, q, cc) for cc in range(DC) for p, q in ((0, 0), (0, 1), (1, 0))]
                    for n, (p, q, cc) in enumerate(terms):
                        mm = nc.tensor.matmul(ps[0:T, 5, :], x[p][:, cc, :], w[q][:, cc, :],
                                              start=n == 0, stop=n == len(terms) - 1)
                    return mm

                def turn(b, u, first=False):
                    pe.wait_ge(m["xn"], done(b))
                    if not first:
                        pe.wait_ge(pts, 4 * b - 3)
                    for cc in range(DC):
                        mm = nc.tensor.transpose(ps[:, 6, T * cc:T * cc + T],
                                                 xn[u][:, 128 * cc:128 * cc + 128], k.ident[0:T, 0:T])
                    mm.then_inc(m["t"], 1)

                def projections(b, u, first=False):
                    pe.wait_ge(m["xT"], done(b))
                    if first:
                        pe.wait_ge(w_in["q"], 16)
                    else:
                        pe.wait_ge(pts, 4 * b - 2)
                    for mo in range(DC):
                        for cc in range(DC):
                            mm = nc.tensor.matmul(ps[:, 7, T * mo:T * mo + T],
                                                  w["q"][:, cc, 128 * mo:128 * mo + 128], xT[u][:, cc, :],
                                                  start=cc == 0, stop=cc == DC - 1)
                    mm.then_inc(m["q"], 1)
                    pe.wait_ge(ctx_in[u], 8 * (b - u) + 16)
                    if first:
                        pe.wait_ge(w_in["k"], 16)
                    pe.wait_ge(m["ys"], done_before(b))
                    for mo in range(DC):
                        for cc in range(DC):
                            mm = nc.tensor.matmul(ps[:, 4, T * mo:T * mo + T],
                                                  w["k"][:, cc, 128 * mo:128 * mo + 128], ctxT[u][:, cc, :],
                                                  start=cc == 0, stop=cc == DC - 1)
                    mm.then_inc(m["kk"], 1)
                    if first:
                        pe.wait_ge(wl_done, 1)
                    pe.wait_ge(m["cl"], done(b))
                    pe.wait_ge(m["os"], done_before(b))
                    split_product(ctxS[u], wv).then_inc(m["v"], 1)

                def scores(b, u, part):
                    if part == 0:
                        pe.wait_ge(m["ks"], done(b))
                        pe.wait_ge(m["nm"], b + AHEAD)
                    for g in (2 * part, 2 * part + 1):
                        mm = nc.tensor.matmul(ps[0:T, g, 0:4 * T], qT[u][:, g, :],
                                              kD[u][:, g, :, :].rearrange("p h t -> p (h t)"),
                                              start=True, stop=True)
                    if part == 1:
                        mm.then_inc(m["s"], 1)

                def turn_probabilities(b, u, last):
                    pe.wait_ge(m["p"], done(b))
                    for g in range(4):
                        if g == 0 and not last:
                            pe.wait_ge(m["xT"], done(b + 1))
                        if g == 1 and not last:
                            pe.wait_ge(m["qs"], done(b + 1))
                        if g >= 2:
                            pe.wait_ge(pts, 4 * b + g + 1)
                        for h in range(4 * g, 4 * g + 4):
                            mm = nc.tensor.transpose(ps[0:T, 6 + g % 2, T * (h % 4):T * (h % 4) + T],
                                                     P[u][:, h, :], k.ident[0:T, 0:T])
                        mm.then_inc(pt, 1)

                def attended(b, u, last):
                    pe.wait_ge(m["vs"], done(b))
                    if not last:
                        pe.wait_ge(m["ks"], done(b + 1))
                    for g in range(4):
                        pe.wait_ge(pts, 4 * b + g + 3)
                        for h in range(4 * g, 4 * g + 4):
                            mm = nc.tensor.matmul(ps[HD0 * (h % 4):HD0 * (h % 4) + HD0, 4, T * g:T * g + T],
                                                  v[u][:, HD0 * h:HD0 * h + HD0], PT[u][:, h, :],
                                                  start=True, stop=True)
                    mm.then_inc(m["y"], 1)

                def output(b, u, last):
                    pe.wait_ge(m["ys"], done(b))
                    if not last:
                        pe.wait_ge(m["vs"], done(b + 1))
                    pe.wait_ge(wl_done, 2)
                    split_product(yT[u], wo).then_inc(m["o"], 1)

                def head():
                    turn(0, 0, True)
                    projections(0, 0, True)
                    scores(0, 0, 0)
                    scores(0, 0, 1)
                    turn(1, 1)

                def step(n, u, last):
                    projections(n, u)
                    turn_probabilities(n - 1, 1 - u, False)
                    scores(n, u, 0)
                    attended(n - 1, 1 - u, False)
                    scores(n, u, 1)
                    if not last:
                        turn(n + 1, 1 - u)
                    output(n - 1, 1 - u, False)

                def tail(b, u):
                    turn_probabilities(b, u, True)
                    attended(b, u, True)
                    output(b, u, True)

                over_batches(pe.Fori, head, step, tail)

            @block.vector
            def _(dve):
                for n in "xn xT qs ks cl vs nm p ys os".split():
                    dve.sem_inc(m[n], AHEAD)
                stats_own = Steps(dve, own_s)
                for n, some in enumerate((range(FIRST), range(FIRST, B))):
                    dve.wait_ge(x_in[n], 16 * len(some))
                    for b in some:
                        stats_own.note(nc.vector.bn_stats(st[:, b, :], k.x[:, b, :]))
                    stats_own.settle()
                    aggregate(k, stats_own, st, mv, rs, va, some)
                HEAD, STEP = 2, 4

                def normalise_rows(b, u):
                    dve.wait_ge(m["t"], done_before(b))
                    nc.vector.tensor_scalar(xn[u][:], at(k.x, b), at(mv, b)[:, 0:1], rs[:, bass.ds(b, 1)],
                                            ALU.subtract, ALU.mult).then_inc(m["xn"], 1)

                def rows_turned(b, u):
                    dve.wait_ge(m["t"], done(b))
                    nc.vector.tensor_copy(xT[u][:].rearrange("p c t -> p (c t)"), ps[:, 6, 0:DC * T])\
                        .then_inc(m["xT"], 1)

                def queries(b, u):
                    dve.wait_ge(m["q"], done(b))
                    nc.vector.tensor_tensor(qT[u][:], ps[:, 7, 0:DC * T].rearrange("p (c t) -> p c t", c=DC),
                                            bc(qb[:], T), ALU.add).then_inc(m["qs"], 1)

                def keys(b, u):
                    dve.wait_ge(m["kk"], done(b))
                    for r in range(4):
                        q = slice(32 * r, 32 * r + 32)
                        ins = nc.vector.tensor_tensor(kD[u][q, :, r, :],
                                                      ps[q, 4, 0:DC * T].rearrange("p (c t) -> p c t", c=DC),
                                                      bc(kb[q, :], T), ALU.add)
                    ins.then_inc(m["ks"], 1)

                def values(b, u):
                    dve.wait_ge(m["v"], done(b))
                    nc.vector.tensor_tensor(v[u][:], ps[0:T, 5, :], vb[:], ALU.add).then_inc(m["vs"], 1)

                def weights_low(n, part, name):
                    dve.wait_ge(wh_done, n)
                    nc.vector.tensor_tensor(part[1][:], w[name][:], part[0][:].bitcast(F32), ALU.subtract)\
                        .then_inc(wl_done, 1)

                def context_low(b, u):
                    dve.wait_ge(m["ch"], done(b))
                    nc.vector.tensor_tensor(ctxS[u][1][:], ctxT[u][:], ctxS[u][0][:].bitcast(F32), ALU.subtract)\
                        .then_inc(m["cl"], 1)

                def attended_low(b, u):
                    dve.wait_ge(m["yh"], done(b))
                    nc.vector.tensor_tensor(yT[u][1][:].rearrange("p c t -> p (c t)"), ps[:, 4, 0:DC * T],
                                            yT[u][0][:].rearrange("p c t -> p (c t)").bitcast(F32), ALU.subtract)\
                        .then_inc(m["ys"], 1)

                def highest(b, u, own, last=False):
                    dve.wait_ge(m["s"], done(b))
                    sc = ps[0:T, 0:4, 0:4 * T].rearrange("p g (h t) -> p g h t", h=4)
                    mk = mask[:].unsqueeze(1).unsqueeze(1).broadcast_to([T, 4, 4, T])
                    dve.wait_ge(m["y"], done_before(b))
                    own.note(nc.vector.tensor_tensor(P[u][:].rearrange("p (g h) t -> p g h t", h=4), sc, mk,
                                                     ALU.add))
                    if not last:
                        rows_turned(b + 1, 1 - u)
                    own.settle()
                    own.link(nc.vector.tensor_reduce(nmax[u][:], P[u][:], AX, ALU.max, negate=True))
                    nc.vector.tensor_scalar(nmax[u][:], nmax[u][:], HD0 ** -0.5, None, ALU.mult)\
                        .then_inc(m["nm"], 1)

                def normalise(b, u, own):
                    dve.wait_ge(m["e"], done(b))
                    own.link(nc.vector.reciprocal(rinv[:], sums[u][:]))
                    nc.vector.tensor_tensor(P[u][:], P[u][:], bc(rinv[:], T), ALU.mult).then_inc(m["p"], 1)

                def add_output(b, own):
                    dve.wait_ge(m["o"], done(b))
                    xb = at(k.x, b)
                    own.link(nc.vector.tensor_tensor(xb, xb, ps[0:T, 5, :], ALU.add))
                    nc.vector.tensor_tensor(xb, xb, ob[:], ALU.add).then_inc(m["os"], 1)
                    dve.wait_ge(m["os"], done(b))
                    nc.vector.bn_stats(at(k.st, b), xb)

                def head():
                    own = Steps(dve, own_v)
                    dve.wait_ge(ri, 1)
                    normalise_rows(0, 0)
                    rows_turned(0, 0)
                    dve.wait_ge(b_in[0], 32)
                    queries(0, 0)
                    context_low(0, 0)
                    dve.wait_ge(kd_zero, 2)
                    weights_low(1, wv, "v")
                    keys(0, 0)
                    dve.wait_ge(b_in[1], 32)
                    values(0, 0)
                    normalise_rows(1, 1)
                    context_low(1, 1)
                    dve.wait_ge(ri, 2)
                    highest(0, 0, own)
                    weights_low(2, wo, "o")
                    assert own.n == HEAD

                def step(n, u, last):
                    own = Steps(dve, own_v, HEAD + STEP * (n - 1))
                    queries(n, u)
                    normalise(n - 1, 1 - u, own)
                    keys(n, u)
                    values(n, u)
                    if not last:
                        normalise_rows(n + 1, 1 - u)
                        context_low(n + 1, 1 - u)
                    attended_low(n - 1, 1 - u)
                    highest(n, u, own, last)
                    add_output(n - 1, own)
                    assert own.n == STEP

                def tail(b, u):
                    own = Steps(dve, own_v, HEAD + STEP * b)
                    normalise(b, u, own)
                    attended_low(b, u)
                    add_output(b, own)

                over_batches(dve.Fori, head, step, tail)

            @block.scalar
            def _(act):
                act.sem_inc(m["e"], AHEAD)
                act.sem_inc(m["yh"], AHEAD)
                act.sem_inc(m["ch"], AHEAD)
                act.sem_inc(pts, 2)

                def exponents(b, u):
                    act.wait_ge(m["nm"], done(b))
                    act.wait_ge(m["p"], done_before(b))
                    for h in range(H0):
                        ins = nc.scalar.activation(P[u][:, h, :], P[u][:, h, :], ACT.Exp, bias=nmax[u][:, h:h + 1],
                                                   scale=HD0 ** -0.5, accum_out=sums[u][:, h:h + 1])
                    ins.then_inc(m["e"], 1)

                def copy_turned(b, u):
                    act.wait_ge(m["y"], done_before(b))
                    for g in range(4):
                        act.wait_ge(pt, 4 * b + g + 1)
                        nc.scalar.copy(PT[u][:, 4 * g:4 * g + 4, :].rearrange("p h t -> p (h t)"),
                                       ps[0:T, 6 + g % 2, 0:4 * T]).then_inc(pts, 1)
                    act.wait_ge(m["y"], done(b))
                    act.wait_ge(m["o"], done_before(b))
                    nc.scalar.copy(yT[u][0][:].rearrange("p c t -> p (c t)"), ps[:, 4, 0:DC * T])\
                        .then_inc(m["yh"], 1)

                def context_high(b, u):
                    act.wait_ge(ctx_in[u], 8 * (b - u) + 16)
                    nc.scalar.copy(ctxS[u][0][:], ctxT[u][:]).then_inc(m["ch"], 1)

                def head():
                    context_high(0, 0)
                    context_high(1, 1)
                    for name, part in (("v", wv), ("o", wo)):
                        act.wait_ge(w_in[name], 16)
                        nc.scalar.copy(part[0][:], w[name][:]).then_inc(wh_done, 1)
                    exponents(0, 0)

                def step(n, u, last):
                    if not last:
                        context_high(n + 1, 1 - u)
                    copy_turned(n - 1, 1 - u)
                    exponents(n, u)

                over_batches(act.Fori, head, step, copy_turned)


def route(k, layer, rows):
    nc, a, ps = k.nc, k.a, k.ps
    L = f"r{layer}_"
    with ExitStack() as c:
        wg = k.sb(c, L + "wg", [128, DC, E])
        gam = k.sb(c, L + "gam", [128, DC])
        bet = k.sb(c, L + "bet", [128, DC])
        bg = k.sb(c, L + "bg", [T, E])
        xT = k.sb(c, L + "xT", [128, B, DC, T])
        mv = k.sb(c, L + "mv", [T, B, 2])
        rs = k.sb(c, L + "rs", [T, B])
        rs2 = k.sb(c, L + "rs2", [T, B])
        pr = k.sb(c, L + "pr", [T, B, E])
        t1 = k.sb(c, L + "t1", [T, B, E])
        m1 = k.sb(c, L + "m1", [T, 2, B])
        sm = k.sb(c, L + "sm", [T, B])
        rev = k.sb(c, L + "rev", [T, E])
        upper = k.sb(c, L + "upper", [T, T])
        ones = k.sb(c, L + "ones", [T, T])
        sel = k.sb(c, L + "sel", [T, B, E])
        before = k.sb(c, L + "before", [T, B + 1, E])
        npass = k.sb(c, L + "npass", [T, E])
        start = k.sb(c, L + "start", [T, E + 1])
        slotf = k.sb(c, L + "slotf", [T, 2, B])
        passno = k.sb(c, L + "passno", [1, PASSES + 1, E])
        tf = k.sb(c, L + "tf", [1, 16])

        w_in = k.sem(L + "w_in")
        made = k.sem(L + "const")
        norm = k.sem(L + "rows_ready")
        t_done, x_done = k.sem(L + "transposed"), [k.sem(f"{L}xT_ready{u}") for u in range(2)]
        lg = k.sem(L + "logits")
        ex, exd = k.sem(L + "exp_asked"), k.sem(L + "exp_done")
        sel_r, cnt = k.sem(L + "chosen"), k.sem(L + "counted")
        both = k.sem(L + "both_norms")
        own_v, own_p, started = k.sem(L + "dve_own"), k.sem(L + "pool_own"), k.sem(L + "first_passes")
        va, ri = k.sem(L + "variance"), k.sem(L + "rstd")

        with nc.Block() as block:
            @block.sync
            def _(sp):
                sp.dma_start(wg[:], a[f"Wg{layer}"].rearrange("(c p) e -> p c e", p=128)).then_inc(w_in, 16)
                if layer == 0:
                    sp.dma_start(gam[:], a["gam0"]).then_inc(w_in, 16)
                    sp.dma_start(bet[:], a["bet0"]).then_inc(w_in, 16)
                    sp.dma_start(bg[:], a["bg0"].partition_broadcast(T)).then_inc(w_in, 16)

            @block.gpsimd
            def _(pool):
                pool.memset(ones[:], 1.0).then_inc(made, 1)
                pool.iota(rev[:], pattern=[[-1, E]], base=E, channel_multiplier=0,
                          allow_small_or_imprecise_dtypes=True).then_inc(made, 1)
                pool.iota(passno[:], pattern=[[1, PASSES + 1], [0, E]], base=0, channel_multiplier=0,
                          allow_small_or_imprecise_dtypes=True).then_inc(made, 1)
                pool.wait_ge(made, 3)
                pool.affine_select(out=upper[:], in_=ones[:], compare_op=ALU.is_gt, fill=0.0,
                                   base=0, pattern=[[1, T]], channel_multiplier=-1).then_inc(made, 1)
                if layer == 0:
                    root(k, pool, rs2[:], both, ri, 1)
                    root(k, pool, rs[:], va, ri, 1)
                else:
                    root(k, pool, rs[:], va, ri, 1)
                own = Steps(pool, own_p)
                own.note(pool.memset(tf[:], 0.0))
                pool.wait_ge(started, 1)
                for half in (4, 2, 1):
                    own.link(pool.tensor_tensor(passno[:, :, 0:half], passno[:, :, 0:half],
                                                passno[:, :, half:2 * half], ALU.add))
                own.link(pool.tensor_copy(tf[:, 0:PASSES + 1], passno[:, :, 0]))
                own.link(pool.tensor_scalar(tf[:], tf[:], float(E - 1), None, ALU.min))
                own.link(pool.tensor_copy(tf[:, 15:16], start[0:1, E:E + 1]))
                own.link(pool.tensor_copy(k.table[:], tf[:]))

            @block.tensor
            def _(pe):
                for b in range(B):
                    pe.wait_ge(norm, b + 1)
                    if b >= 4:
                        pe.wait_ge(x_done[b % 2], b // 2 - 1)
                    for cc in range(DC):
                        mm = nc.tensor.transpose(ps[:, b % 4, T * cc:T * cc + T],
                                                 rows[:, b, 128 * cc:128 * cc + 128], k.ident[0:T, 0:T])
                    mm.then_inc(t_done, 1)
                pe.wait_ge(w_in, 64 if layer == 0 else 16)
                for b in range(B):
                    pe.wait_ge(x_done[b % 2], b // 2 + 1)
                    for cc in range(DC):
                        mm = nc.tensor.matmul(ps[0:T, 4, E * b:E * b + E], xT[:, b, cc, :], wg[:, cc, :],
                                              start=cc == 0, stop=cc == DC - 1)
                mm.then_inc(lg, 1)
                pe.wait_ge(sel_r, 1)
                pe.wait_ge(made, 4)
                flat = sel[:].rearrange("p b e -> p (b e)")
                nc.tensor.matmul(ps[0:T, 5, 0:B * E], upper[:], flat, start=True, stop=True)
                nc.tensor.matmul(ps[0:T, 6, 0:B * E], ones[:], flat, start=True, stop=True).then_inc(cnt, 1)

            @block.vector
            def _(dve):
                own = Steps(dve, own_v)

                aggregate(k, own, k.st, mv, rs, va)
                if layer == 0:
                    both_norms(k, mv, rs2[:]).then_inc(both, 1)
                dve.wait_ge(ri, 1)
                scale = rs2 if layer == 0 else rs
                for b in range(B):
                    nc.vector.tensor_scalar(rows[:, b, :], k.x[:, b, :], mv[:, b, 0:1], scale[:, b:b + 1],
                                            ALU.subtract, ALU.mult).then_inc(norm, 1)
                if layer == 0:
                    dve.wait_ge(w_in, 64)
                for b in range(1, B, 2):
                    dve.wait_ge(t_done, b + 1)
                    if layer == 0:
                        for cc in range(DC):
                            ins = nc.vector.tensor_scalar(xT[:, b, cc, :], ps[:, b % 4, T * cc:T * cc + T],
                                                          gam[:, cc:cc + 1], bet[:, cc:cc + 1], ALU.mult, ALU.add)
                    else:
                        ins = nc.vector.tensor_copy(xT[:, b].rearrange("p c t -> p (c t)"), ps[:, b % 4, 0:DC * T])
                    ins.then_inc(x_done[1], 1)
                if layer == 0:
                    dve.wait_ge(norm, B)
                    dve.wait_ge(ri, 2)
                    own.note(nc.vector.tensor_tensor(mv[:, :, 0], mv[:, :, 0], rs[:], ALU.mult))
                    own.link(nc.vector.tensor_scalar(rs[:], rs[:], 1.0, None, ALU.add))
                    for b in range(B):
                        own.note(nc.vector.tensor_scalar(k.x[:, b, :], k.x[:, b, :], rs[:, b:b + 1], mv[:, b, 0:1],
                                                         ALU.mult, ALU.subtract))
                dve.wait_ge(lg, 1)
                dve.wait_ge(made, 4)
                logits = ps[0:T, 4, 0:B * E].rearrange("p (b e) -> p b e", e=E)
                if layer == 0:
                    own.link(nc.vector.tensor_tensor(pr[:], logits, bg[:].unsqueeze(1).broadcast_to([T, B, E]), ALU.add))
                    own.link(nc.vector.tensor_reduce(sm[:], pr[:], AX, ALU.max))
                    nc.vector.tensor_tensor(pr[:], pr[:], bc(sm[:], E), ALU.subtract).then_inc(ex, 1)
                    dve.wait_ge(exd, 1)
                    own.link(nc.vector.tensor_reduce(sm[:], pr[:], AX, ALU.add))
                    own.link(nc.vector.reciprocal(sm[:], sm[:]))
                    own.link(nc.vector.tensor_tensor(pr[:], pr[:], bc(sm[:], E), ALU.mult))
                else:
                    own.link(nc.vector.tensor_copy(pr[:], logits))
                for j in range(2):
                    own.link(nc.vector.tensor_reduce(m1[:, j, :], pr[:], AX, ALU.max))
                    own.link(nc.vector.tensor_tensor(t1[:], pr[:], bc(m1[:, j, :], E), ALU.is_equal))
                    own.link(nc.vector.tensor_tensor(t1[:], t1[:], rev[:].unsqueeze(1).broadcast_to([T, B, E]), ALU.mult))
                    own.link(nc.vector.tensor_reduce(sm[:], t1[:], AX, ALU.max))
                    own.link(nc.vector.tensor_tensor(k.oh[j][:], bc(sm[:], E),
                                                     rev[:].unsqueeze(1).broadcast_to([T, B, E]), ALU.is_equal))
                    if j == 0:
                        own.link(nc.vector.scalar_tensor_tensor(out=pr[:], in0=k.oh[0][:], scalar=-3.0e38, in1=pr[:],
                                                                op0=ALU.mult, op1=ALU.add))
                nc.vector.tensor_tensor(sel[:], k.oh[0][:], k.oh[1][:], ALU.add).then_inc(sel_r, 1)
                if layer == 0:
                    own.link(nc.vector.tensor_tensor(sm[:], m1[:, 0, :], m1[:, 1, :], ALU.add))
                    own.link(nc.vector.tensor_scalar(sm[:], sm[:], 1e-8, None, ALU.add))
                    own.link(nc.vector.reciprocal(sm[:], sm[:]))
                    for j in range(2):
                        own.note(nc.vector.tensor_tensor(k.wt[:, j, :], m1[:, j, :], sm[:], ALU.mult))
                else:
                    nc.vector.tensor_tensor(sm[:], m1[:, 1, :], m1[:, 0, :], ALU.subtract).then_inc(ex, 1)
                    dve.wait_ge(exd, 1)
                    own.link(nc.vector.tensor_scalar(rs[:], sm[:], 1.0, None, ALU.add))
                    own.link(nc.vector.reciprocal(k.wt[:, 0, :], rs[:]))
                    own.note(nc.vector.tensor_tensor(k.wt[:, 1, :], k.wt[:, 0, :], sm[:], ALU.mult))
                own.note(nc.vector.memset(before[:, 0, :], 0.0))
                own.note(nc.vector.memset(start[:, 0:1], 0.0))
                own.link(nc.vector.memset(npass[:], 0.0))
                dve.wait_ge(cnt, 1)
                for b in range(B):
                    own.link(nc.vector.tensor_tensor(before[:, b + 1, :], before[:, b, :], ps[0:T, 6, E * b:E * b + E],
                                                     ALU.add))
                for n in range(-(-B * T // CAP)):
                    own.link(nc.vector.scalar_tensor_tensor(out=npass[:], in0=before[:, B, :], scalar=float(n * CAP),
                                                            in1=npass[:], op0=ALU.is_gt, op1=ALU.add))
                for e in range(E):
                    own.link(nc.vector.tensor_tensor(start[:, e + 1:e + 2], start[:, e:e + 1], npass[:, e:e + 1], ALU.add))
                nc.vector.tensor_tensor(passno[:], passno[:], start[0:1, 1:E + 1].unsqueeze(1)
                                        .broadcast_to([1, PASSES + 1, E]), ALU.is_ge).then_inc(started, 1)
                own.link(nc.vector.scalar_tensor_tensor(out=pr[:], in0=start[:, 0:E].unsqueeze(1).broadcast_to([T, B, E]),
                                                        scalar=float(CAP), in1=before[:, 0:B, :],
                                                        op0=ALU.mult, op1=ALU.add))
                own.link(nc.vector.tensor_tensor(pr[:], pr[:], ps[0:T, 5, 0:B * E].rearrange("p (b e) -> p b e", e=E),
                                                 ALU.add))
                for j in range(2):
                    own.link(nc.vector.tensor_tensor(t1[:], pr[:], k.oh[j][:], ALU.mult))
                    own.link(nc.vector.tensor_reduce(slotf[:, j, :], t1[:], AX, ALU.add))
                own.note(nc.vector.tensor_copy(k.slot[:], slotf[:]))

            @block.scalar
            def _(act):
                if layer == 0:
                    act.wait_ge(w_in, 64)
                for b in range(0, B, 2):
                    act.wait_ge(t_done, b + 1)
                    if layer == 0:
                        for cc in range(DC):
                            ins = nc.scalar.activation(xT[:, b, cc, :], ps[:, b % 4, T * cc:T * cc + T], ACT.Identity,
                                                       bias=bet[:, cc:cc + 1], scale=gam[:, cc:cc + 1])
                    else:
                        ins = nc.scalar.copy(xT[:, b].rearrange("p c t -> p (c t)"), ps[:, b % 4, 0:DC * T])
                    ins.then_inc(x_done[0], 1)
                act.wait_ge(ex, 1)
                if layer == 0:
                    nc.scalar.activation(pr[:], pr[:], ACT.Exp).then_inc(exd, 1)
                else:
                    nc.scalar.activation(sm[:], sm[:], ACT.Exp).then_inc(exd, 1)


def experts(k, layer, rows_in, s1=None):
    nc, a, ps = k.nc, k.a, k.ps
    L = f"e{layer}_"
    gated = layer == 1
    FG = 2 if gated else 4
    NB = 4 * FG
    ups = ["wgate", "wup"] if gated else ["w1"]
    CH = len(ups) + 1
    OUT = CH - 1
    Q = FG * CH
    RAW = Q // 2
    USED = 8
    LAG = 3
    with ExitStack() as c:
        raw = [k.sb(c, f"{L}raw{q}", [128, 4, 512]) for q in range(RAW)]
        hi = [[k.sb(c, f"{L}hi{u}_{n}", [128, 4, 512], F32R) for n in range(CH)] for u in range(2)]
        lo = [[k.sb(c, f"{L}lo{u}_{n}", [128, 4, 512], F32R) for n in range(CH)] for u in range(2)]
        xs = k.sb(c, L + "xs", [128, 2, D])
        xf = k.sb(c, L + "xf", [128, DC, CAP])
        xh = k.sb(c, L + "xh", [128, DC, CAP], F32R)
        xl = k.sb(c, L + "xl", [128, DC, CAP], F32R)
        hf = [k.sb(c, f"{L}hf{n}", [128, CAP]) for n in range(4)]
        hh = [k.sb(c, f"{L}hh{n}", [128, CAP], F32R) for n in range(4)]
        hl = [k.sb(c, f"{L}hl{n}", [128, CAP], F32R) for n in range(4)]
        gt = [k.sb(c, f"{L}gt{n}", [128, CAP]) for n in range(2)]
        y = k.sb(c, L + "y", [128, 2, D])
        b1 = k.sb(c, L + "b1", [128, E * NB])
        gam = k.sb(c, L + "gam", [128, DC])
        bet = k.sb(c, L + "bet", [128, DC])

        w_in = [k.sem(f"{L}w_in{q}") for q in range(Q)]
        scattered = k.sem(L + "scattered")
        c_in, x_in, ahead = k.sem(L + "c_in"), k.sem(L + "x_in"), k.sem(L + "ahead")
        t_done, xf_v, xf_a = k.sem(L + "transposed"), k.sem(L + "xf_dve"), k.sem(L + "xf_act")
        xh_done, xl_done = k.sem(L + "xh_done"), k.sem(L + "xl_done")
        hi_done, lo_done = k.sem(L + "hi_done"), k.sem(L + "lo_done")
        up_done, out_done = k.sem(L + "up_done"), k.sem(L + "out_done")
        a_done, f_done = k.sem(L + "act_done"), k.sem(L + "hf_done")
        hh_done, h_done = k.sem(L + "hh_done"), k.sem(L + "hl_done")
        y_v, y_a, y_out, y_free = (k.sem(L + n) for n in ("y_dve", "y_act", "y_out", "y_free"))
        last = k.table[0:1, 15:16]

        FIRST = [(0, i) for i in range(CH)]
        LATE = [] if gated else [(1, 0)]
        AT_BLOCK = {0: [0], 1: [1], 2: [2]} if gated else {0: [0], 2: [1]}

        def next_chunks(kb):
            g, r = kb // 4, kb % 4
            return [((g + 1) // FG, (g + 1) % FG, i) for i in AT_BLOCK.get(r, []) if (g + 1, i) not in LATE]

        with nc.Block() as block:
            @block.sync
            def _(sp):
                if not gated:
                    sp.dma_start(b1[:], a["b1"]).then_inc(c_in, 16)
                    sp.dma_start(gam[:], a["gam0"]).then_inc(c_in, 16)
                    sp.dma_start(bet[:], a["bet0"]).then_inc(c_in, 16)
                n = sp.value_load(last, min_val=LEAST, max_val=PASSES)

                def rows(j):
                    sp.wait_ge(t_done, j + 1)
                    sp.dma_start(xs[:], k.rows[bass.ds(j * CAP, CAP), :].rearrange("(s p) d -> p s d", p=128))\
                        .then_inc(x_in, 16)

                def load(j, e, chunks):
                    for g, i in chunks:
                        q = g * CH + i
                        src = a[ups[i] if i < OUT else f"wout{layer}"][bass.ds(e * FG + g, 1)]
                        sp.wait_ge(lo_done, Q * j + q + 1 + Q - RAW)
                        sp.dma_start(raw[q % RAW][:], src.rearrange("o p c f -> (o p) c f")).then_inc(w_in[q], 16)

                def expert(j):
                    return sp.value_load(k.table[0:1, bass.ds(j, 1)], min_val=0, max_val=E - 1)

                first = expert(0)
                load(0, first, FIRST)
                sp.wait_ge(scattered, 16 * 2 * B)
                rows(0)
                load(0, first, LATE)
                with sp.Fori(0, n) as j:
                    e = expert(j)
                    load(j, e, [(g, i) for g in range(1, FG) for i in range(CH) if (g, i) not in LATE])
                    rows(j + 1)
                    load(j + 1, expert(j + 1), FIRST + LATE)
                if s1 is not None:
                    for n in range(s1.AHEAD):
                        sp.dma_start(s1.ahead(n), s1.chunk(a, n)).then_inc(ahead, 16)
                    sp.dma_start(s1.gam[:], a["ln_g"]).then_inc(ahead, 16)
                    sp.dma_start(s1.bet[:], a["ln_b"]).then_inc(ahead, 16)
                    sp.wait_ge(ahead, 64)

            @block.gpsimd
            def _(pool):
                for b in range(B):
                    for j in range(2):
                        pool.indirect_dma_start(out=k.rows[:, :],
                                                out_offset=bass.IndirectOffsetOnAxis(ap=k.slot[:, j, b:b + 1], axis=0),
                                                in_=rows_in[:, b, :], in_offset=None).then_inc(scattered, 16)
                n = pool.value_load(last, min_val=LEAST, max_val=PASSES)
                pool.sem_inc(y_free, 1)
                with pool.Fori(0, n) as j:
                    pool.wait_ge(y_v, j + 2)
                    pool.wait_ge(y_a, j + 2)
                    pool.dma_start(k.outs[bass.ds(j * CAP, CAP), :].rearrange("(s p) d -> p s d", p=128), y[:])\
                        .then_inc(y_out, 16)
                    pool.wait_ge(y_out, j * 16 + 16)
                    pool.sem_inc(y_free, 1)

            @block.tensor
            def _(pe):
                n = pe.value_load(last, min_val=LEAST, max_val=PASSES)
                pe.sem_inc(t_done, 1)
                pe.sem_inc(up_done, USED)
                pe.sem_inc(out_done, USED)

                def turn(j):
                    pe.wait_ge(x_in, j * 16 + 16)
                    pe.wait_ge(xf_v, j + 1)
                    pe.wait_ge(xf_a, j + 1)
                    for s in range(2):
                        for cc in range(DC):
                            mm = nc.tensor.transpose(ps[:, 6 + s, 128 * cc:128 * cc + 128],
                                                     xs[:, s, 128 * cc:128 * cc + 128], k.ident[:])
                    mm.then_inc(t_done, 1)

                turn(0)
                with pe.Fori(0, n) as j:
                    for kb in range(NB + LAG):
                        if kb < NB:
                            g = kb // 4
                            if kb == 0:
                                pe.wait_ge(xl_done, j + 1 + 1)
                            pe.wait_ge(f_done, NB * j + kb + (3 if gated else 1))
                            cut = slice(128 * (kb % 4), 128 * (kb % 4) + 128)
                            for i in range(len(ups)):
                                if kb % 4 == 0:
                                    pe.wait_ge(lo_done, Q * j + Q + g * CH + i + 1)
                                bank = 2 * i + kb % 2 if gated else kb % 4
                                wh, wl = hi[g % 2][i], lo[g % 2][i]
                                terms = [(w, x, cc) for cc in range(DC) for w, x in ((wh, xh), (wh, xl), (wl, xh))]
                                for t, (w, x, cc) in enumerate(terms):
                                    mm = nc.tensor.matmul(ps[:, bank, 0:CAP], w[:, cc, cut], x[:, cc, :],
                                                          start=t == 0, stop=t == len(terms) - 1)
                            mm.then_inc(up_done, 1)
                        if kb == NB - 3:
                            turn(j + 1)
                        if kb >= LAG:
                            q = kb - LAG
                            if q == 0:
                                pe.wait_ge(y_v, j + 1)
                                pe.wait_ge(y_a, j + 1)
                            if q % 4 == 0:
                                pe.wait_ge(lo_done, Q * j + Q + (q // 4) * CH + OUT + 1)
                            pe.wait_ge(h_done, NB * j + q + 4 + 1)
                            wh, wl = hi[q // 4 % 2][OUT], lo[q // 4 % 2][OUT]
                            for s in range(2):
                                cut = slice(128 * s, 128 * s + 128)
                                for t, (h, w) in enumerate(((hh, wh), (hh, wl), (hl, wh))):
                                    mm = nc.tensor.matmul(ps[:, 4 + s, :], h[q % 4][:, cut], w[:, q % 4, :],
                                                          start=q == 0 and t == 0, stop=q == NB - 1 and t == 2)
                            mm.then_inc(out_done, 1)

            @block.vector
            def _(dve):
                n = dve.value_load(last, min_val=LEAST, max_val=PASSES)
                dve.sem_inc(xf_v, 1)
                dve.sem_inc(xl_done, 1)
                dve.sem_inc(lo_done, Q)
                dve.sem_inc(h_done, 4)
                dve.sem_inc(y_v, 1)
                if gated:
                    dve.sem_inc(f_done, 4)
                else:
                    dve.wait_ge(c_in, 48)

                def low(j, g, i):
                    q = g * CH + i
                    dve.wait_ge(hi_done, Q * j + q + 1)
                    nc.vector.tensor_tensor(lo[g % 2][i][:], raw[q % RAW][:], hi[g % 2][i][:].bitcast(F32), ALU.subtract)\
                        .then_inc(lo_done, 1)

                def rows(j):
                    dve.wait_ge(t_done, j + 2)
                    dve.wait_ge(xl_done, j + 1)
                    if gated:
                        ins = nc.vector.tensor_copy(xf[:, :, 0:128], ps[:, 6, :].rearrange("p (c t) -> p c t", c=DC))
                    else:
                        for cc in range(DC):
                            ins = nc.vector.tensor_scalar(xf[:, cc, 0:128], ps[:, 6, 128 * cc:128 * cc + 128],
                                                          gam[:, cc:cc + 1], bet[:, cc:cc + 1], ALU.mult, ALU.add)
                    ins.then_inc(xf_v, 1)

                def rows_low(j):
                    dve.wait_ge(xh_done, j + 1)
                    nc.vector.tensor_tensor(xl[:], xf[:], xh[:].bitcast(F32), ALU.subtract).then_inc(xl_done, 1)

                for g, i in FIRST:
                    low(0, g, i)
                rows(0)
                rows_low(0)
                for g, i in LATE:
                    low(0, g, i)
                with dve.Fori(0, n) as j:
                    for kb in range(NB):
                        dve.wait_ge(out_done, NB * j + USED + kb - 3)
                        if gated:
                            dve.wait_ge(a_done, NB * j + kb + 1 + 2)
                            nc.vector.tensor_tensor(hf[kb % 4][:], gt[kb % 2][:], ps[:, 2 + kb % 2, 0:CAP],
                                                    ALU.mult).then_inc(f_done, 1)
                        dve.wait_ge(f_done, NB * j + kb + 4 + 1)
                        nc.vector.tensor_copy(hh[kb % 4][:], hf[kb % 4][:]).then_inc(hh_done, 1)
                        dve.wait_ge(hh_done, NB * j + kb + 1)
                        nc.vector.tensor_tensor(hl[kb % 4][:], hf[kb % 4][:], hh[kb % 4][:].bitcast(F32),
                                                ALU.subtract).then_inc(h_done, 1)
                        for dj, g, i in next_chunks(kb):
                            low(j + dj, g, i)
                        if kb == NB - 3:
                            rows(j + 1)
                    rows_low(j + 1)
                    dve.wait_ge(out_done, NB * j + USED + NB)
                    dve.wait_ge(y_free, j + 1)
                    nc.vector.tensor_copy(y[:, 0, :], ps[:, 4, :]).then_inc(y_v, 1)
                    for g, i in LATE:
                        low(j + 1, g, i)

            @block.scalar
            def _(act):
                n = act.value_load(last, min_val=LEAST, max_val=PASSES)
                act.sem_inc(xf_a, 1)
                act.sem_inc(y_a, 1)
                if gated:
                    act.sem_inc(a_done, 2)
                else:
                    act.sem_inc(f_done, 4)
                    act.wait_ge(c_in, 48)

                def high(j, g, i):
                    q = g * CH + i
                    act.wait_ge(w_in[q], j * 16 + 16)
                    act.wait_ge(out_done if i == OUT else up_done, NB * j + 4 * g + 4)
                    nc.scalar.copy(hi[g % 2][i][:], raw[q % RAW][:]).then_inc(hi_done, 1)

                def rows(j):
                    act.wait_ge(t_done, j + 2)
                    act.wait_ge(xl_done, j + 1)
                    if gated:
                        ins = nc.scalar.copy(xf[:, :, 128:256], ps[:, 7, :].rearrange("p (c t) -> p c t", c=DC))
                    else:
                        for cc in range(DC):
                            ins = nc.scalar.activation(xf[:, cc, 128:256], ps[:, 7, 128 * cc:128 * cc + 128],
                                                       ACT.Identity, bias=bet[:, cc:cc + 1], scale=gam[:, cc:cc + 1])
                    ins.then_inc(xf_a, 1)

                def rows_high(j):
                    act.wait_ge(xf_v, j + 2)
                    act.wait_ge(xf_a, j + 2)
                    act.wait_ge(up_done, NB * j + USED)
                    nc.scalar.copy(xh[:], xf[:]).then_inc(xh_done, 1)

                for g, i in FIRST:
                    high(0, g, i)
                rows(0)
                rows_high(0)
                for g, i in LATE:
                    high(0, g, i)
                with act.Fori(0, n) as j:
                    e = 0 if gated else act.value_load(k.table[0:1, bass.ds(j, 1)], min_val=0, max_val=E - 1)
                    for kb in range(NB):
                        act.wait_ge(up_done, NB * j + USED + kb + 1)
                        act.wait_ge(h_done, NB * j + kb + 1)
                        if gated:
                            act.wait_ge(f_done, NB * j + kb + 3)
                            nc.scalar.activation(gt[kb % 2][:], ps[:, kb % 2, 0:CAP], ACT.Silu).then_inc(a_done, 1)
                        else:
                            nc.scalar.activation(hf[kb % 4][:], ps[:, kb % 4, 0:CAP], ACT.Gelu,
                                                 bias=b1[:, bass.ds(e * NB + kb, 1)]).then_inc(f_done, 1)
                        for dj, g, i in next_chunks(kb):
                            high(j + dj, g, i)
                        if kb == NB - 3:
                            rows(j + 1)
                    rows_high(j + 1)
                    for g, i in LATE:
                        high(j + 1, g, i)
                    act.wait_ge(out_done, NB * j + USED + NB)
                    act.wait_ge(y_free, j + 1)
                    nc.scalar.copy(y[:, 1, :], ps[:, 5, :]).then_inc(y_a, 1)


def combine(k, layer):
    nc, a, ps = k.nc, k.a, k.ps
    L = f"c{layer}_"
    EARLY = B - 2
    with ExitStack() as c:
        y = k.sb(c, L + "y", [T + E, 2, B, D])
        dg = k.sb(c, L + "dg", [T, 2, B, T + E])
        dT = k.sb(c, L + "dT", [T + E, B, T])
        w8 = k.sb(c, L + "w8", [T, 2, B, E])
        lg = k.sb(c, L + "lg", [T, D])
        lb = k.sb(c, L + "lb", [T, D])
        z = k.sb(c, L + "z", [T, B, D])
        mv = k.sb(c, L + "mv", [T, B, 2])
        rs = k.sb(c, L + "rs", [T, B])
        y_in = [k.sem(f"{L}y_in{b}") for b in range(B)]
        c_in = k.sem(L + "c_in")
        wt, wc = k.sem(L + "turned"), k.sem(L + "dT_ready")
        dr, added = k.sem(L + "diagonals"), k.sem(L + "added")
        own_v = k.sem(L + "dve_own")
        fin, stored = k.sem(L + "out_ready"), k.sem(L + "stored")
        va, ri = k.sem(L + "variance"), k.sem(L + "rstd")
        with nc.Block() as block:
            @block.sync
            def _(sp):
                if layer == 0:
                    sp.dma_start(y[T:T + E, 1], a["b2"].unsqueeze(1).broadcast_to([E, B, D])).then_inc(c_in, 16)
                else:
                    sp.dma_start(lg[:], a["gam1"].partition_broadcast(T)).then_inc(c_in, 16)
                    sp.dma_start(lb[:], a["bet1"].partition_broadcast(T)).then_inc(c_in, 16)
                    for b in range(B):
                        sp.wait_ge(fin, b + 1)
                        sp.dma_start(a["out"][b], k.x[:, b, :]).then_inc(stored, 16)
                    sp.wait_ge(stored, 16 * B)

            @block.gpsimd
            def _(pool):
                for b in range(B):
                    for j in range(2):
                        pool.indirect_dma_start(out=y[0:T, j, b, :], out_offset=None, in_=k.outs[:, :],
                                                in_offset=bass.IndirectOffsetOnAxis(ap=k.slot[:, j, b:b + 1], axis=0))\
                            .then_inc(y_in[b], 16)
                if layer == 1:
                    root(k, pool, rs[:, 0:EARLY], va, ri, 1)
                    root(k, pool, rs[:, EARLY:B], va, ri, 2)

            @block.tensor
            def _(pe):
                if layer == 0:
                    for b in range(B):
                        pe.wait_ge(dr, b + 1)
                        mm = nc.tensor.transpose(ps[0:T + E, b // 4, T * (b % 4):T * (b % 4) + T], dg[:, 1, b, :],
                                                 k.ident[0:T, 0:T])
                    mm.then_inc(wt, 1)
                    pe.wait_ge(wc, 1)
                    pe.wait_ge(c_in, 16)
                for b in range(B):
                    pe.wait_ge(dr, b + 1)
                    pe.wait_ge(y_in[b], 32)
                    nc.tensor.matmul(ps[0:T, b, :], dg[:, 0, b, 0:T], y[0:T, 0, b, :], start=True, stop=False)
                    second = (dT[:, b, :], y[:, 1, b, :]) if layer == 0 else (dg[:, 1, b, 0:T], y[0:T, 1, b, :])
                    nc.tensor.matmul(ps[0:T, b, :], *second, start=False, stop=True).then_inc(added, 1)

            @block.vector
            def _(dve):
                own = Steps(dve, own_v)
                if layer == 0:
                    for j in range(2):
                        own.note(nc.vector.tensor_tensor(w8[:, j], k.oh[j][:], bc(k.wt[:, j, :], E), ALU.mult))
                    own.settle()
                    own.link(nc.vector.tensor_tensor(dg[:, 1, :, T:T + E], w8[:, 0], w8[:, 1], ALU.add))
                for b in range(B):
                    for j in range(2):
                        ins = nc.vector.tensor_scalar(dg[:, j, b, 0:T], k.ident[0:T, 0:T], k.wt[:, j, b:b + 1], None,
                                                      ALU.mult)
                    ins.then_inc(dr, 1)
                if layer == 0:
                    dve.wait_ge(wt, 1)
                    for g in range(2):
                        ins = nc.vector.tensor_copy(dT[:, 4 * g:4 * g + 4, :].rearrange("p b t -> p (b t)"),
                                                    ps[0:T + E, g, 0:4 * T])
                    ins.then_inc(wc, 1)
                if layer == 0:
                    for b in range(B):
                        dve.wait_ge(added, b + 1)
                        own.link(nc.vector.tensor_tensor(k.x[:, b, :], k.x[:, b, :], ps[0:T, b, :], ALU.add))
                        nc.vector.bn_stats(k.st[:, b, :], k.x[:, b, :])
                else:
                    dve.wait_ge(c_in, 32)
                    for b in range(B):
                        own.note(nc.vector.tensor_tensor(k.x[:, b, :], k.x[:, b, :], lb[:], ALU.add))
                    for part in (slice(0, EARLY), slice(EARLY, B)):
                        for b in range(B)[part]:
                            dve.wait_ge(added, b + 1)
                            own.link(nc.vector.bn_stats(k.st[:, b, :], ps[0:T, b, :]))
                            own.link(nc.vector.bn_aggr(mv[:, b, :], k.st[:, b, :]))
                            own.note(nc.vector.scalar_tensor_tensor(out=z[:, b, :], in0=ps[0:T, b, :],
                                                                    scalar=mv[:, b, 0:1], in1=lg[:],
                                                                    op0=ALU.subtract, op1=ALU.mult))
                        own.settle()
                        nc.vector.tensor_scalar(rs[:, part], mv[:, part, 1], EPS, None, ALU.add).then_inc(va, 1)
                    for b in range(B):
                        dve.wait_ge(ri, 1 if b < EARLY else 2)
                        nc.vector.scalar_tensor_tensor(out=k.x[:, b, :], in0=z[:, b, :], scalar=rs[:, b:b + 1],
                                                       in1=k.x[:, b, :], op0=ALU.mult, op1=ALU.add).then_inc(fin, 1)


class Attention1:
    AHEAD = 2

    def __init__(self, k, ctx):
        nc = k.nc
        self.q = nc.dram_tensor("own_q", (2, B, 128, IC, T), F32, kind="Internal").ap()
        self.kk = nc.dram_tensor("own_k", (2, B, 128, IC, T), F32, kind="Internal").ap()
        self.v = nc.dram_tensor("own_v", (B, T, INNER), F32, kind="Internal").ap()
        self.wo = k.sb(ctx, "a1_wo", [128, IC, D])
        self.gam = k.sb(ctx, "a1_gam", [128, DC])
        self.bet = k.sb(ctx, "a1_bet", [128, DC])

    def context_weights(self, k, ctx):
        self.wm = [k.sb(ctx, f"a1_wm{n}", [128, DC, INNER], F32R) for n in range(2)]
        self.craw = [k.sb(ctx, f"a1_craw{u}", [128, DC, 128]) for u in range(3)]

    def ahead(self, n):
        return self.wo[:, 4 * n:4 * n + 4, :]

    @staticmethod
    def chunk(a, n):
        w, first = [(a["Wq"], 0), (a["Wkv"], 0), (a["Wkv"], INNER), (a["Wm"], 0)][n // 2]
        first += 512 * (n % 2)
        return w[:, first:first + 512].rearrange("(c p) n -> p c n", p=128)


def project(k, s1):
    nc, a, ps = k.nc, k.a, k.ps
    N = 4 * T
    with ExitStack() as c:
        CHUNKS = 8
        later = [k.sb(c, f"p_raw{n}", [128, DC, 512]) for n in range(4)]
        raw = [s1.ahead(n) if n < s1.AHEAD else later[n % 4][:] for n in range(CHUNKS)]
        hi = [k.sb(c, f"p_hi{u}", [128, DC, 512], F32R) for u in range(2)]
        lo = [k.sb(c, f"p_lo{u}", [128, DC, 512], F32R) for u in range(2)]
        xn = [k.sb(c, f"p_xn{u}", [T, D]) for u in range(2)]
        xf = k.sb(c, "p_xf", [128, DC, B * T])
        xh = k.sb(c, "p_xh", [128, DC, B * T], F32R)
        xl = k.sb(c, "p_xl", [128, DC, B * T], F32R)
        sth = [k.sb(c, f"p_sth{u}", [128, 4, 4, T], F32R) for u in range(2)]
        stl = [k.sb(c, f"p_stl{u}", [128, 4, 4, T], F32R) for u in range(2)]
        vst = [k.sb(c, f"p_vst{u}", [T, 512]) for u in range(2)]
        scale = (HD1 ** -0.5, 1.0)
        mv = k.sb(c, "p_mv", [T, B, 2])
        rs = k.sb(c, "p_rs", [T, B])

        va, ri, own_v = k.sem("p_variance"), k.sem("p_rstd"), k.sem("p_dve_own")
        xn_r, t_done = k.sem("p_xn_ready"), k.sem("p_transposed")
        xf_v, ctx_in = k.sem("p_xf_dve"), k.sem("p_ctx_in")
        xf_r, xh_r, xl_r = k.sem("p_xf"), k.sem("p_xh"), k.sem("p_xl")
        w_in = [k.sem(f"p_w_in{n}") for n in range(8)]
        hi_done, lo_done = k.sem("p_hi_done"), k.sem("p_lo_done")
        pj, st_hi, st_lo = k.sem("p_projected"), k.sem("p_staged_hi"), k.sem("p_staged_lo")
        st_out, st_free = k.sem("p_stored"), k.sem("p_stage_free")
        v_st, v_out = [k.sem(f"p_v_staged{u}") for u in range(2)], [k.sem(f"p_v_stored{u}") for u in range(2)]

        def row_bank(b, cc):
            return 4 + 2 * (b % 2) + cc // 2

        def out_of(t, pair, i, half):
            return t[pair, 4 * half:4 * half + 4, :, 4 * i:4 * i + 4, :].rearrange("b p m t -> p b (m t)")

        with nc.Block() as block:
            @block.sync
            def _(sp):
                sp.sem_inc(st_free, 2)
                for n in range(s1.AHEAD, CHUNKS):
                    if n >= s1.AHEAD + 4:
                        sp.wait_ge(lo_done, n - 3)
                    sp.dma_start(raw[n], s1.chunk(a, n)).then_inc(w_in[n], 16)
                for nb in range(3):
                    sp.dma_start(s1.craw[nb][:], a["ctxT"][0].rearrange("(c p) s -> p c s", p=128)
                                 [:, :, 128 * nb:128 * nb + 128]).then_inc(ctx_in, 16)
                sp.wait_ge(ctx_in, 48)

            @block.gpsimd
            def _(pool):
                root(k, pool, rs[:], va, ri, 1)
                for t, n in ((s1.q, 0), (s1.kk, 1)):
                    for i in range(2):
                        for half in range(2):
                            g = 4 * n + 2 * i + half
                            pool.wait_ge(st_lo, 4 * g + 4 + 4)
                            for pair, tile in ((0, sth), (1, stl)):
                                pool.dma_start(out_of(t, pair, i, half),
                                               tile[half][:].bitcast(F32).rearrange("p b m t -> p b (m t)"))\
                                    .then_inc(st_out, 16)
                            pool.wait_ge(st_out, 32 * (g + 1))
                            pool.sem_inc(st_free, 1)
                for n in range(2):
                    for b in range(B):
                        u = b % 2
                        pool.wait_ge(v_st[u], 4 * n + b // 2 + 1)
                        pool.dma_start(s1.v[b][:, 512 * n:512 * n + 512], vst[u][:]).then_inc(v_out[u], 16)
                for u in range(2):
                    pool.wait_ge(v_out[u], 16 * B)

            @block.tensor
            def _(pe):
                pe.sem_inc(pj, 8)

                def turn(b):
                    pe.wait_ge(xn_r, b + 1)
                    if b >= 2:
                        pe.wait_ge(xf_r, b - 1)
                        pe.wait_ge(xf_v, b - 1)
                    for cc in range(DC):
                        mm = nc.tensor.transpose(ps[:, row_bank(b, cc), T * cc:T * cc + T],
                                                 xn[b % 2][:, 128 * cc:128 * cc + 128], k.ident[0:T, 0:T])
                    mm.then_inc(t_done, 1)

                for b in range(5):
                    turn(b)
                for t in range(2):
                    for i in range(2):
                        pe.wait_ge(lo_done, 2 * t + i + 1)
                        for half in range(2):
                            if t == 0 and i == 0:
                                pe.wait_ge(xl_r, 4 * half + 4)
                            for m in range(4):
                                job = 8 * i + 4 * half + m
                                pe.wait_ge(st_lo, 16 * t + job + 1)
                                terms = [(w, x, cc) for cc in range(DC)
                                         for w, x in ((hi[i], xh), (hi[i], xl), (lo[i], xh))]
                                for n, (w, x, cc) in enumerate(terms):
                                    mm = nc.tensor.matmul(ps[:, m, 0:N], w[:, cc, 128 * m:128 * m + 128],
                                                          x[:, cc, N * half:N * half + N],
                                                          start=n == 0, stop=n == len(terms) - 1)
                                mm.then_inc(pj, 1)
                                if t == 0 and job < 3:
                                    turn(5 + job)
                for n in range(2):
                    pe.wait_ge(lo_done, 4 + n + 1)
                    for b in range(B):
                        if n == 0 and b < 4:
                            pe.wait_ge(st_lo, 4 + 32 - 3 + b)
                        else:
                            pe.wait_ge(v_st[b % 2], 4 * n + b // 2 - 1)
                        terms = [(x, w, cc) for cc in range(DC)
                                 for x, w in ((xh, hi[n]), (xh, lo[n]), (xl, hi[n]))]
                        for q, (x, w, cc) in enumerate(terms):
                            mm = nc.tensor.matmul(ps[0:T, b % 4, :], x[:, cc, T * b:T * b + T], w[:, cc, :],
                                                  start=q == 0, stop=q == len(terms) - 1)
                        mm.then_inc(pj, 1)

            def staged_v(eng, copy, u):
                def run(n):
                    for b in range(u, B, 2):
                        eng.wait_ge(pj, 8 + 32 + 8 * n + b + 1)
                        if 4 * n + b // 2 >= 1:
                            eng.wait_ge(v_out[u], 16 * (4 * n + b // 2))
                        copy(vst[u][:], ps[0:T, b % 4, :]).then_inc(v_st[u], 1)
                return run

            @block.vector
            def _(dve):
                own = Steps(dve, own_v)
                dve.sem_inc(st_lo, 4)
                def low_of(n, dst, top):
                    dve.wait_ge(hi_done, n + 1)
                    nc.vector.tensor_tensor(dst, raw[n],
                                            top.bitcast(F32), ALU.subtract).then_inc(lo_done, 1)

                for b in range(B):
                    own.note(nc.vector.bn_aggr(mv[:, b, :], k.st[:, b, :]))
                own.settle()
                both_norms(k, mv, rs[:]).then_inc(va, 1)
                low_of(0, lo[0][:], hi[0][:])
                dve.wait_ge(ri, 1)

                def rows_low(b):
                    dve.wait_ge(xh_r, b + 1)
                    nc.vector.tensor_tensor(xl[:, :, T * b:T * b + T], xf[:, :, T * b:T * b + T],
                                            xh[:, :, T * b:T * b + T].bitcast(F32), ALU.subtract).then_inc(xl_r, 1)

                def rows_scaled(b):
                    dve.wait_ge(t_done, b + 1)
                    for cc in range(DC // 2, DC):
                        ins = nc.vector.tensor_scalar(xf[:, cc, T * b:T * b + T], ps[:, row_bank(b, cc), T * cc:T * cc + T],
                                                      s1.gam[:, cc:cc + 1], s1.bet[:, cc:cc + 1], ALU.mult, ALU.add)
                    ins.then_inc(xf_v, 1)

                for b in range(B):
                    if b >= 2:
                        dve.wait_ge(t_done, b - 1)
                    nc.vector.tensor_scalar(xn[b % 2][:], k.x[:, b, :], mv[:, b, 0:1], rs[:, b:b + 1],
                                            ALU.subtract, ALU.mult).then_inc(xn_r, 1)
                    if b >= 2:
                        rows_low(b - 2)
                    if b >= 1:
                        rows_scaled(b - 1)
                rows_low(B - 2)
                rows_scaled(B - 1)
                rows_low(B - 1)
                for t in range(2):
                    for i in range(2):
                        for half in range(2):
                            for m in range(4):
                                job = 8 * i + 4 * half + m
                                dve.wait_ge(st_hi, 16 * t + job + 1)
                                nc.vector.scalar_tensor_tensor(
                                    out=stl[half][:, :, m, :], in0=ps[:, m, 0:N].rearrange("p (b t) -> p b t", t=T),
                                    scalar=scale[t], in1=sth[half][:, :, m, :].bitcast(F32),
                                    op0=ALU.mult, op1=ALU.subtract).then_inc(st_lo, 1)
                            if half == 0:
                                if i == 0:
                                    low_of(2 * t + 1, lo[1][:], hi[1][:])
                                else:
                                    low_of(2 * t + 2, lo[0][:], hi[0][:])
                run = staged_v(dve, nc.vector.tensor_copy, 1)
                low_of(5, lo[1][:], hi[1][:])
                low_of(6, s1.wm[1][:, :, 0:512], s1.wm[0][:, :, 0:512])
                run(0)
                low_of(7, s1.wm[1][:, :, 512:1024], s1.wm[0][:, :, 512:1024])
                run(1)

            @block.scalar
            def _(act):
                nc.scalar.copy(hi[0][:], raw[0]).then_inc(hi_done, 1)
                for b in range(B):
                    act.wait_ge(t_done, b + 1)
                    for cc in range(DC // 2):
                        ins = nc.scalar.activation(xf[:, cc, T * b:T * b + T], ps[:, row_bank(b, cc), T * cc:T * cc + T],
                                                   ACT.Identity, bias=s1.bet[:, cc:cc + 1], scale=s1.gam[:, cc:cc + 1])
                    ins.then_inc(xf_r, 1)
                    act.wait_ge(xf_r, b + 1)
                    act.wait_ge(xf_v, b + 1)
                    nc.scalar.copy(xh[:, :, T * b:T * b + T], xf[:, :, T * b:T * b + T]).then_inc(xh_r, 1)

                def high(n, dst):
                    if n >= s1.AHEAD:
                        act.wait_ge(w_in[n], 16)
                    nc.scalar.copy(dst, raw[n]).then_inc(hi_done, 1)

                for t in range(2):
                    for i in range(2):
                        for half in range(2):
                            act.wait_ge(st_free, 4 * t + 2 * i + half + 1)
                            for m in range(4):
                                job = 8 * i + 4 * half + m
                                act.wait_ge(pj, 16 * t + job + 8 + 1)
                                nc.scalar.activation(sth[half][:, :, m, :], ps[:, m, 0:N].rearrange("p (b t) -> p b t", t=T),
                                                     ACT.Identity, scale=scale[t]).then_inc(st_hi, 1)
                            if half == 0:
                                if i == 0:
                                    act.wait_ge(pj, 16 * t + 8)
                                    high(2 * t + 1, hi[1][:])
                                else:
                                    act.wait_ge(pj, 16 * t + 16)
                                    high(2 * t + 2, hi[0][:])
                run = staged_v(act, nc.scalar.copy, 0)
                act.wait_ge(pj, 8 + 32)
                high(5, hi[1][:])
                high(6, s1.wm[0][:, :, 0:512])
                run(0)
                high(7, s1.wm[0][:, :, 512:1024])
                run(1)


def attend(k, s1):
    nc, a, ps = k.nc, k.a, k.ps
    NB = len(MB)
    NV = 2 * NB
    ORDER = [(0, 0), (1, 0), (0, 1), (1, 1)] + [(nb, g) for nb in range(2, NB) for g in range(2)]
    FINAL = [max(n for n in range(NV) if ORDER[n][0] == nb) for nb in range(NB)]
    MIDDLE = {0: 0, 1: 2, 2: 3, 3: 5, 4: 7, 5: 9, 6: 10, 7: 11}
    END = {0: 1, 2: 4, 3: 6, 4: 8}
    SPLIT = {0: (1, 2), 1: (1, 3), 2: (1, 4), 3: (1, 5), 6: (2, 0), 7: (2, 1)}
    WIDE = [(0, 512), (512, KEYS - 512)]
    SLOTS = 4
    assert KEYS - 512 >= 256 and len(MIDDLE) + len(END) == NV
    with ExitStack() as c:
        craw = s1.craw
        ch = [k.sb(c, f"a1_ch{u}", [128, DC, 128], F32R) for u in range(3)]
        cl = [k.sb(c, f"a1_cl{u}", [128, DC, 128], F32R) for u in range(3)]
        qD = [k.sb(c, f"a1_qD{u}", [128, 2, 2, T], F32R) for u in range(SLOTS)]
        kT = [k.sb(c, f"a1_kT{u}", [128, 2, KEYS], F32R) for u in range(SLOTS)]
        v = [k.sb(c, f"a1_v{u}", [128, len(KB1), INNER]) for u in range(2)]
        P = [k.sb(c, f"a1_P{u}", [T, KEYS]) for u in range(4)]
        PT = [k.sb(c, f"a1_PT{u}", [128, len(KB1), T]) for u in range(4)]
        yT = k.sb(c, "a1_yT", [128, IC, T])
        bo = k.sb(c, "a1_bo", [T, D])
        nmax = k.sb(c, "a1_nmax", [T, H1])
        sums = k.sb(c, "a1_sums", [T, H1])
        rinv = k.sb(c, "a1_rinv", [T, H1])

        made = k.sem("a1_const")
        craw_in = [k.sem(f"a1_craw_in{u}") for u in range(3)]
        ch_done, cl_done = k.sem("a1_ch_done"), k.sem("a1_cl_done")
        qk_in = [k.sem(f"a1_qk_in{u}") for u in range(SLOTS)]
        v_in = [k.sem(f"a1_v_in{u}") for u in range(2)]
        val, val_v, val_a = k.sem("a1_values"), k.sem("a1_values_dve"), k.sem("a1_values_act")
        tk, th, tl = k.sem("a1_keys_turned"), k.sem("a1_keys_hi"), k.sem("a1_keys_lo")
        sc, nm, ex = k.sem("a1_scores"), k.sem("a1_max"), k.sem("a1_exp")
        ri, pn, pt = k.sem("a1_rinv"), k.sem("a1_prob"), k.sem("a1_prob_turned")
        pt_v, pt_a = k.sem("a1_probT_dve"), k.sem("a1_probT_act")
        yd, ys = k.sem("a1_y"), k.sem("a1_yT_ready")
        o_in = k.sem("a1_o_in")
        od, os_, own_v = k.sem("a1_o"), k.sem("a1_added"), k.sem("a1_dve_own")

        def two_banks(n):
            return ps[:, n:n + 2, :].rearrange("p a n -> p (a n)")

        def over_steps(eng, step):
            def body(b, u, left):
                for m in range(2, IC):
                    step(b, u, m, left)
                for m in range(2):
                    step(b + 1, 1 - u, m, left - 1 if left < 2 else 2 if type(b) is not int else B - 2 - b)

            for m in range(2):
                step(0, 0, m, 2)
            with eng.Fori(0, (B - 2) // 2) as i:
                body(2 * i, 0, 2)
                body(2 * i + 1, 1, 2)
            body(B - 2, 0, 1)
            body(B - 1, 1, 0)

        def exists(p):
            return type(p) is not int or 0 <= p < B * IC

        with nc.Block() as block:
            @block.sync
            def _(sp):
                def context(b, nb):
                    b, nb = b + nb // NB, nb % NB
                    if type(b) is int and b >= B:
                        return
                    first, size = MB[nb][0] - T, MB[nb][1]
                    after(sp, cl_done, NB * b + nb - 2)
                    src = a["ctxT"][bass.ds(b, 1)].rearrange("b (c p) s -> p (b c) s", p=128)
                    sp.dma_start(craw[nb % 3][:, :, 0:size], src[:, :, first:first + size])\
                        .then_inc(craw_in[nb % 3], 16)

                def own(b, m):
                    b, m = b + m // IC, m % IC
                    if not exists(IC * b + m):
                        return
                    s = m % SLOTS
                    after(sp, sc, 2 * (IC * b + m - SLOTS + 1))
                    for two in range(2):
                        r = slice(64 * two, 64 * two + 64)
                        sp.dma_start(qD[s][r, :, two, :].bitcast(F32),
                                     s1.q[:, bass.ds(b, 1), r, m, :].rearrange("n b p t -> p (n b) t"))\
                            .then_inc(qk_in[s], 16)
                    sp.dma_start(kT[s][:, :, 0:T].bitcast(F32),
                                 s1.kk[:, bass.ds(b, 1), :, m, :].rearrange("n b p t -> p (n b) t"))\
                        .then_inc(qk_in[s], 16)

                def own_values(b, u):
                    after(sp, yd, IC * (b - 1))
                    sp.dma_start(v[u][0:T, 0, :], s1.v[bass.ds(b, 1)].rearrange("b t n -> t (b n)"))\
                        .then_inc(v_in[u], 16)

                for u in range(3):
                    sp.sem_inc(craw_in[u], 16)
                sp.wait_ge(made, SLOTS)
                for m in range(SLOTS - 1):
                    own(0, m)
                own_values(0, 0)
                own_values(1, 1)
                sp.dma_start(s1.wo[:], a["Wo"].rearrange("(c p) n -> p c n", p=128)).then_inc(o_in, 16)
                sp.dma_start(bo[:], a["bo"].partition_broadcast(T)).then_inc(o_in, 16)
                for nb in range(3, NB + 4):
                    context(0, nb)

                def step(b, u, m, left):
                    if left >= 0:
                        own(b, m + SLOTS - 1)
                    if m in SPLIT and left >= SPLIT[m][0]:
                        context(b + SPLIT[m][0], SPLIT[m][1] + 2)
                    if m == 1 and left >= 1 and not (type(b) is int and b == 0):
                        own_values(b + 1, 1 - u)

                over_steps(sp, step)

            @block.gpsimd
            def _(pool):
                for s in range(SLOTS):
                    pool.memset(qD[s][:].bitcast(U32), 0).then_inc(made, 1)

            @block.tensor
            def _(pe):
                def values(b, n, bank):
                    nb, g = ORDER[n]
                    size = MB[nb][1]
                    pe.wait_ge(cl_done, NB * b + nb + 1)
                    terms = [(x, w, cc) for cc in range(DC) for x, w in
                             ((ch[nb % 3], s1.wm[0]), (ch[nb % 3], s1.wm[1]), (cl[nb % 3], s1.wm[0]))]
                    for t, (x, w, cc) in enumerate(terms):
                        mm = nc.tensor.matmul(ps[0:size, bank, :], x[:, cc, 0:size],
                                              w[:, cc, 512 * g:512 * g + 512],
                                              start=t == 0, stop=t == len(terms) - 1)
                    mm.then_inc(val, 1)

                def values_copied(b, n):
                    pe.wait_ge(val_v if n % 2 else val_a, NB * b + n // 2 + 1)

                def values_ahead(b, n):
                    if n == 0:
                        values_copied(b, NV - 1)
                    else:
                        values_copied(b + 1, n - 1)
                    if n == FINAL[0] + 1:
                        pe.wait_ge(os_, b + 1)
                    values(b + 1, n, 6)

                def keys(p, m, u):
                    after(pe, pt_v, 2 * p - 4)
                    after(pe, pt_a, 2 * p - 4)
                    for nb, (first, size) in enumerate(MB):
                        o = 128 * nb
                        mm = nc.tensor.transpose(ps[:, 4 + o // 512, o % 512:o % 512 + size],
                                                 v[u][0:size, 1 + nb, 128 * m:128 * m + 128], k.ident[0:size, 0:size])
                    mm.then_inc(tk, 1)

                def scores(p, m, two):
                    s = m % SLOTS
                    after(pe, ex, 2 * p + two - 1)
                    for f, (first, wide) in enumerate(WIDE):
                        for t, (q, kk) in enumerate(((0, 0), (0, 1), (1, 0))):
                            mm = nc.tensor.matmul(ps[0:T, 2 * two + f, 0:wide], qD[s][:, q, two, :],
                                                  kT[s][:, kk, first:first + wide], start=t == 0, stop=t == 2)
                    mm.then_inc(sc, 1)

                def turn(p, m, two):
                    h = 2 * p + two
                    pe.wait_ge(pn, h + 1)
                    after(pe, pt_v, h)
                    after(pe, pt_a, h)
                    for n, (first, size) in enumerate(KB1):
                        mm = nc.tensor.transpose(ps[0:size, 4 + n // 5, T * (n % 5):T * (n % 5) + T],
                                                 P[(2 * m + two) % 4][:, first:first + size], k.ident[0:T, 0:T])
                    mm.then_inc(pt, 1)

                def attended(p, m, u):
                    pe.wait_ge(pt_v, 2 * p + 2)
                    pe.wait_ge(pt_a, 2 * p + 2)
                    pe.wait_ge(ys, p - 1 + 2)
                    for n, (first, size) in enumerate(KB1):
                        for two in range(2):
                            h = 2 * m + two
                            mm = nc.tensor.matmul(ps[64 * two:64 * two + 64, 7, 128 * (m % 2):128 * (m % 2) + T],
                                                  v[u][0:size, n, HD1 * h:HD1 * h + HD1], PT[h % 4][0:size, n, :],
                                                  start=n == 0, stop=n == len(KB1) - 1)
                    mm.then_inc(yd, 1)

                def step(b, u, m, left):
                    p = IC * b + m
                    if left >= 0:
                        pe.wait_ge(qk_in[m % SLOTS], 48 * (2 * b + m // SLOTS + 1))
                        pe.wait_ge(tl, p + 1)
                        scores(p, m, 0)
                    ahead = left >= (1 if m == IC - 1 else 0)
                    if ahead:
                        if m == IC - 1:
                            values_copied(b + 1, NV - 2)
                            keys(p + 1, 0, 1 - u)
                        else:
                            if m + 1 == IC // 2:
                                values_copied(b, NV - 1)
                            keys(p + 1, m + 1, u)
                    if exists(p - 2):
                        ub = u if m >= 2 else 1 - u
                        if m == 2:
                            pe.wait_ge(v_in[u], 8 * (b - u) + 16)
                        attended(p - 2, (m - 2) % IC, ub)
                    if left >= 1 and m in MIDDLE:
                        values_ahead(b, MIDDLE[m])
                    if exists(p - 1):
                        if ahead:
                            pe.wait_ge(tl, p + 2)
                        turn(p - 1, (m - 1) % IC, 0)
                    if left >= 0:
                        scores(p, m, 1)
                    if exists(p - 1):
                        turn(p - 1, (m - 1) % IC, 1)
                    if left >= 1 and m in END:
                        values_ahead(b, END[m])
                    if m == 1 and exists(p - 2):
                        pe.wait_ge(ys, IC * b + 2)
                        if left >= 1:
                            values_copied(b + 1, MIDDLE[1])
                        elif type(b) is int:
                            pe.wait_ge(os_, b)
                        for j in range(IC):
                            mm = nc.tensor.matmul(ps[0:T, 6, :], yT[:, j, :], s1.wo[:, j, :],
                                                  start=j == 0, stop=j == IC - 1)
                        mm.then_inc(od, 1)

                for n in range(NV):
                    if n >= 4:
                        values_copied(0, n - 4)
                    values(0, n, n % 4)
                values_copied(0, NV - 2)
                values_copied(0, NV - 1)
                keys(0, 0, 0)
                pe.wait_ge(o_in, 32)
                over_steps(pe, step)

            def copy_values(eng, copy, done, b, u, n, bank):
                nb, g = ORDER[n]
                size = MB[nb][1]
                eng.wait_ge(val, NV * b + n + 1)
                copy(v[u][0:size, 1 + nb, 512 * g:512 * g + 512], ps[0:size, bank, :]).then_inc(done, 1)

            def begin(split, evacuate):
                for nb in range(3):
                    split(0, nb)
                for n in range(NV):
                    evacuate(0, 0, n, n % 4)
                    if n in FINAL and FINAL.index(n) + 3 < NB + 2:
                        split(0, FINAL.index(n) + 3)

            @block.vector
            def _(dve):
                dve.sem_inc(os_, 1)

                def split(b, nb):
                    b, nb = b + nb // NB, nb % NB
                    size = MB[nb][1]
                    dve.wait_ge(ch_done, NB * b + nb + 1)
                    nc.vector.tensor_tensor(cl[nb % 3][:, :, 0:size], craw[nb % 3][:, :, 0:size],
                                            ch[nb % 3][:, :, 0:size].bitcast(F32), ALU.subtract).then_inc(cl_done, 1)

                def evacuate(b, u, n, bank):
                    if n % 2 == 1:
                        copy_values(dve, nc.vector.tensor_copy, val_v, b, u, n, bank)

                def keys(p, m):
                    s = m % SLOTS
                    dve.wait_ge(th, p + 1)
                    nc.vector.tensor_tensor(kT[s][:, 1, T:KEYS], two_banks(4)[:, 0:S],
                                            kT[s][:, 0, T:KEYS].bitcast(F32), ALU.subtract).then_inc(tl, 1)

                def highest(p, m, two):
                    h = 2 * m + two
                    dve.wait_ge(sc, 2 * p + two + 1)
                    nc.vector.tensor_reduce(nmax[:, h:h + 1], two_banks(2 * two)[0:T, 0:KEYS], AX, ALU.max, negate=True)\
                        .then_inc(nm, 1)

                def normalise(p, m, two):
                    h = 2 * m + two
                    dve.wait_ge(ex, 2 * p + two + 1)
                    nc.vector.reciprocal(rinv[:, h:h + 1], sums[:, h:h + 1]).then_inc(ri, 1)
                    dve.wait_ge(ri, 2 * p + two + 1)
                    nc.vector.tensor_scalar(P[h % 4][:], P[h % 4][:], rinv[:, h:h + 1], None, ALU.mult)\
                        .then_inc(pn, 1)

                def turned(p, m, two):
                    dve.wait_ge(pt, 2 * p + two + 1)
                    nc.vector.tensor_copy(PT[(2 * m + two) % 4][:, 5:7, :].rearrange("p n t -> p (n t)"),
                                          ps[:, 5, 0:2 * T]).then_inc(pt_v, 1)

                def step(b, u, m, left):
                    p = IC * b + m
                    if left >= 0:
                        highest(p, m, 0)
                    if left >= (1 if m == IC - 1 else 0):
                        keys(p + 1, (m + 1) % IC)
                    if exists(p - 1):
                        normalise(p - 1, (m - 1) % IC, 1)
                    if left >= 0:
                        normalise(p, m, 0)
                    if left >= 1 and m in MIDDLE:
                        evacuate(b + 1, 1 - u, MIDDLE[m], 6)
                    if exists(p - 1):
                        turned(p - 1, (m - 1) % IC, 0)
                    if left >= 0:
                        highest(p, m, 1)
                    if exists(p - 1):
                        turned(p - 1, (m - 1) % IC, 1)
                    if left >= 1 and m in END:
                        evacuate(b + 1, 1 - u, END[m], 6)
                    if m in SPLIT and left >= SPLIT[m][0]:
                        split(b + SPLIT[m][0], SPLIT[m][1])
                    if m == 1 and exists(p - 2):
                        xb = at(k.x, b - 1)
                        dve.wait_ge(od, b)
                        nc.vector.tensor_tensor(xb, xb, ps[0:T, 6, :], ALU.add).then_inc(own_v, 1)
                        dve.wait_ge(own_v, b)
                        nc.vector.tensor_tensor(xb, xb, bo[:], ALU.add).then_inc(os_, 1)
                        dve.wait_ge(os_, b + 1)
                        nc.vector.bn_stats(at(k.st, b - 1), xb)

                begin(split, evacuate)
                keys(0, 0)
                over_steps(dve, step)

            @block.scalar
            def _(act):
                act.sem_inc(ys, 2)

                def split(b, nb):
                    b, nb = b + nb // NB, nb % NB
                    size = MB[nb][1]
                    act.wait_ge(craw_in[nb % 3], 32 * b + 16 * (nb // 3) + 16)
                    pb, pn_ = (b, nb - 3) if nb >= 3 else (b - 1, nb + 3)
                    after(act, val, NV * pb + FINAL[pn_] + 1)
                    nc.scalar.copy(ch[nb % 3][:, :, 0:size], craw[nb % 3][:, :, 0:size]).then_inc(ch_done, 1)

                def evacuate(b, u, n, bank):
                    if n % 2 == 0:
                        copy_values(act, nc.scalar.copy, val_a, b, u, n, bank)

                def keys(p, m):
                    act.wait_ge(tk, p + 1)
                    nc.scalar.copy(kT[m % SLOTS][:, 0, T:KEYS], two_banks(4)[:, 0:S]).then_inc(th, 1)

                def exponent(p, m, two):
                    h = 2 * m + two
                    act.wait_ge(nm, 2 * p + two + 1)
                    nc.scalar.activation(P[h % 4][:], two_banks(2 * two)[0:T, 0:KEYS], ACT.Exp, bias=nmax[:, h:h + 1],
                                         accum_out=sums[:, h:h + 1]).then_inc(ex, 1)

                def turned(p, m, two):
                    act.wait_ge(pt, 2 * p + two + 1)
                    nc.scalar.copy(PT[(2 * m + two) % 4][:, 0:5, :].rearrange("p n t -> p (n t)"), ps[:, 4, 0:5 * T])\
                        .then_inc(pt_a, 1)

                def attended(p, m):
                    act.wait_ge(yd, p + 1)
                    nc.scalar.copy(yT[:, m, :], ps[:, 7, 128 * (m % 2):128 * (m % 2) + T]).then_inc(ys, 1)

                def step(b, u, m, left):
                    p = IC * b + m
                    if left >= (1 if m == IC - 1 else 0):
                        keys(p + 1, (m + 1) % IC)
                    if left >= 0:
                        exponent(p, m, 0)
                    if exists(p - 2):
                        attended(p - 2, (m - 2) % IC)
                    if left >= 1 and m in MIDDLE:
                        evacuate(b + 1, 1 - u, MIDDLE[m], 6)
                    if exists(p - 1):
                        turned(p - 1, (m - 1) % IC, 0)
                        turned(p - 1, (m - 1) % IC, 1)
                    if left >= 0:
                        exponent(p, m, 1)
                    if left >= 1 and m in END:
                        evacuate(b + 1, 1 - u, END[m], 6)
                    if m in SPLIT and left >= SPLIT[m][0]:
                        split(b + SPLIT[m][0], SPLIT[m][1])

                begin(split, evacuate)
                keys(0, 0)
                over_steps(act, step)


def build(nc, a):
    with ExitStack() as ctx:
        k = Core(nc, ctx, a)

        def routed(layer, s1=None):
            with ExitStack() as c:
                rows = k.sb(c, f"rows{layer}", [T, B, D])
                route(k, layer, rows)
                k.end_stage()
                experts(k, layer, rows, s1)
                k.end_stage()

        attention_0(k)
        k.end_stage()
        with ExitStack() as shared:
            s1 = Attention1(k, shared)
            routed(0, s1)
            combine(k, 0)
            k.end_stage()
            s1.context_weights(k, shared)
            for stage in (project, attend):
                stage(k, s1)
                k.end_stage()
        routed(1)
        combine(k, 1)
        k.end_stage()


def lay_out(i):
    g = {n: np.asarray(v) for n, v in i.items()}

    def chunks_in(w, fg):
        return w.reshape(E, fg, 512, DC, 128).transpose(0, 1, 4, 3, 2).reshape(E * fg, 128, DC, 512)

    def chunks_out(w, fg):
        return w.reshape(E, D, fg, 4, 128).transpose(0, 2, 4, 3, 1).reshape(E * fg, 128, 4, D)

    def column(b):
        return b.reshape(-1, 128).T

    p0, p1, q0, q1 = "L0_xattn_", "L1_xattn_", "L0_ffn_", "L1_ffn_"
    return {k_: np.ascontiguousarray(v) for k_, v in {
        "x": g["x"], "ctxT": g["ctx_1024"].transpose(0, 2, 1),
        "q_w": g[p0 + "q_w"], "k_w": g[p0 + "k_w"], "v_w": g[p0 + "v_w"], "o_w": g[p0 + "o_w"],
        "q_b": column(g[p0 + "q_b"]), "k_b": column(g[p0 + "k_b"]), "v_b": g[p0 + "v_b"], "o_b": g[p0 + "o_b"],
        "gam0": column(g[q0 + "gamma"]), "bet0": column(g[q0 + "beta"]),
        "Wg0": g[q0 + "Wg"].T, "bg0": g[q0 + "bg"],
        "w1": chunks_in(g[q0 + "W1"], 4), "b1": g[q0 + "b1"].reshape(E * 16, 128).T,
        "wout0": chunks_out(g[q0 + "W2"], 4), "b2": g[q0 + "b2"],
        "ln_g": column(g[p1 + "ln_g"]), "ln_b": column(g[p1 + "ln_b"]),
        "Wq": g[p1 + "Wq"], "Wkv": g[p1 + "Wkv"], "Wm": g[p1 + "Wm"], "Wo": g[p1 + "Wo"], "bo": g[p1 + "bo"],
        "Wg1": g[q1 + "w_router"].T, "wgate": chunks_in(g[q1 + "w_gate"], 2), "wup": chunks_in(g[q1 + "w_up"], 2),
        "wout1": chunks_out(g[q1 + "w_down"], 2), "gam1": g[q1 + "ln_gamma"], "bet1": g[q1 + "ln_beta"],
    }.items()}


def kernel(**inputs):
    import concourse.bacc as bacc
    from concourse.bass_utils import run_bass_kernel_spmd

    nc = bacc.Bacc("TRN2", target_bir_lowering=False, num_devices=1)
    arrays = lay_out(inputs)
    a = {n: nc.dram_tensor(n, v.shape, F32, kind="ExternalInput").ap() for n, v in arrays.items()}
    a["out"] = nc.dram_tensor("out", (B, T, D), F32, kind="ExternalOutput").ap()
    build(nc, a)
    r = run_bass_kernel_spmd(nc, [arrays], core_ids=[0])
    return r.results[0]["out"]
```
